# Optimizing a Trainium2 kernel written in Bass

```python
import numpy as np
import jax
import jax.numpy as jnp

def _softmax(x, axis=-1):
    return jax.nn.softmax(x, axis=axis)

def _gelu(x):
    return jax.nn.gelu(x, approximate=True)

def _silu(x):
    return jax.nn.silu(x)

def _sigmoid(x):
    return jax.nn.sigmoid(x)

def _layernorm(x, axis=-1, eps=1e-05):
    m = jnp.mean(x, axis=axis, keepdims=True)
    v = jnp.var(x, axis=axis, keepdims=True)
    return (x - m) / jnp.sqrt(v + eps)

def _scatter_add(tgt, idx, src, axis=0):
    return tgt.at[idx].add(src)

def _segment_sum(src, seg, n):
    return jax.ops.segment_sum(src, seg, n)
kernel_name = 'mk_gnn_resnorm_d2_gnn_r32_1f45b6'

def setup_inputs(seed: int=0):
    np.random.seed(seed)
    _w = jnp.asarray

    def _rec_inputs():
        import jax
        import jax.numpy as jnp
        _gk = jax.random.key(seed)
        x = -0.000202 + 1 * jax.random.normal(jax.random.fold_in(_gk, 1), (50000, 128), jnp.float32)
        src = jax.random.randint(jax.random.fold_in(_gk, 2), (50000,), 0, 50000, jnp.int32)
        dst = jnp.minimum((50000 * jax.random.uniform(jax.random.fold_in(_gk, 3), (50000,)) ** 2.0).astype(jnp.int32), 49999)
        _o = jnp.argsort(dst, stable=True)
        src = src[_o]
        dst = dst[_o]
        edge_type_8 = jax.random.randint(jax.random.fold_in(_gk, 13), (50000,), 0, 8, jnp.int32)
        return (x, src, dst, edge_type_8)
    x, src, dst, edge_type_8 = _rec_inputs()

    def _L0_gnn_setup():
        import jax, jax.numpy as jnp
        import numpy as np
        N = 50000
        E = 25000
        D = 128
        R = 8
        B = 4
        L = 2
        BN_EPS = 0.001

        def _edge_norm(etype, dst, dtype):
            node_norm = jnp.zeros((N,), dtype=dtype)
            for r in range(R):
                mask = (etype == r).astype(dtype)
                cnt = jax.ops.segment_sum(mask, dst, num_segments=N)
                node_norm = jnp.where(cnt > 0, 1.0 / jnp.maximum(cnt, 1.0), node_norm)
            return node_norm[dst][:, None]
        key = jax.random.key(seed)
        ks = jax.random.split(key, 10)
        node_feat = jax.random.normal(ks[0], (N, D), dtype=jnp.float32)
        src = jax.random.randint(ks[1], (E,), 0, N)
        dst = jax.random.randint(ks[2], (E,), 0, N)
        etype = jax.random.randint(ks[3], (E,), 0, R)
        s = 1.0 / np.sqrt(D)
        W_emb = jax.random.normal(ks[4], (D, D), dtype=jnp.float32) * s
        b_emb = jnp.zeros((D,), dtype=jnp.float32)
        bases = jax.random.normal(ks[5], (L, B, D, D), dtype=jnp.float32) * s
        w_coe = jax.random.normal(ks[6], (L, R, B), dtype=jnp.float32) * 0.3
        self_loop = jax.random.normal(ks[7], (L, D, D), dtype=jnp.float32) * s
        bn_gamma = jnp.ones((L, D), dtype=jnp.float32)
        bn_beta = jnp.zeros((L, D), dtype=jnp.float32)
        bn_mean = jnp.zeros((L, D), dtype=jnp.float32)
        bn_var = jnp.ones((L, D), dtype=jnp.float32)
        return {'node_feat': node_feat, 'W_emb': W_emb, 'b_emb': b_emb, 'bases': bases, 'w_coe': w_coe, 'self_loop': self_loop, 'bn_gamma': bn_gamma, 'bn_beta': bn_beta, 'bn_mean': bn_mean, 'bn_var': bn_var, 'src': src, 'dst': dst, 'etype': etype}
    _L0_gnn_all = _L0_gnn_setup()
    _L0_gnn_in = {k: v for k, v in _L0_gnn_all.items() if k in ('W_emb', 'b_emb', 'bases', 'w_coe', 'self_loop', 'bn_gamma', 'bn_beta', 'bn_mean', 'bn_var')}
    del _L0_gnn_all

    def _L1_gnn_setup():
        import jax, jax.numpy as jnp
        import numpy as np
        N, E = (50000, 25000)
        D, H = (128, 8)
        DPH = D // H
        SQRT_D = DPH ** 0.5
        EPS = 1e-05

        def _batch_norm(h, g, b):
            mu = jnp.mean(h, axis=0)
            var = jnp.mean((h - mu) ** 2, axis=0)
            return g * (h - mu) * jax.lax.rsqrt(var + EPS) + b

        def _graph_attention(x, edge_index, Wq, Wk, Wv):
            Q = (x @ Wq).reshape(N, H, DPH)
            K = (x @ Wk).reshape(N, H, DPH)
            V = (x @ Wv).reshape(N, H, DPH)
            src, dst = (edge_index[0], edge_index[1])
            score = jnp.einsum('ehd,ehd->eh', Q[dst], K[src]) / SQRT_D
            score = jnp.clip(score, -5.0, 5.0)
            smax = jax.ops.segment_max(score, dst, num_segments=N)
            ex = jnp.exp(score - smax[dst])
            denom = jax.ops.segment_sum(ex, dst, num_segments=N)
            alpha = ex / denom[dst]
            msg = V[src] * alpha[..., None]
            out = jax.ops.segment_sum(msg, dst, num_segments=N)
            return out.reshape(N, H * DPH)
        key = jax.random.key(seed)
        ks = jax.random.split(key, 12)
        w = lambda k, shape: jax.random.normal(k, shape, jnp.float32) * 0.05
        return {'x': jax.random.normal(ks[0], (N, D), jnp.float32), 'edge_index': jax.random.randint(ks[1], (2, E), 0, N, jnp.int64), 'Wq': w(ks[2], (D, D)), 'Wk': w(ks[3], (D, D)), 'Wv': w(ks[4], (D, D)), 'Wo': w(ks[5], (D, D)), 'bo': jnp.zeros((D,), jnp.float32), 'W1': w(ks[6], (D, 2 * D)), 'b1': jnp.zeros((2 * D,), jnp.float32), 'W2': w(ks[7], (2 * D, D)), 'b2': jnp.zeros((D,), jnp.float32), 'g1': jnp.ones((D,), jnp.float32), 'be1': jnp.zeros((D,), jnp.float32), 'g2': jnp.ones((D,), jnp.float32), 'be2': jnp.zeros((D,), jnp.float32)}
    _L1_gnn_all = _L1_gnn_setup()
    _L1_gnn_in = {k: v for k, v in _L1_gnn_all.items() if k in ('Wq', 'Wk', 'Wv', 'Wo', 'bo', 'W1', 'b1', 'W2', 'b2', 'g1', 'be1', 'g2', 'be2')}
    del _L1_gnn_all
    return {'x': x, 'src': src, 'dst': dst, 'edge_type_8': edge_type_8, 'L0_gnn_W_emb': _L0_gnn_in['W_emb'], 'L0_gnn_b_emb': _L0_gnn_in['b_emb'], 'L0_gnn_bases': _L0_gnn_in['bases'], 'L0_gnn_w_coe': _L0_gnn_in['w_coe'], 'L0_gnn_self_loop': _L0_gnn_in['self_loop'], 'L0_gnn_bn_gamma': _L0_gnn_in['bn_gamma'], 'L0_gnn_bn_beta': _L0_gnn_in['bn_beta'], 'L0_gnn_bn_mean': _L0_gnn_in['bn_mean'], 'L0_gnn_bn_var': _L0_gnn_in['bn_var'], 'L1_gnn_Wq': _L1_gnn_in['Wq'], 'L1_gnn_Wk': _L1_gnn_in['Wk'], 'L1_gnn_Wv': _L1_gnn_in['Wv'], 'L1_gnn_Wo': _L1_gnn_in['Wo'], 'L1_gnn_bo': _L1_gnn_in['bo'], 'L1_gnn_W1': _L1_gnn_in['W1'], 'L1_gnn_b1': _L1_gnn_in['b1'], 'L1_gnn_W2': _L1_gnn_in['W2'], 'L1_gnn_b2': _L1_gnn_in['b2'], 'L1_gnn_g1': _L1_gnn_in['g1'], 'L1_gnn_be1': _L1_gnn_in['be1'], 'L1_gnn_g2': _L1_gnn_in['g2'], 'L1_gnn_be2': _L1_gnn_in['be2']}

def reference(x, src, dst, edge_type_8, L0_gnn_W_emb, L0_gnn_b_emb, L0_gnn_bases, L0_gnn_w_coe, L0_gnn_self_loop, L0_gnn_bn_gamma, L0_gnn_bn_beta, L0_gnn_bn_mean, L0_gnn_bn_var, L1_gnn_Wq, L1_gnn_Wk, L1_gnn_Wv, L1_gnn_Wo, L1_gnn_bo, L1_gnn_W1, L1_gnn_b1, L1_gnn_W2, L1_gnn_b2, L1_gnn_g1, L1_gnn_be1, L1_gnn_g2, L1_gnn_be2):
    import jax
    import jax.numpy as jnp

    def _L0_gnn_ref(node_feat, W_emb, b_emb, bases, w_coe, self_loop, bn_gamma, bn_beta, bn_mean, bn_var, src, dst, etype):
        import jax, jax.numpy as jnp
        import numpy as np
        N = 50000
        E = 25000
        D = 128
        R = 8
        B = 4
        L = 2
        BN_EPS = 0.001

        def _edge_norm(etype, dst, dtype):
            node_norm = jnp.zeros((N,), dtype=dtype)
            for r in range(R):
                mask = (etype == r).astype(dtype)
                cnt = jax.ops.segment_sum(mask, dst, num_segments=N)
                node_norm = jnp.where(cnt > 0, 1.0 / jnp.maximum(cnt, 1.0), node_norm)
            return node_norm[dst][:, None]
        h = node_feat @ W_emb + b_emb
        norm = _edge_norm(etype, dst, h.dtype)
        for l in range(L):
            W = jnp.einsum('rb,bdf->rdf', w_coe[l], bases[l])
            T = jnp.einsum('nd,rdf->rnf', h, W)
            msg = T[etype, src] * norm
            agg = jax.ops.segment_sum(msg, dst, num_segments=N)
            h = agg + h @ self_loop[l]
            h = bn_gamma[l] * (h - bn_mean[l]) * jax.lax.rsqrt(bn_var[l] + BN_EPS) + bn_beta[l]
            h = jax.nn.relu(h)
        return h

    def _L1_gnn_ref(x, edge_index, Wq, Wk, Wv, Wo, bo, W1, b1, W2, b2, g1, be1, g2, be2):
        import jax, jax.numpy as jnp
        import numpy as np
        N, E = (50000, 25000)
        D, H = (128, 8)
        DPH = D // H
        SQRT_D = DPH ** 0.5
        EPS = 1e-05

        def _batch_norm(h, g, b):
            mu = jnp.mean(h, axis=0)
            var = jnp.mean((h - mu) ** 2, axis=0)
            return g * (h - mu) * jax.lax.rsqrt(var + EPS) + b

        def _graph_attention(x, edge_index, Wq, Wk, Wv):
            Q = (x @ Wq).reshape(N, H, DPH)
            K = (x @ Wk).reshape(N, H, DPH)
            V = (x @ Wv).reshape(N, H, DPH)
            src, dst = (edge_index[0], edge_index[1])
            score = jnp.einsum('ehd,ehd->eh', Q[dst], K[src]) / SQRT_D
            score = jnp.clip(score, -5.0, 5.0)
            smax = jax.ops.segment_max(score, dst, num_segments=N)
            ex = jnp.exp(score - smax[dst])
            denom = jax.ops.segment_sum(ex, dst, num_segments=N)
            alpha = ex / denom[dst]
            msg = V[src] * alpha[..., None]
            out = jax.ops.segment_sum(msg, dst, num_segments=N)
            return out.reshape(N, H * DPH)
        h_in1 = x
        h = _graph_attention(x, edge_index, Wq, Wk, Wv)
        h = h @ Wo + bo
        h = h_in1 + h
        h = _batch_norm(h, g1, be1)
        h_in2 = h
        h = jax.nn.relu(h @ W1 + b1)
        h = h @ W2 + b2
        h = h_in2 + h
        h = _batch_norm(h, g2, be2)
        return h
    edge_index = jnp.stack([src, dst])
    x = _layernorm(x + _L0_gnn_ref(x, L0_gnn_W_emb, L0_gnn_b_emb, L0_gnn_bases, L0_gnn_w_coe, L0_gnn_self_loop, L0_gnn_bn_gamma, L0_gnn_bn_beta, L0_gnn_bn_mean, L0_gnn_bn_var, src, dst, edge_type_8), axis=-1)
    x = _layernorm(x + _L1_gnn_ref(x, edge_index, L1_gnn_Wq, L1_gnn_Wk, L1_gnn_Wv, L1_gnn_Wo, L1_gnn_bo, L1_gnn_W1, L1_gnn_b1, L1_gnn_W2, L1_gnn_b2, L1_gnn_g1, L1_gnn_be1, L1_gnn_g2, L1_gnn_be2), axis=-1)
    return x

_drawn_inputs = setup_inputs


def setup_inputs(seed=0):
    import zlib

    import numpy as np

    out = dict(_drawn_inputs(seed))
    spreads = {'L0_gnn_b_emb': (0.0, 0.1),
     'L0_gnn_bn_gamma': (1.0, 0.2),
     'L0_gnn_bn_beta': (0.0, 0.1),
     'L0_gnn_bn_mean': (0.0, 0.1),
     'L0_gnn_bn_var': (1.0, 0.2),
     'L1_gnn_bo': (0.0, 0.8),
     'L1_gnn_b1': (0.0, 0.411),
     'L1_gnn_b2': (0.0, 0.8),
     'L1_gnn_g1': (1.0, 0.2),
     'L1_gnn_be1': (0.0, 0.763),
     'L1_gnn_g2': (1.0, 0.2),
     'L1_gnn_be2': (0.0, 0.1)}
    factors = {'L1_gnn_Wq': 4.832, 'L1_gnn_Wk': 4.785}
    for name, (base, spread) in spreads.items():
        noise = np.random.default_rng([zlib.crc32(name.encode()), seed]).standard_normal(out[name].shape)
        drawn = base * np.exp(spread * noise) if base else spread * noise
        out[name] = jnp.asarray(drawn.astype(out[name].dtype))
    for name, factor in factors.items():
        out[name] = (out[name] * factor).astype(out[name].dtype)
    return out
```

```python
import numpy as np
import concourse.bass as bass
from concourse import mybir
from concourse.alu_op_type import AluOpType as ALU
from contextlib import ExitStack

F32 = mybir.dt.float32
F16 = mybir.dt.float16
I32 = mybir.dt.int32
ACT = mybir.ActivationFunctionType
X = mybir.AxisListType.X

NODES, EDGES, D, P = 50000, 50000, 128, 128
TYPES, BASES, LAYERS = 8, 4, 2
HEADS, HD = 8, 16
BN_EPS, EPS = 0.001, 1e-5
JN = 4
GROUP = P * JN
FULL = NODES // GROUP
TAIL_P = (NODES - FULL * GROUP) // JN
assert FULL * GROUP + TAIL_P * JN == NODES
GROUPS = FULL + 1
UT = 4
TILES = 392
STEPS = TILES // UT
EPAD = TILES * P
ZROW = EPAD
PAD_DST = 60000
CNT = D + TYPES


class Step:

    def __init__(self, unroll, i, h, parts=P):
        self.u, self.h, self.i, self.k = unroll, h, i, i * unroll + h
        self.p, self.n = parts, parts * JN


def timeline(eng, full, tail, depth, body, unroll=2):
    total = full + (1 if tail else 0)
    lo = -(-(depth - 1) // unroll) * unroll
    rounds = (full - lo) // unroll

    def peeled(t):
        def at(s):
            k = t - s
            if 0 <= k < total:
                return Step(unroll, k // unroll, k % unroll, P if k < full else TAIL_P)
        body(at)

    for t in range(lo):
        peeled(t)
    with eng.Fori(lo // unroll, lo // unroll + rounds) as i:
        for h in range(unroll):
            body(lambda s: Step(unroll, i + (h - s) // unroll, (h - s) % unroll))
    for t in range(lo + unroll * rounds, total + depth - 1):
        peeled(t)


class Phase:

    def __init__(self, nc, name):
        self.nc, self.name, self.ctx, self.sems = nc, name, ExitStack(), []

    def sem(self, name):
        s = self.nc.alloc_semaphore(f"{self.name}_{name}")
        self.sems.append(s)
        return s

    def sem2(self, name, n=2):
        return [self.sem(f"{name}{h}") for h in range(n)]

    def sb(self, name, shape, dt=F32):
        return self.ctx.enter_context(self.nc.sbuf_tensor(f"{self.name}_{name}", shape, dt))

    def sb2(self, name, shape, dt=F32, n=2):
        return [self.sb(f"{name}{h}", shape, dt) for h in range(n)]

    def ps2(self, name, shape, n=2):
        return [self.ps(f"{name}{h}", shape) for h in range(n)]

    def ps(self, name, shape, dt=F32):
        return self.ctx.enter_context(self.nc.psum_tensor(f"{self.name}_{name}", shape, dt))

    def close(self):
        self.nc.clear_and_free_semaphores(self.sems)
        self.nc.all_engine_barrier()
        self.ctx.close()


def start(eng, sems, steps=2, counts=1):
    for q in sems:
        eng.sem_inc(q, steps * counts)


def start_dma(eng, *sets):
    for sems in sets:
        for q in sems:
            eng.sem_inc(q, 16)


def after(s, back=0):
    return s.k + (1 - back + s.u)


def after_tile(s, u, back=0):
    return s.k * UT + (UT - u + (s.u - back) * UT)


def arrived(s, transfers=1):
    return (s.i + 1) * (16 * transfers) + 16


def vacated(s, transfers=1):
    return s.i * (16 * transfers) + 16


def landed(s, transfers):
    return (s.i + 1) * (16 * transfers)


def wait_indices_used(eng, gathered, s, transfers):
    if not isinstance(s.i, int) or s.i > 0:
        eng.wait_ge(gathered[s.h], s.i * (16 * transfers))


def bc(ap, n):
    ap = ap.unsqueeze(len(ap.shape))
    return ap.to_broadcast(list(ap.shape[:-1]) + [n])


def mid(ap, n):
    ap = ap.unsqueeze(1)
    return ap.to_broadcast([ap.shape[0], n] + list(ap.shape[2:]))


def group_rows(table, s):
    start = s.k * GROUP
    return table[bass.ds(start, s.n), :].rearrange("(p j) d -> p j d", j=JN)


def load_constants(nc, c, w):
    ph = Phase(nc, "const")
    loaded, made, zeroed = ph.sem("loaded"), ph.sem("made"), ph.sem("zeroed")
    with nc.Block() as block:
        @block.sync
        def _(sp):
            def load(out, in_):
                sp.dma_start(out, in_).then_inc(loaded, 16)
                return 1
            sp.wait_ge(zeroed, 1)
            n = 0
            for a, name in enumerate(("src", "dst", "edge_type_8")):
                v = w[name]
                n += load(c.rows[:, a, 0:3, :], v[0:3 * P * P].rearrange("(c p f) -> p c f", p=P, f=P))
                n += load(c.rows[0:6, a, 3, :], v[3 * P * P:3 * P * P + 6 * P].rearrange("(p f) -> p f", f=P))
                n += load(c.rows[6:7, a, 3, 0:80], v[EDGES - 80:EDGES].rearrange("(p f) -> p f", p=1))
            v = w["dst"]
            n += load(c.after[:, 0:3, :], v[1:3 * P * P + 1].rearrange("(c p f) -> p c f", p=P, f=P))
            n += load(c.after[0:6, 3, :], v[3 * P * P + 1:3 * P * P + 6 * P + 1].rearrange("(p f) -> p f", f=P))
            n += load(c.after[6:7, 3, 0:79], v[EDGES - 79:EDGES].rearrange("(p f) -> p f", p=1))
            n += load(c.w_emb[:, :], w["L0_gnn_W_emb"])
            n += load(c.b_emb[:, :], w["L0_gnn_b_emb"].partition_broadcast(P))
            for l in range(LAYERS):
                n += load(c.bases[:, l, :, :], w["L0_gnn_bases"][l].rearrange("b d f -> d b f"))
                n += load(c.loop[:, l, :], w["L0_gnn_self_loop"][l])
                n += load(c.coe[:, l, :], w["L0_gnn_w_coe"][l].rearrange("r b -> (r b)").partition_broadcast(P))
                for a, name in enumerate(("gamma", "beta", "mean", "var")):
                    n += load(c.bn[:, l, a, :], w["L0_gnn_bn_" + name][l].partition_broadcast(P))
            for a, name in enumerate(("Wq", "Wk", "Wv")):
                n += load(c.qkv[:, a * D:(a + 1) * D], w["L1_gnn_" + name])
            n += load(c.wo[:, :], w["L1_gnn_Wo"])
            n += load(c.w1[:, :], w["L1_gnn_W1"])
            n += load(c.w2[:, :, :], w["L1_gnn_W2"].rearrange("(a p) f -> p a f", p=P))
            for a in range(2):
                n += load(c.b1[:, a:a + 1], w["L1_gnn_b1"][a * P:(a + 1) * P].rearrange("(p a) -> p a", a=1))
            for a, name in enumerate(("bo", "b2", "g1", "be1", "g2", "be2")):
                n += load(c.col[:, a:a + 1], w["L1_gnn_" + name].rearrange("(p a) -> p a", a=1))
            for table, width in c.zero_rows:
                n += load(table[ZROW:ZROW + 1, :], c.zero[0:1, 0:width])
            sp.wait_ge(loaded, 16 * n)

        @block.gpsimd
        def _(pool):
            pool.memset(c.ident[:, :], 0.0).then_inc(made, 1)
            pool.memset(c.ones[:, :], 1.0).then_inc(made, 1)
            pool.memset(c.lower[:, :], 0.0).then_inc(made, 1)
            pool.wait_ge(made, 3)
            pool.affine_select(out=c.ident[:, :], in_=c.ident[:, :], compare_op=ALU.not_equal, fill=1.0,
                               base=0, pattern=[[-1, P]], channel_multiplier=1).then_inc(made, 1)
            pool.affine_select(out=c.lower[:, :], in_=c.lower[:, :], compare_op=ALU.is_ge, fill=1.0,
                               base=0, pattern=[[-1, P]], channel_multiplier=1).then_inc(made, 1)
            pool.iota(c.iota_i[:, :], pattern=[[1, TILES]], base=0, channel_multiplier=0).then_inc(made, 1)

        @block.vector
        def _(dve):
            nc.vector.memset(c.zero[:, :], 0.0)
            nc.vector.memset(c.norm[:, :], 1.0)
            nc.vector.memset(c.eps[:, 0:1], BN_EPS)
            nc.vector.memset(c.eps[:, 1:2], EPS)
            nc.vector.memset(c.rows[:, 0, 3, :], 0)
            nc.vector.memset(c.rows[:, 2, 3, :], 0)
            nc.vector.memset(c.rows[:, 1, 3, :], PAD_DST)
            nc.vector.memset(c.after[:, 3, :], PAD_DST).then_inc(zeroed, 1)
            dve.wait_ge(made, 6)
            nc.vector.tensor_copy(c.iota16[:, :], c.iota_i[:, :])
            nc.vector.tensor_copy(c.iota[:, :], c.iota_i[:, 0:TYPES])
            nc.vector.tensor_copy(c.iota1[:, :], c.iota_i[:, 1:TYPES + 1])
    ph.close()


def arrange_edges(nc, c):
    ph = Phase(nc, "arr")
    rf = ph.sb("rf", [P, 3, 4, P])
    pt = [ph.ps(f"pt{a}", [P, 4 * P]) for a in range(3)]
    floats, turned, cols, ints = ph.sem("floats"), ph.sem("turned"), ph.sem("cols"), ph.sem("ints")
    lows, roots = ph.sem("lows"), ph.sem("roots")
    b1, b2, bn1, bn2 = ph.sem("w_scale"), ph.sem("w_shift"), ph.sem("w_var"), ph.sem("w_prod")
    lo_i = ph.sb("lo_i", [P, TILES], I32)
    hi_i = ph.sb("hi_i", [P, TILES], I32)
    j_i = ph.sb("j_i", [P, TILES], I32)
    d_i = ph.sb("d_i", [P, TILES], I32)
    hi_f = ph.sb("hi_f", [P, TILES])
    with nc.Block() as block:
        @block.vector
        def _(dve):
            nc.vector.tensor_copy(rf[:, :, :, :], c.rows[:, :, :, :]).then_inc(floats, 1)
            dve.wait_ge(turned, 3)
            nc.vector.tensor_copy(c.src_i[:, :], pt[0][:, 0:TILES])
            nc.vector.tensor_copy(c.dst_f[:, :], pt[1][:, 0:TILES]).then_inc(cols, 1)
            nc.vector.tensor_copy(d_i[:, :], pt[1][:, 0:TILES]).then_inc(ints, 1)
            nc.vector.tensor_copy(c.typ_f[:, :], pt[2][:, 0:TILES])
            nc.vector.memset(c.next_f[:, TILES - 1:TILES], -1.0)
            dve.wait_ge(cols, 1)
            nc.vector.tensor_copy(c.next_f[:, 0:TILES - 1], c.dst_f[0:1, 1:TILES])
            nc.vector.tensor_scalar(c.dst_i[:, :], c.dst_f[:, :], float(NODES - 1), None, ALU.min)
            dve.wait_ge(ints, 1)
            nc.vector.tensor_scalar(lo_i[:, :], d_i[:, :], 2, P - 1, ALU.logical_shift_right, ALU.bitwise_and).then_inc(lows, 1)
            nc.vector.tensor_scalar(hi_i[:, :], d_i[:, :], 9, 2, ALU.logical_shift_right, ALU.logical_shift_left).then_inc(lows, 1)
            nc.vector.tensor_scalar(j_i[:, :], d_i[:, :], JN - 1, None, ALU.bitwise_and).then_inc(lows, 1)
            dve.wait_ge(lows, 3)
            nc.vector.tensor_copy(c.place_p[:, :], lo_i[:, :])
            nc.vector.tensor_copy(hi_f[:, :], hi_i[:, :]).then_inc(lows, 1)
            dve.wait_ge(lows, 4)
            nc.vector.tensor_tensor(c.place_f[:, :], hi_f[:, :], j_i[:, :], ALU.add)
            dve.wait_ge(roots, 1)
            for l in range(LAYERS):
                gamma, beta, mean, var = (c.bn[:, l, a, :] for a in range(4))
                nc.vector.reciprocal(var, var).then_inc(bn1, 1)
                dve.wait_ge(bn1, l + 1)
                nc.vector.tensor_tensor(gamma, gamma, var, ALU.mult).then_inc(b1, 1)
                dve.wait_ge(b1, l + 1)
                nc.vector.tensor_tensor(mean, mean, gamma, ALU.mult).then_inc(bn2, 1)
                dve.wait_ge(bn2, l + 1)
                nc.vector.tensor_tensor(beta, beta, mean, ALU.subtract).then_inc(b2, 1)
                nc.vector.tensor_tensor(c.loop[:, l, :], c.loop[:, l, :], gamma, ALU.mult)
                nc.vector.tensor_tensor(c.bases[:, l, :, :], c.bases[:, l, :, :], mid(gamma, BASES), ALU.mult)

        @block.scalar
        def _(act):
            var = c.bn[:, :, 3, :]
            nc.scalar.activation(var, var, ACT.Sqrt, bias=c.eps[:, 0:1]).then_inc(roots, 1)

        @block.tensor
        def _(pe):
            pe.wait_ge(floats, 1)
            for a in range(3):
                for q in range(4):
                    last = nc.tensor.transpose(pt[a][:, q * P:(q + 1) * P], rf[:, a, q, :], c.ident[:, :])
                last.then_inc(turned, 1)
    ph.close()


def embed_nodes(nc, c, x, h0):
    ph = Phase(nc, "emb")
    xt, xT, hs = ph.sb2("xt", [P, JN, D]), ph.sb2("xT", [P, GROUP]), ph.sb2("hs", [P, JN, D])
    hot_p, hot_f = ph.sb2("hot_p", [P, UT, P], F16), ph.sb2("hot_f", [P, UT, TILES], F16)
    zero16 = ph.sb("zero16", [P, P], F16)
    xT_ps = [ph.ps(f"xT_ps{h}", [P, GROUP]) for h in range(2)]
    h_ps = [ph.ps(f"h_ps{h}", [P, JN, D]) for h in range(2)]
    hist = ph.ps("hist", [P, TILES])
    x_in, h_out = ph.sem2("x_in"), ph.sem2("h_out")
    turned, copied, mul, biased = ph.sem("turned"), ph.sem("copied"), ph.sem("mul"), ph.sem("biased")
    hot, binned, zeroed, counted = ph.sem("hot"), ph.sem("binned"), ph.sem("zeroed"), ph.sem("counted")
    with nc.Block() as block:
        @block.sync
        def _(sp):
            start_dma(sp, x_in, h_out)

            def body(at):
                if s := at(0):
                    sp.wait_ge(turned, after(s, 2))
                    sp.dma_start(xt[s.h][0:s.p, 0:JN, :], group_rows(x, s)).then_inc(x_in[s.h], 16)
                if s := at(2):
                    sp.wait_ge(biased, after(s))
                    sp.dma_start(group_rows(h0, s), hs[s.h][0:s.p, 0:JN, :]).then_inc(h_out[s.h], 16)
            timeline(sp, FULL, True, 3, body)
            for h in range(2):
                sp.wait_ge(h_out[h], 16 + 16 * (GROUPS // 2))

        @block.tensor
        def _(pe):
            start(pe, (turned, mul, binned))
            pe.wait_ge(zeroed, 1)
            nc.tensor.matmul(hist[:, :], zero16[:, :], c.iota16[:, :], start=True, stop=False)

            def body(at):
                if s := at(0):
                    pe.wait_ge(x_in[s.h], arrived(s))
                    pe.wait_ge(copied, after(s, 2))
                    for j in range(JN):
                        last = nc.tensor.transpose(xT_ps[s.h][:, j * s.p:(j + 1) * s.p], xt[s.h][0:s.p, j, :],
                                                   c.ident[0:s.p, 0:s.p])
                    last.then_inc(turned, 1)
                if s := at(1):
                    pe.wait_ge(copied, after(s))
                    pe.wait_ge(biased, after(s, 2))
                    for j in range(JN):
                        last = nc.tensor.matmul(h_ps[s.h][0:s.p, j, :], xT[s.h][:, j * s.p:(j + 1) * s.p],
                                                c.w_emb[:, :], start=True, stop=True)
                    last.then_inc(mul, 1)
                    pe.wait_ge(hot, after(s))
                    for u in range(UT):
                        last = nc.tensor.matmul(hist[:, :], hot_p[s.h][:, u, :], hot_f[s.h][:, u, :],
                                                start=False, stop=False)
                    last.then_inc(binned, 1)
            timeline(pe, FULL, True, 2, body)
            nc.tensor.matmul(hist[:, :], zero16[:, :], c.iota16[:, :], start=False, stop=True).then_inc(counted, 1)

        @block.scalar
        def _(act):
            start(act, (copied,))

            def body(at):
                if s := at(0):
                    act.wait_ge(turned, after(s))
                    act.wait_ge(mul, after(s, 2))
                    nc.scalar.copy(xT[s.h][:, 0:s.n], xT_ps[s.h][:, 0:s.n]).then_inc(copied, 1)
            timeline(act, FULL, True, 1, body)

        @block.vector
        def _(dve):
            start(dve, (biased, hot))
            nc.vector.memset(zero16[:, :], 0.0).then_inc(zeroed, 1)

            def body(at):
                if s := at(0):
                    dve.wait_ge(binned, after(s, 2))
                    for u in range(UT):
                        t = s.k * UT + u
                        nc.vector.tensor_scalar(hot_p[s.h][:, u, :], c.iota16[:, 0:P],
                                                c.place_p[:, bass.ds(t, 1)], None, ALU.is_equal)
                        last = nc.vector.tensor_scalar(hot_f[s.h][:, u, :], c.iota16[:, :],
                                                       c.place_f[:, bass.ds(t, 1)], None, ALU.is_equal)
                    last.then_inc(hot, 1)
                if s := at(1):
                    dve.wait_ge(mul, after(s))
                    dve.wait_ge(h_out[s.h], vacated(s))
                    nc.vector.tensor_tensor(hs[s.h][0:s.p, 0:JN, :], h_ps[s.h][0:s.p, 0:JN, :],
                                            mid(c.b_emb[0:s.p, :], JN), ALU.add).then_inc(biased, 1)
            timeline(dve, FULL, True, 2, body)
            dve.wait_ge(counted, 1)
            nc.vector.tensor_copy(c.count[:, :], hist[:, :])
    ph.close()


def index_nodes(nc, c):
    ph = Phase(nc, "idx")
    rows = ph.sb("rows", [P, GROUPS])
    totals = ph.sb("totals", [GROUPS, P])
    base = ph.sb("base", [P, GROUPS])
    first, some, off = (ph.sb(n, [P, GROUPS, JN]) for n in ("first", "some", "off"))
    ps_t, ps_b, ps_g = ph.ps("ps_t", [GROUPS, P]), ph.ps("ps_b", [P, GROUPS]), ph.ps("ps_g", [P, GROUPS])
    summed, products, link = ph.sem("summed"), ph.sem("products"), ph.sem("link")
    count = c.count[:, :].rearrange("p (g j) -> p g j", j=JN)
    with nc.Block() as block:
        @block.tensor
        def _(pe):
            pe.wait_ge(summed, 1)
            nc.tensor.matmul(ps_t[:, :], rows[:, :], c.ones[:, :], start=True, stop=True).then_inc(products, 1)
            nc.tensor.matmul(ps_b[:, :], c.lower[:, :], rows[:, :], start=True, stop=True).then_inc(products, 1)
            pe.wait_ge(summed, 2)
            nc.tensor.matmul(ps_g[:, :], totals[:, :], c.lower[0:GROUPS, 0:GROUPS], start=True, stop=True)\
              .then_inc(products, 1)

        @block.vector
        def _(dve):
            links = [0]

            def chain(op):
                links[0] += 1
                op.then_inc(link, 1)
                dve.wait_ge(link, links[0])
            nc.vector.tensor_reduce(rows[:, :], count, X, ALU.add).then_inc(summed, 1)
            dve.wait_ge(products, 1)
            nc.vector.tensor_copy(totals[:, :], ps_t[:, :]).then_inc(summed, 1)
            dve.wait_ge(products, 2)
            chain(nc.vector.tensor_copy(base[:, :], ps_b[:, :]))
            dve.wait_ge(products, 3)
            chain(nc.vector.tensor_tensor(first[:, :, 0], base[:, :], ps_g[:, :], ALU.add))
            for j in range(1, JN):
                chain(nc.vector.tensor_tensor(first[:, :, j], first[:, :, j - 1], count[:, :, j - 1], ALU.add))
            chain(nc.vector.tensor_scalar(some[:, :, :], count, 0.0, None, ALU.is_gt))
            chain(nc.vector.tensor_scalar(off[:, :, :], first[:, :, :], -float(ZROW), None, ALU.add))
            chain(nc.vector.tensor_tensor(off[:, :, :], off[:, :, :], some[:, :, :], ALU.mult))
            nc.vector.tensor_scalar(c.start_i[:, :].rearrange("p (g j) -> p g j", j=JN), off[:, :, :], float(ZROW),
                                    None, ALU.add)
    ph.close()


def tile_columns(s):
    return (STEPS - 1 - s.k) * UT if isinstance(s.k, int) else (STEPS - 1) * UT - s.k * UT


def tile_rows(table, s):
    return table[bass.ds(tile_columns(s) * P, UT * P), :].rearrange("(u p) d -> p u d", p=P)


UP = tuple(range(UT - 1, -1, -1))


def conv_edges(nc, c, layer, nodes, table, width):
    ph = Phase(nc, f"conv{layer}")
    src4, dst4, next4 = ph.sb2("src4", [P, UT], I32), ph.sb2("dst4", [P, UT]), ph.sb2("next4", [1, UT])
    hot, prod, coe = ph.sb2("hot", [P, UT, TYPES]), ph.sb("prod", [P, UT, BASES, TYPES]), ph.sb2("coe", [P, UT, BASES])
    xg, xT = ph.sb2("xg", [P, UT, D]), ph.sb2("xT", [P, UT, P])
    same, join = ph.sb2("same", [P, UT, P]), ph.sb2("join", [1, UT, P])
    val, out = ph.sb2("val", [P, UT, width]), ph.sb2("out", [P, UT, width])
    part = ph.sb("part", [P, UT, BASES - 1, D])
    dst_ps, xT_ps = ph.ps("dst_ps", [P, UT, P]), ph.ps("xT_ps", [P, UT, P])
    mul_ps = [ph.ps(f"mul_ps{u}", [P, BASES, D]) for u in range(UT)]
    sum_ps = ph.ps("sum_ps", [P, UT, 256])
    gathered, stored, pace, pace_out = ph.sem2("gathered"), ph.sem2("stored"), ph.sem("pace"), ph.sem("pace_out")
    src_set, dst_set, hot_set, prod_set, coe_set = (
        ph.sem(n) for n in ("src_set", "dst_set", "hot_set", "prod_set", "coe_set"))
    dst_turned, x_turned, xT_set, same_set = (ph.sem(n) for n in ("dst_turned", "x_turned", "xT_set", "same_set"))
    mul, scaled, added, val_set, summed, out_set = (
        ph.sem(n) for n in ("mul", "scaled", "added", "val_set", "summed", "out_set"))
    with nc.Block() as block:
        @block.gpsimd
        def _(pool):
            def body(at):
                if s := at(0):
                    pool.wait_ge(x_turned, after(s, 2))
                    pool.wait_ge(src_set, after(s))
                    pool.sem_inc(pace, 1)
                    for u in UP:
                        pool.indirect_dma_start(out=xg[s.h][:, u, :], out_offset=None, in_=nodes,
                                                in_offset=bass.IndirectOffsetOnAxis(ap=src4[s.h][:, u:u + 1], axis=0))\
                            .then_inc(gathered[s.h], 16)
            timeline(pool, STEPS, False, 1, body)

        @block.vector
        def _(dve):
            start(dve, (src_set, dst_set, hot_set, prod_set, coe_set, same_set))
            start(dve, (val_set,), counts=UT)

            def body(at):
                if s := at(0):
                    wait_indices_used(dve, gathered, s, UT)
                    nc.vector.tensor_copy(src4[s.h][:, :], c.src_i[:, bass.ds(tile_columns(s), UT)]).then_inc(src_set, 1)
                if s := at(1):
                    t = bass.ds(tile_columns(s), UT)
                    dve.wait_ge(dst_turned, after(s, 2))
                    nc.vector.tensor_copy(next4[s.h][:, :], c.next_f[:, t])
                    nc.vector.tensor_copy(dst4[s.h][:, :], c.dst_f[:, t]).then_inc(dst_set, 1)
                    nc.vector.tensor_tensor(hot[s.h][:, :, :], bc(c.typ_f[:, t], TYPES), mid(c.iota[:, :], UT),
                                            ALU.is_equal).then_inc(hot_set, 1)
                    w = c.coe[:, layer, :].rearrange("p (r b) -> p b r", b=BASES)
                    dve.wait_ge(hot_set, after(s))
                    for u in range(UT):
                        last = nc.vector.tensor_tensor(prod[:, u, :, :], mid(hot[s.h][:, u, :], BASES), w, ALU.mult)
                    last.then_inc(prod_set, 1)
                    dve.wait_ge(scaled, after_tile(s, 0, 2))
                    dve.wait_ge(prod_set, after(s))
                    nc.vector.tensor_reduce(coe[s.h][:, :, :], prod[:, :, :, :], X, ALU.add).then_inc(coe_set, 1)
                if s := at(2):
                    dve.wait_ge(summed, after_tile(s, 0, 2))
                    if width > D:
                        nc.vector.tensor_copy(val[s.h][:, :, D:], hot[s.h][:, :, :])
                    n = 0
                    for pair in (UP[0:2], UP[2:4]):
                        for b in range(1, BASES):
                            for u in pair:
                                if b == 1:
                                    dve.wait_ge(scaled, after_tile(s, u))
                                else:
                                    n += 1
                                    dve.wait_ge(added, s.k * (2 * UT) + n)
                                into = val[s.h][:, u, 0:D] if b == BASES - 1 else part[:, u, b, :]
                                nc.vector.scalar_tensor_tensor(into, mul_ps[u][:, b, :], coe[s.h][:, u, b:b + 1],
                                                               part[:, u, b - 1, :], ALU.mult, ALU.add)\
                                    .then_inc(val_set if b == BASES - 1 else added, 1)
                if s := at(1):
                    dve.wait_ge(summed, after_tile(s, 0, 2))
                    dve.wait_ge(dst_turned, after(s))
                    nc.vector.tensor_tensor(join[s.h][:, :, :], dst_ps[0:1, :, :], bc(next4[s.h][:, :], P), ALU.is_equal)
                    nc.vector.tensor_tensor(same[s.h][:, :, :], dst_ps[:, :, :], bc(dst4[s.h][:, :], P), ALU.is_equal)\
                        .then_inc(same_set, 1)
            timeline(dve, STEPS, False, 3, body)

        @block.scalar
        def _(act):
            start(act, (xT_set,))
            start(act, (scaled, out_set), counts=UT)

            def body(at):
                for u in UP:
                    if s := at(2):
                        if u == UP[0]:
                            act.wait_ge(coe_set, after(s))
                        act.wait_ge(val_set, after_tile(s, u, 1))
                        act.wait_ge(mul, after_tile(s, u))
                        nc.scalar.activation(part[:, u, 0, :], mul_ps[u][:, 0, :], ACT.Copy, scale=coe[s.h][:, u, 0:1])\
                            .then_inc(scaled, 1)
                    if s := at(3):
                        if u == UP[0]:
                            act.wait_ge(stored[s.h], vacated(s))
                        act.wait_ge(summed, after_tile(s, u))
                        nc.scalar.copy(out[s.h][:, u, :], sum_ps[:, u, 0:width]).then_inc(out_set, 1)
                if s := at(1):
                    act.wait_ge(mul, after_tile(s, 0, 2))
                    act.wait_ge(x_turned, after(s))
                    nc.scalar.copy(xT[s.h][:, :, :], xT_ps[:, :, :]).then_inc(xT_set, 1)
            timeline(act, STEPS, False, 4, body)

        @block.tensor
        def _(pe):
            start(pe, (dst_turned, x_turned))
            start(pe, (mul, summed), counts=UT)
            basis = c.bases[:, layer, :, :].rearrange("p b d -> p (b d)")

            def body(at):
                for u in UP:
                    if s := at(2):
                        if u == UP[0]:
                            pe.wait_ge(xT_set, after(s))
                        pe.wait_ge(val_set, after_tile(s, u, 1))
                        nc.tensor.matmul(mul_ps[u][:, :, :].rearrange("p b d -> p (b d)"), xT[s.h][:, u, :], basis,
                                         start=True, stop=True).then_inc(mul, 1)
                    if s := at(3):
                        first = isinstance(s.k, int) and s.k == 0 and u == UP[0]
                        if u == UP[0]:
                            pe.wait_ge(same_set, after(s))
                        pe.wait_ge(val_set, after_tile(s, u))
                        pe.wait_ge(out_set, after_tile(s, u) - 1)
                        total = nc.tensor.matmul(sum_ps[:, u, 0:width], same[s.h][:, u, :], val[s.h][:, u, :],
                                                 start=True, stop=first)
                        if not first:
                            above = out[1 - s.h][0:1, 0, :] if u == UP[0] else out[s.h][0:1, u + 1, :]
                            total = nc.tensor.matmul(sum_ps[:, u, 0:width], join[s.h][:, u, :], above,
                                                     start=False, stop=True)
                        total.then_inc(summed, 1)
                if s := at(1):
                    turn_targets(nc, c, pe, s, dst4, dst_set, dst_ps, same_set, dst_turned)
                    pe.wait_ge(xT_set, after(s, 1))
                    pe.wait_ge(gathered[s.h], landed(s, UT))
                    for u in UP:
                        last = nc.tensor.transpose(xT_ps[:, u, :], xg[s.h][:, u, :], c.ident[:, :])
                    last.then_inc(x_turned, 1)
            timeline(pe, STEPS, False, 4, body)

        @block.sync
        def _(sp):
            start_dma(sp, stored)

            def body(at):
                if s := at(0):
                    sp.wait_ge(out_set, after_tile(s, 0))
                    sp.sem_inc(pace_out, 1)
                    sp.dma_start(tile_rows(table, s), out[s.h][:, :, :]).then_inc(stored[s.h], 16)
            timeline(sp, STEPS, False, 1, body)
            for h in range(2):
                sp.wait_ge(stored[h], 16 + 16 * (STEPS // 2))
    ph.close()


def turn_targets(nc, c, pe, s, dst4, dst_set, dst_ps, same_set, dst_turned):
    pe.wait_ge(same_set, after(s, 1))
    pe.wait_ge(dst_set, after(s))
    for u in UP:
        last = nc.tensor.transpose(dst_ps[:, u, :], dst4[s.h][:, u:u + 1].to_broadcast([P, P]), c.ident[:, :])
    last.then_inc(dst_turned, 1)


def attend_edges(nc, c, q, kv, table):
    ph = Phase(nc, "att")
    src4, dsti4 = ph.sb2("src4", [P, UT], I32), ph.sb2("dsti4", [P, UT], I32)
    dst4, next4 = ph.sb2("dst4", [P, UT]), ph.sb2("next4", [1, UT])
    qg, kvg = ph.sb2("qg", [P, UT, D]), ph.sb2("kvg", [P, UT, 2 * D])
    qk, score = ph.sb("qk", [P, UT, D]), ph.sb2("score", [P, UT, HEADS])
    same, join = ph.sb2("same", [P, UT, P]), ph.sb2("join", [1, UT, P])
    val, out = ph.sb2("val", [P, UT, CNT]), ph.sb2("out", [P, UT, CNT])
    dst_ps, sum_ps = ph.ps("dst_ps", [P, UT, P]), ph.ps("sum_ps", [P, UT, 256])
    gathered, stored, pace, pace_out = ph.sem2("gathered"), ph.sem2("stored"), ph.sem("pace"), ph.sem("pace_out")
    idx_set, dst_set, dst_turned, same_set = (ph.sem(n) for n in ("idx_set", "dst_set", "dst_turned", "same_set"))
    qk_set, dots_set, score_set, low_set, exp_set, val_set = (
        ph.sem(n) for n in ("qk_set", "dots_set", "score_set", "low_set", "exp_set", "val_set"))
    summed, out_set = ph.sem("summed"), ph.sem("out_set")
    loads = 2 * UT
    with nc.Block() as block:
        @block.gpsimd
        def _(pool):
            def body(at):
                if s := at(0):
                    pool.wait_ge(val_set, after(s, 2))
                    pool.wait_ge(idx_set, after(s))
                    pool.sem_inc(pace, 1)
                    for u in UP:
                        for into, rows, idx in ((qg, q, dsti4), (kvg, kv, src4)):
                            pool.indirect_dma_start(out=into[s.h][:, u, :], out_offset=None, in_=rows,
                                                    in_offset=bass.IndirectOffsetOnAxis(ap=idx[s.h][:, u:u + 1], axis=0))\
                                .then_inc(gathered[s.h], 16)
            timeline(pool, STEPS, False, 1, body)

        @block.vector
        def _(dve):
            start(dve, (idx_set, dst_set, same_set, qk_set, dots_set, score_set, low_set, val_set))

            def body(at):
                if s := at(0):
                    t = bass.ds(tile_columns(s), UT)
                    wait_indices_used(dve, gathered, s, loads)
                    nc.vector.tensor_copy(src4[s.h][:, :], c.src_i[:, t])
                    nc.vector.tensor_copy(dsti4[s.h][:, :], c.dst_i[:, t]).then_inc(idx_set, 1)
                if s := at(1):
                    t = bass.ds(tile_columns(s), UT)
                    dve.wait_ge(dst_turned, after(s, 2))
                    nc.vector.tensor_copy(next4[s.h][:, :], c.next_f[:, t])
                    nc.vector.tensor_copy(dst4[s.h][:, :], c.dst_f[:, t]).then_inc(dst_set, 1)
                    dve.wait_ge(gathered[s.h], landed(s, loads))
                    nc.vector.tensor_tensor(qk[:, :, :], qg[s.h][:, :, :], kvg[s.h][:, :, 0:D], ALU.mult).then_inc(qk_set, 1)
                    dve.wait_ge(qk_set, after(s))
                    nc.vector.tensor_reduce(score[s.h][:, :, :], qk[:, :, :].rearrange("p u (h e) -> p u h e", e=HD), X,
                                            ALU.add).then_inc(dots_set, 1)
                    dve.wait_ge(dots_set, after(s))
                    nc.vector.tensor_scalar(score[s.h][:, :, :], score[s.h][:, :, :], 1.0 / HD ** 0.5, 5.0, ALU.mult,
                                            ALU.min).then_inc(low_set, 1)
                    dve.wait_ge(low_set, after(s))
                    nc.vector.tensor_scalar(score[s.h][:, :, :], score[s.h][:, :, :], -5.0, None, ALU.max)\
                        .then_inc(score_set, 1)
                    dve.wait_ge(summed, after_tile(s, 0, 2))
                    dve.wait_ge(dst_turned, after(s))
                    nc.vector.tensor_tensor(join[s.h][:, :, :], dst_ps[0:1, :, :], bc(next4[s.h][:, :], P), ALU.is_equal)
                    nc.vector.tensor_tensor(same[s.h][:, :, :], dst_ps[:, :, :], bc(dst4[s.h][:, :], P), ALU.is_equal)\
                        .then_inc(same_set, 1)
                    dve.wait_ge(exp_set, after(s))
                    for u in UP:
                        last = nc.vector.tensor_tensor(val[s.h][:, u, 0:D].rearrange("p (h e) -> p h e", e=HD),
                                                       kvg[s.h][:, u, D:].rearrange("p (h e) -> p h e", e=HD),
                                                       bc(val[s.h][:, u, D:], HD), ALU.mult)
                    last.then_inc(val_set, 1)
            timeline(dve, STEPS, False, 2, body)

        @block.scalar
        def _(act):
            start(act, (exp_set,))
            start(act, (out_set,), counts=UT)

            def body(at):
                if s := at(0):
                    act.wait_ge(summed, after_tile(s, 0, 2))
                    act.wait_ge(score_set, after(s))
                    nc.scalar.activation(val[s.h][:, :, D:], score[s.h][:, :, :], ACT.Exp).then_inc(exp_set, 1)
                if s := at(1):
                    for u in UP:
                        if u == UP[0]:
                            act.wait_ge(stored[s.h], vacated(s))
                        act.wait_ge(summed, after_tile(s, u))
                        nc.scalar.copy(out[s.h][:, u, :], sum_ps[:, u, 0:CNT]).then_inc(out_set, 1)
            timeline(act, STEPS, False, 2, body)

        @block.tensor
        def _(pe):
            start(pe, (dst_turned,))
            start(pe, (summed,), counts=UT)

            def body(at):
                if s := at(0):
                    turn_targets(nc, c, pe, s, dst4, dst_set, dst_ps, same_set, dst_turned)
                if s := at(1):
                    pe.wait_ge(same_set, after(s))
                    pe.wait_ge(val_set, after(s))
                    for u in UP:
                        first = isinstance(s.k, int) and s.k == 0 and u == UP[0]
                        pe.wait_ge(out_set, after_tile(s, u) - 1)
                        total = nc.tensor.matmul(sum_ps[:, u, 0:CNT], same[s.h][:, u, :], val[s.h][:, u, :],
                                                 start=True, stop=first)
                        if not first:
                            above = out[1 - s.h][0:1, 0, :] if u == UP[0] else out[s.h][0:1, u + 1, :]
                            total = nc.tensor.matmul(sum_ps[:, u, 0:CNT], join[s.h][:, u, :], above,
                                                     start=False, stop=True)
                        total.then_inc(summed, 1)
            timeline(pe, STEPS, False, 2, body)

        @block.sync
        def _(sp):
            start_dma(sp, stored)

            def body(at):
                if s := at(0):
                    sp.wait_ge(out_set, after_tile(s, 0))
                    sp.sem_inc(pace_out, 1)
                    sp.dma_start(tile_rows(table, s), out[s.h][:, :, :]).then_inc(stored[s.h], 16)
            timeline(sp, STEPS, False, 1, body)
            for h in range(2):
                sp.wait_ge(stored[h], 16 + 16 * (STEPS // 2))
    ph.close()


def gather_groups(nc, c, pool, table, into, idx4, idx_set, used, gathered, pace):
    def body(at):
        if s := at(0):
            pool.wait_ge(used, after(s, 2))
            pool.wait_ge(idx_set, after(s))
            pool.sem_inc(pace, 1)
            for j in range(JN):
                pool.indirect_dma_start(out=into[s.h][0:s.p, j, :], out_offset=None, in_=table,
                                        in_offset=bass.IndirectOffsetOnAxis(ap=idx4[s.h][0:s.p, j:j + 1], axis=0))\
                    .then_inc(gathered[s.h], 16)
    timeline(pool, FULL, True, 1, body)


def turn(nc, c, ps, rows, s):
    for j in range(JN):
        last = nc.tensor.transpose(ps[:, j * s.p:(j + 1) * s.p], rows[0:s.p, j, :], c.ident[0:s.p, 0:s.p])
    return last


def update_nodes(nc, c, h_in, table, h_out):
    ph = Phase(nc, "node0")
    idx4 = ph.sb2("idx4", [P, JN], I32)
    ag, ht, hT, hs = ph.sb2("ag", [P, JN, CNT]), ph.sb2("ht", [P, JN, D]), ph.sb2("hT", [P, GROUP]), ph.sb2("hs", [P, JN, D])
    rank, top, norm = ph.sb("rank", [P, JN, TYPES]), ph.sb("top", [P, JN]), ph.sb("norm", [P, JN])
    z = ph.sb2("z", [P, JN, D])
    hT_ps, mul_ps = ph.ps2("hT_ps", [P, GROUP]), ph.ps2("mul_ps", [P, JN, D])
    h_in_s, gathered, stored = ph.sem2("h_in"), ph.sem2("gathered"), ph.sem2("stored")
    pace, idx_set, turned, copied, mul = (ph.sem(n) for n in ("pace", "idx_set", "turned", "copied", "mul"))
    norm_step, scaled, shifted, rectified = (ph.sem(n) for n in ("norm_step", "scaled", "shifted", "rectified"))
    LINKS = 8
    with nc.Block() as block:
        @block.gpsimd
        def _(pool):
            gather_groups(nc, c, pool, table, ag, idx4, idx_set, shifted, gathered, pace)

        @block.sync
        def _(sp):
            start_dma(sp, h_in_s, stored)

            def body(at):
                if s := at(0):
                    sp.wait_ge(turned, after(s, 2))
                    sp.dma_start(ht[s.h][0:s.p, :, :], group_rows(h_in, s)).then_inc(h_in_s[s.h], 16)
                if s := at(2):
                    sp.wait_ge(rectified, after(s))
                    sp.dma_start(group_rows(h_out, s), hs[s.h][0:s.p, :, :]).then_inc(stored[s.h], 16)
            timeline(sp, FULL, True, 3, body)
            for h in range(2):
                sp.wait_ge(stored[h], 16 + 16 * (GROUPS // 2))

        @block.tensor
        def _(pe):
            start(pe, (turned, mul))

            def body(at):
                if s := at(0):
                    pe.wait_ge(h_in_s[s.h], arrived(s))
                    pe.wait_ge(copied, after(s, 2))
                    turn(nc, c, hT_ps[s.h], ht[s.h], s).then_inc(turned, 1)
                if s := at(1):
                    pe.wait_ge(copied, after(s))
                    pe.wait_ge(scaled, after(s, 2))
                    for j in range(JN):
                        last = nc.tensor.matmul(mul_ps[s.h][0:s.p, j, :], hT[s.h][:, j * s.p:(j + 1) * s.p],
                                                c.loop[:, 0, :], start=True, stop=True)
                    last.then_inc(mul, 1)
            timeline(pe, FULL, True, 2, body)

        @block.scalar
        def _(act):
            start(act, (copied, rectified))

            def body(at):
                if s := at(0):
                    act.wait_ge(mul, after(s, 2))
                    act.wait_ge(turned, after(s))
                    nc.scalar.copy(hT[s.h][:, 0:s.n], hT_ps[s.h][:, 0:s.n]).then_inc(copied, 1)
                if s := at(1):
                    act.wait_ge(stored[s.h], vacated(s))
                    act.wait_ge(shifted, after(s))
                    nc.scalar.activation(hs[s.h][0:s.p, :, :], z[s.h][0:s.p, :, :], ACT.Relu).then_inc(rectified, 1)
            timeline(act, FULL, True, 2, body)

        @block.vector
        def _(dve):
            start(dve, (idx_set, scaled, shifted))

            def body(at):
                if s := at(0):
                    wait_indices_used(dve, gathered, s, JN)
                    nc.vector.tensor_copy(idx4[s.h][:, :], c.start_i[:, bass.ds(s.k * JN, JN)]).then_inc(idx_set, 1)
                if s := at(1):
                    p, n = s.p, 0
                    counts = ag[s.h][0:p, :, D:]
                    steps = [
                        lambda: nc.vector.tensor_scalar(rank[0:p, :, :], counts, 0.0, None, ALU.is_gt),
                        lambda: nc.vector.tensor_tensor(rank[0:p, :, :], rank[0:p, :, :], mid(c.iota1[0:p, :], JN), ALU.mult),
                        lambda: nc.vector.tensor_reduce(top[0:p, :], rank[0:p, :, :], X, ALU.max),
                        lambda: nc.vector.tensor_tensor(rank[0:p, :, :], rank[0:p, :, :], bc(top[0:p, :], TYPES), ALU.is_equal),
                        lambda: nc.vector.tensor_tensor(rank[0:p, :, :], rank[0:p, :, :], counts, ALU.mult),
                        lambda: nc.vector.tensor_reduce(top[0:p, :], rank[0:p, :, :], X, ALU.add),
                        lambda: nc.vector.tensor_scalar(top[0:p, :], top[0:p, :], 1.0, None, ALU.max),
                        lambda: nc.vector.reciprocal(top[0:p, :], top[0:p, :]),
                    ]
                    dve.wait_ge(gathered[s.h], landed(s, JN))
                    for step in steps:
                        n += 1
                        step().then_inc(norm_step, 1)
                        dve.wait_ge(norm_step, s.k * LINKS + n)
                    nc.vector.tensor_copy(c.norm[0:p, bass.ds(s.k * JN, JN)], top[0:p, :])
                    dve.wait_ge(mul, after(s))
                    dve.wait_ge(rectified, after(s, 2))
                    for j in range(JN):
                        last = nc.vector.scalar_tensor_tensor(z[s.h][0:p, j, :], ag[s.h][0:p, j, 0:D], top[0:p, j:j + 1],
                                                              mul_ps[s.h][0:p, j, :], ALU.mult, ALU.add)
                    last.then_inc(scaled, 1)
                    dve.wait_ge(scaled, after(s))
                    nc.vector.tensor_tensor(z[s.h][0:p, :, :], z[s.h][0:p, :, :], mid(c.bn[0:p, 0, 1, :], JN), ALU.add)\
                        .then_inc(shifted, 1)
            timeline(dve, FULL, True, 2, body)
    ph.close()


def finish_conv(nc, c, x, h_in, table, xT_out, q_out, kv_out):
    ph = Phase(nc, "node1")
    idx4, norm4 = ph.sb2("idx4", [P, JN], I32), ph.sb2("norm4", [P, JN])
    ag, ht, xt, hT = ph.sb2("ag", [P, JN, D]), ph.sb2("ht", [P, JN, D]), ph.sb2("xt", [P, JN, D]), ph.sb2("hT", [P, GROUP])
    z, x1, x1T = ph.sb2("z", [P, JN, D]), ph.sb2("x1", [P, JN, D]), ph.sb2("x1T", [P, GROUP])
    qkv = ph.sb2("qkv", [P, JN, 3 * D])
    stats, mv, sd, rstd = ph.sb("stats", [P, JN, 6]), ph.sb2("mv", [P, JN, 2]), ph.sb2("sd", [P, JN]), ph.sb("rstd", [P, JN])
    hT_ps, mul_ps, x1T_ps = ph.ps("hT_ps", [P, GROUP]), ph.ps2("mul_ps", [P, JN, D]), ph.ps("x1T_ps", [P, GROUP])
    qkv_ps = [ph.ps(f"qkv_ps{j}", [P, 3 * D]) for j in range(JN)]
    h_in_s, x_in, gathered = ph.sem2("h_in"), ph.sem2("x_in"), ph.sem2("gathered")
    xT_st, qkv_st, pace_bn = ph.sem2("xT_st"), ph.sem2("qkv_st"), ph.sem("pace_bn")
    pace, idx_set, turned, copied, mul = (ph.sem(n) for n in ("pace", "idx_set", "turned", "copied", "mul"))
    scaled, shifted, summed, counted, mv_set, sd_set, rstd_set, x1_set = (
        ph.sem(n) for n in ("scaled", "shifted", "summed", "counted", "mv_set", "sd_set", "rstd_set", "x1_set"))
    x1_turned, x1_copied, qkv_mul, qkv_copied = (ph.sem(n) for n in ("x1_turned", "x1_copied", "qkv_mul", "qkv_copied"))
    with nc.Block() as block:
        @block.gpsimd
        def _(pool):
            gather_groups(nc, c, pool, table, ag, idx4, idx_set, scaled, gathered, pace)

        @block.sync
        def _(sp):
            start_dma(sp, h_in_s, x_in, xT_st, qkv_st)

            def body(at):
                if s := at(0):
                    sp.wait_ge(turned, after(s, 2))
                    sp.dma_start(ht[s.h][0:s.p, :, :], group_rows(h_in, s)).then_inc(h_in_s[s.h], 16)
                    sp.wait_ge(summed, after(s, 2))
                    sp.dma_start(xt[s.h][0:s.p, :, :], group_rows(x, s)).then_inc(x_in[s.h], 16)
                if s := at(3):
                    sp.wait_ge(x1_copied, after(s))
                    sp.dma_start(group_cols(xT_out, s), x1T[s.h][:, 0:s.n]).then_inc(xT_st[s.h], 16)
                if s := at(4):
                    sp.wait_ge(qkv_copied, after_tile(s, 0))
                    sp.dma_start(group_rows(q_out, s), qkv[s.h][0:s.p, :, 0:D]).then_inc(qkv_st[s.h], 16)
                    sp.dma_start(group_rows(kv_out, s), qkv[s.h][0:s.p, :, D:]).then_inc(qkv_st[s.h], 16)
            timeline(sp, FULL, True, 5, body)
            for h in range(2):
                sp.wait_ge(xT_st[h], 16 + 16 * (GROUPS // 2))
                sp.wait_ge(qkv_st[h], 16 + 32 * (GROUPS // 2))

        @block.tensor
        def _(pe):
            start(pe, (turned, mul, x1_turned))
            start(pe, (qkv_mul,), counts=UT)

            def body(at):
                if s := at(0):
                    pe.wait_ge(h_in_s[s.h], arrived(s))
                    pe.wait_ge(copied, after(s, 1))
                    turn(nc, c, hT_ps, ht[s.h], s).then_inc(turned, 1)
                if s := at(1):
                    pe.wait_ge(copied, after(s))
                    pe.wait_ge(scaled, after(s, 2))
                    for j in range(JN):
                        last = nc.tensor.matmul(mul_ps[s.h][0:s.p, j, :], hT[s.h][:, j * s.p:(j + 1) * s.p],
                                                c.loop[:, 1, :], start=True, stop=True)
                    last.then_inc(mul, 1)
                if s := at(2):
                    pe.wait_ge(x1_set, after(s))
                    pe.wait_ge(x1_copied, after(s, 1))
                    turn(nc, c, x1T_ps, x1[s.h], s).then_inc(x1_turned, 1)
                if s := at(3):
                    pe.wait_ge(x1_copied, after(s))
                    for n, u in enumerate(UP):
                        pe.wait_ge(qkv_copied, after_tile(s, u, 1))
                        nc.tensor.matmul(qkv_ps[n][0:s.p, :], x1T[s.h][:, n * s.p:(n + 1) * s.p], c.qkv[:, :],
                                         start=True, stop=True).then_inc(qkv_mul, 1)
            timeline(pe, FULL, True, 4, body)

        @block.scalar
        def _(act):
            start(act, (copied, x1_copied, sd_set))
            start(act, (qkv_copied,), counts=UT)

            def body(at):
                if s := at(0):
                    act.wait_ge(mul, after(s, 2))
                    act.wait_ge(turned, after(s))
                    nc.scalar.copy(hT[s.h][:, 0:s.n], hT_ps[:, 0:s.n]).then_inc(copied, 1)
                if s := at(2):
                    act.wait_ge(qkv_mul, after_tile(s, 0, 2))
                    act.wait_ge(xT_st[s.h], vacated(s))
                    act.wait_ge(x1_turned, after(s))
                    nc.scalar.copy(x1T[s.h][:, 0:s.n], x1T_ps[:, 0:s.n]).then_inc(x1_copied, 1)
                if s := at(3):
                    act.wait_ge(qkv_st[s.h], vacated(s, 2))
                    for n, u in enumerate(UP):
                        act.wait_ge(qkv_mul, after_tile(s, u))
                        nc.scalar.copy(qkv[s.h][0:s.p, n, :], qkv_ps[n][0:s.p, :]).then_inc(qkv_copied, 1)
                if s := at(1):
                    act.wait_ge(rstd_set, after(s, 2))
                    act.wait_ge(mv_set, after(s))
                    nc.scalar.activation(sd[s.h][0:s.p, :], mv[s.h][0:s.p, :, 1], ACT.Sqrt, bias=c.eps[0:s.p, 1:2])\
                        .then_inc(sd_set, 1)
            timeline(act, FULL, True, 4, body)

        @block.vector
        def _(dve):
            start(dve, (idx_set, scaled, shifted, summed, counted, mv_set, rstd_set, x1_set))

            def body(at):
                if s := at(0):
                    wait_indices_used(dve, gathered, s, JN)
                    nc.vector.tensor_copy(norm4[s.h][:, :], c.norm[:, bass.ds(s.k * JN, JN)])
                    nc.vector.tensor_copy(idx4[s.h][:, :], c.start_i[:, bass.ds(s.k * JN, JN)]).then_inc(idx_set, 1)
                if s := at(2):
                    p = s.p
                    dve.wait_ge(sd_set, after(s))
                    nc.vector.reciprocal(rstd[0:p, :], sd[s.h][0:p, :]).then_inc(rstd_set, 1)
                    dve.wait_ge(x1_turned, after(s, 2))
                    dve.wait_ge(rstd_set, after(s))
                    for j in range(JN):
                        last = nc.vector.tensor_scalar(x1[s.h][0:p, j, :], z[s.h][0:p, j, :], mv[s.h][0:p, j, 0:1],
                                                       rstd[0:p, j:j + 1], ALU.subtract, ALU.mult)
                    last.then_inc(x1_set, 1)
                if s := at(1):
                    p, r = s.p, z[s.h]
                    dve.wait_ge(idx_set, after(s))
                    dve.wait_ge(gathered[s.h], landed(s, JN))
                    dve.wait_ge(mul, after(s))
                    for j in range(JN):
                        last = nc.vector.scalar_tensor_tensor(r[0:p, j, :], ag[s.h][0:p, j, :], norm4[s.h][0:p, j:j + 1],
                                                              mul_ps[s.h][0:p, j, :], ALU.mult, ALU.add)
                    last.then_inc(scaled, 1)
                    dve.wait_ge(scaled, after(s))
                    nc.vector.tensor_tensor(r[0:p, :, :], r[0:p, :, :], mid(c.bn[0:p, 1, 1, :], JN), ALU.add)\
                        .then_inc(shifted, 1)
                    dve.wait_ge(shifted, after(s))
                    dve.wait_ge(x_in[s.h], arrived(s))
                    nc.vector.scalar_tensor_tensor(r[0:p, :, :], r[0:p, :, :], 0.0, xt[s.h][0:p, :, :], ALU.max, ALU.add)\
                        .then_inc(summed, 1)
                    dve.wait_ge(summed, after(s))
                    for j in range(JN):
                        last = nc.vector.bn_stats(stats[0:p, j, :], r[0:p, j, :])
                    last.then_inc(counted, 1)
                    dve.wait_ge(sd_set, after(s, 2))
                    dve.wait_ge(counted, after(s))
                    dve.sem_inc(pace_bn, 1)
                    for j in range(JN):
                        last = nc.vector.bn_aggr(mv[s.h][0:p, j, :], stats[0:p, j, :])
                    last.then_inc(mv_set, 1)
            timeline(dve, FULL, True, 3, body)
    ph.close()


def group_cols(table, s):
    return table[bass.ds(s.k, 1), :, 0:s.n].rearrange("g f n -> (g f) n")


def project_nodes(nc, c, table, xT_in, y_out):
    ph = Phase(nc, "proj")
    idx4 = ph.sb2("idx4", [P, JN], I32)
    ag, xb, o, oT, y = (ph.sb2("ag", [P, JN, CNT]), ph.sb2("xb", [P, GROUP]), ph.sb2("o", [P, JN, D]),
                        ph.sb2("oT", [P, GROUP]), ph.sb2("y", [P, GROUP]))
    den, inv = ph.sb("den", [P, JN, HEADS]), ph.sb("inv", [P, JN, HEADS])
    oT_ps, mul_ps = ph.ps2("oT_ps", [P, GROUP]), ph.ps2("mul_ps", [P, GROUP])
    x_in, gathered, stored = ph.sem2("x_in"), ph.sem2("gathered"), ph.sem2("stored")
    pace, idx_set, den_set, inv_set, o_set, turned, copied, mul, y_set = (
        ph.sem(n) for n in ("pace", "idx_set", "den_set", "inv_set", "o_set", "turned", "copied", "mul", "y_set"))
    with nc.Block() as block:
        @block.gpsimd
        def _(pool):
            gather_groups(nc, c, pool, table, ag, idx4, idx_set, o_set, gathered, pace)

        @block.sync
        def _(sp):
            start_dma(sp, x_in, stored)

            def body(at):
                if s := at(0):
                    sp.wait_ge(y_set, after(s, 2))
                    sp.dma_start(xb[s.h][:, 0:s.n], group_cols(xT_in, s)).then_inc(x_in[s.h], 16)
                if s := at(1):
                    sp.wait_ge(y_set, after(s))
                    sp.dma_start(group_cols(y_out, s), y[s.h][:, 0:s.n]).then_inc(stored[s.h], 16)
            timeline(sp, FULL, True, 2, body)
            for h in range(2):
                sp.wait_ge(stored[h], 16 + 16 * (GROUPS // 2))

        @block.vector
        def _(dve):
            start(dve, (idx_set, den_set, inv_set, o_set, y_set))

            def body(at):
                if s := at(0):
                    wait_indices_used(dve, gathered, s, JN)
                    nc.vector.tensor_copy(idx4[s.h][:, :], c.start_i[:, bass.ds(s.k * JN, JN)]).then_inc(idx_set, 1)
                if s := at(1):
                    p = s.p
                    dve.wait_ge(gathered[s.h], landed(s, JN))
                    nc.vector.tensor_scalar(den[0:p, :, :], ag[s.h][0:p, :, D:], 1e-30, None, ALU.max).then_inc(den_set, 1)
                    dve.wait_ge(den_set, after(s))
                    nc.vector.reciprocal(inv[0:p, :, :], den[0:p, :, :]).then_inc(inv_set, 1)
                    dve.wait_ge(inv_set, after(s))
                    dve.wait_ge(turned, after(s, 2))
                    for j in range(JN):
                        last = nc.vector.tensor_tensor(o[s.h][0:p, j, :].rearrange("p (h e) -> p h e", e=HD),
                                                       ag[s.h][0:p, j, 0:D].rearrange("p (h e) -> p h e", e=HD),
                                                       bc(inv[0:p, j, :], HD), ALU.mult)
                    last.then_inc(o_set, 1)
                if s := at(2):
                    dve.wait_ge(stored[s.h], vacated(s))
                    dve.wait_ge(x_in[s.h], arrived(s))
                    dve.wait_ge(mul, after(s))
                    nc.vector.scalar_tensor_tensor(y[s.h][:, 0:s.n], mul_ps[s.h][:, 0:s.n], c.col[:, 0:1],
                                                   xb[s.h][:, 0:s.n], ALU.add, ALU.add).then_inc(y_set, 1)
                    dve.wait_ge(y_set, after(s))
                    nc.vector.bn_stats(c.stats[:, bass.ds(s.k * 6, 6)], y[s.h][:, 0:s.n])
            timeline(dve, FULL, True, 3, body)

        @block.tensor
        def _(pe):
            start(pe, (turned, mul))

            def body(at):
                if s := at(0):
                    pe.wait_ge(o_set, after(s))
                    pe.wait_ge(copied, after(s, 2))
                    turn(nc, c, oT_ps[s.h], o[s.h], s).then_inc(turned, 1)
                if s := at(1):
                    pe.wait_ge(copied, after(s))
                    pe.wait_ge(y_set, after(s, 2))
                    nc.tensor.matmul(mul_ps[s.h][:, 0:s.n], c.wo[:, :], oT[s.h][:, 0:s.n], start=True, stop=True)\
                        .then_inc(mul, 1)
            timeline(pe, FULL, True, 2, body)

        @block.scalar
        def _(act):
            start(act, (copied,))

            def body(at):
                if s := at(0):
                    act.wait_ge(mul, after(s, 2))
                    act.wait_ge(turned, after(s))
                    nc.scalar.copy(oT[s.h][:, 0:s.n], oT_ps[s.h][:, 0:s.n]).then_inc(copied, 1)
            timeline(act, FULL, True, 1, body)
    ph.close()


def close_stats(nc, dve, c, mv, aff, gamma, beta, link, root):
    nc.vector.bn_aggr(mv[:, :], c.stats[:, :]).then_inc(link, 1)
    dve.wait_ge(link, 1)
    dve.wait_ge(root, 1)
    nc.vector.reciprocal(aff[:, 2:3], aff[:, 2:3]).then_inc(link, 1)
    dve.wait_ge(link, 2)
    nc.vector.tensor_tensor(aff[:, 0:1], aff[:, 2:3], gamma, ALU.mult).then_inc(link, 1)
    dve.wait_ge(link, 3)
    nc.vector.tensor_tensor(aff[:, 2:3], aff[:, 0:1], mv[:, 0:1], ALU.mult).then_inc(link, 1)
    dve.wait_ge(link, 4)
    nc.vector.tensor_tensor(aff[:, 1:2], beta, aff[:, 2:3], ALU.subtract).then_inc(link, 1)


def root_stats(nc, act, c, mv, aff, link, root):
    act.wait_ge(link, 1)
    nc.scalar.activation(aff[:, 2:3], mv[:, 1:2], ACT.Sqrt, bias=c.eps[:, 1:2]).then_inc(root, 1)
    act.wait_ge(link, 5)


def feed_forward(nc, c, y_in, y_out):
    U = 4
    ph = Phase(nc, "ffn")
    yb, hb, f, y2 = (ph.sb2("yb", [P, GROUP], n=U), ph.sb2("hb", [P, GROUP], n=U), ph.sb2("f", [P, 2, GROUP]),
                     ph.sb2("y2", [P, GROUP], n=U))
    mv, aff = ph.sb("mv", [P, 2]), ph.sb("aff", [P, 3])
    f_ps = [ph.ps2(f"f{a}_ps", [P, GROUP]) for a in range(2)]
    g_ps = ph.ps2("g_ps", [P, GROUP])
    y_in_s, stored = ph.sem2("y_in", U), ph.sem2("stored", U)
    link, root, h_set, f_mul, f0_set, f1_set, mul, y2_set, counted = (
        ph.sem(n) for n in ("link", "root", "h_set", "f_mul", "f0_set", "f1_set", "mul", "y2_set", "counted"))
    with nc.Block() as block:
        @block.sync
        def _(sp):
            start_dma(sp, y_in_s, stored)

            def body(at):
                if s := at(0):
                    sp.wait_ge(h_set, after(s, U))
                    sp.dma_start(yb[s.h][:, 0:s.n], group_cols(y_in, s)).then_inc(y_in_s[s.h], 16)
                if s := at(3):
                    sp.wait_ge(y2_set, after(s))
                    sp.dma_start(group_cols(y_out, s), y2[s.h][:, 0:s.n]).then_inc(stored[s.h], 16)
            timeline(sp, FULL, True, 4, body, U)
            for h in range(U):
                sp.wait_ge(stored[h], 16 + 16 * len(range(h, GROUPS, U)))

        @block.scalar
        def _(act):
            start(act, (h_set, f0_set), U)
            root_stats(nc, act, c, mv, aff, link, root)

            def body(at):
                if s := at(0):
                    act.wait_ge(y2_set, after(s, U))
                    act.wait_ge(y_in_s[s.h], arrived(s))
                    nc.scalar.activation(hb[s.h][:, 0:s.n], yb[s.h][:, 0:s.n], ACT.Identity, bias=aff[:, 1:2],
                                         scale=aff[:, 0:1]).then_inc(h_set, 1)
                if s := at(1):
                    act.wait_ge(mul, after(s, 2))
                    act.wait_ge(f_mul, after(s))
                    nc.scalar.activation(f[s.h % 2][:, 0, 0:s.n], f_ps[0][s.h % 2][:, 0:s.n], ACT.Relu, bias=c.b1[:, 0:1])\
                        .then_inc(f0_set, 1)
            timeline(act, FULL, True, 2, body, U)

        @block.tensor
        def _(pe):
            start(pe, (f_mul, mul), U)

            def body(at):
                if s := at(0):
                    pe.wait_ge(f0_set, after(s, 2))
                    pe.wait_ge(f1_set, after(s, 2))
                    pe.wait_ge(h_set, after(s))
                    for a in range(2):
                        last = nc.tensor.matmul(f_ps[a][s.h % 2][:, 0:s.n], c.w1[:, a * P:(a + 1) * P], hb[s.h][:, 0:s.n],
                                                start=True, stop=True)
                    last.then_inc(f_mul, 1)
                if s := at(1):
                    pe.wait_ge(y2_set, after(s, 2))
                    pe.wait_ge(f0_set, after(s))
                    pe.wait_ge(f1_set, after(s))
                    for a in range(2):
                        last = nc.tensor.matmul(g_ps[s.h % 2][:, 0:s.n], c.w2[:, a, :], f[s.h % 2][:, a, 0:s.n],
                                                start=a == 0, stop=a == 1)
                    last.then_inc(mul, 1)
            timeline(pe, FULL, True, 2, body, U)

        @block.vector
        def _(dve):
            start(dve, (f1_set, y2_set, counted), U)
            close_stats(nc, dve, c, mv, aff, c.col[:, 2:3], c.col[:, 3:4], link, root)

            def body(at):
                if s := at(0):
                    dve.wait_ge(mul, after(s, 2))
                    dve.wait_ge(f_mul, after(s))
                    nc.vector.tensor_scalar(f[s.h % 2][:, 1, 0:s.n], f_ps[1][s.h % 2][:, 0:s.n], c.b1[:, 1:2], 0.0,
                                            ALU.add, ALU.max).then_inc(f1_set, 1)
                if s := at(1):
                    dve.wait_ge(stored[s.h], vacated(s))
                    dve.wait_ge(mul, after(s))
                    nc.vector.scalar_tensor_tensor(y2[s.h][:, 0:s.n], g_ps[s.h % 2][:, 0:s.n], c.col[:, 1:2],
                                                   hb[s.h][:, 0:s.n], ALU.add, ALU.add).then_inc(y2_set, 1)
                    dve.wait_ge(y2_set, after(s))
                    nc.vector.bn_stats(c.stats[:, bass.ds(s.k * 6, 6)], y2[s.h][:, 0:s.n]).then_inc(counted, 1)
            timeline(dve, FULL, True, 2, body, U)
    ph.close()


def final_norm(nc, c, xT_in, y_in, out):
    U = 4
    ph = Phase(nc, "fin")
    yb, xb, ub, vb = (ph.sb2(n, [P, GROUP], n=U) for n in ("yb", "xb", "ub", "vb"))
    rows = ph.sb2("rows", [P, JN, D], n=U)
    stats, mv2, sd = ph.sb("stats", [P, JN, 6]), ph.sb2("mv2", [P, JN, 2]), ph.sb2("sd", [P, JN])
    rstd, off = ph.sb2("rstd", [P, JN]), ph.sb2("off", [P, JN])
    mv, aff = ph.sb("mv", [P, 2]), ph.sb("aff", [P, 3])
    v_ps = ph.ps2("v_ps", [P, JN, D], 4)
    pace_bn = ph.sem("pace_bn")
    y_in_s, x_in, stored = ph.sem2("y_in", U), ph.sem2("x_in", U), ph.sem2("stored", U)
    link, root, u_set, v_set, turned, counted, mv_set, sd_set, rstd_set, off_set, rows_set = (
        ph.sem(n) for n in ("link", "root", "u_set", "v_set", "turned", "counted", "mv_set", "sd_set", "rstd_set", "off_set", "rows_set"))
    with nc.Block() as block:
        @block.sync
        def _(sp):
            start_dma(sp, y_in_s, x_in, stored)

            def body(at):
                if s := at(0):
                    sp.wait_ge(u_set, after(s, U))
                    sp.dma_start(yb[s.h][:, 0:s.n], group_cols(y_in, s)).then_inc(y_in_s[s.h], 16)
                    sp.wait_ge(v_set, after(s, U))
                    sp.dma_start(xb[s.h][:, 0:s.n], group_cols(xT_in, s)).then_inc(x_in[s.h], 16)
                if s := at(3):
                    sp.wait_ge(rows_set, after(s))
                    sp.dma_start(group_rows(out, s), rows[s.h][0:s.p, :, :]).then_inc(stored[s.h], 16)
            timeline(sp, FULL, True, 4, body, U)
            for h in range(U):
                sp.wait_ge(stored[h], 16 + 16 * len(range(h, GROUPS, U)))

        @block.scalar
        def _(act):
            start(act, (u_set, sd_set, rows_set), U)
            root_stats(nc, act, c, mv, aff, link, root)

            def body(at):
                if s := at(0):
                    act.wait_ge(v_set, after(s, U))
                    act.wait_ge(y_in_s[s.h], arrived(s))
                    nc.scalar.activation(ub[s.h][:, 0:s.n], yb[s.h][:, 0:s.n], ACT.Identity, bias=aff[:, 1:2],
                                         scale=aff[:, 0:1]).then_inc(u_set, 1)
                if s := at(1):
                    act.wait_ge(rstd_set, after(s, 2))
                    act.wait_ge(mv_set, after(s))
                    nc.scalar.activation(sd[s.h % 2][0:s.p, :], mv2[s.h % 2][0:s.p, :, 1], ACT.Sqrt, bias=c.eps[0:s.p, 1:2])\
                        .then_inc(sd_set, 1)
                if s := at(3):
                    act.wait_ge(stored[s.h], vacated(s))
                    act.wait_ge(off_set, after(s))
                    for j in range(JN):
                        last = nc.scalar.activation(rows[s.h][0:s.p, j, :], v_ps[s.h][0:s.p, j, :], ACT.Identity,
                                                    bias=off[s.h % 2][0:s.p, j:j + 1], scale=rstd[s.h % 2][0:s.p, j:j + 1])
                    last.then_inc(rows_set, 1)
            timeline(act, FULL, True, 4, body, U)

        @block.tensor
        def _(pe):
            start(pe, (turned,), U)

            def body(at):
                if s := at(0):
                    pe.wait_ge(rows_set, after(s, U))
                    pe.wait_ge(v_set, after(s))
                    for j in range(JN):
                        last = nc.tensor.transpose(v_ps[s.h][0:s.p, j, :], vb[s.h][:, j * s.p:(j + 1) * s.p], c.ident[:, :])
                    last.then_inc(turned, 1)
            timeline(pe, FULL, True, 1, body, U)

        @block.vector
        def _(dve):
            start(dve, (v_set, counted, mv_set, rstd_set, off_set), U)
            close_stats(nc, dve, c, mv, aff, c.col[:, 4:5], c.col[:, 5:6], link, root)

            def body(at):
                if s := at(0):
                    dve.wait_ge(turned, after(s, U))
                    dve.wait_ge(x_in[s.h], arrived(s))
                    dve.wait_ge(u_set, after(s))
                    nc.vector.tensor_tensor(vb[s.h][:, 0:s.n], ub[s.h][:, 0:s.n], xb[s.h][:, 0:s.n], ALU.add)\
                        .then_inc(v_set, 1)
                if s := at(2):
                    p, h = s.p, s.h % 2
                    dve.wait_ge(rows_set, after(s, 2))
                    dve.wait_ge(sd_set, after(s))
                    nc.vector.reciprocal(rstd[h][0:p, :], sd[h][0:p, :]).then_inc(rstd_set, 1)
                    dve.wait_ge(rstd_set, after(s))
                    nc.vector.scalar_tensor_tensor(off[h][0:p, :], mv2[h][0:p, :, 0], -1.0, rstd[h][0:p, :], ALU.mult,
                                                   ALU.mult).then_inc(off_set, 1)
                if s := at(1):
                    p, h = s.p, s.h % 2
                    dve.wait_ge(turned, after(s))
                    for j in range(JN):
                        last = nc.vector.bn_stats(stats[0:p, j, :], v_ps[s.h][0:p, j, :])
                    last.then_inc(counted, 1)
                    dve.wait_ge(sd_set, after(s, 2))
                    dve.wait_ge(counted, after(s))
                    dve.sem_inc(pace_bn, 1)
                    for j in range(JN):
                        last = nc.vector.bn_aggr(mv2[h][0:p, j, :], stats[0:p, j, :])
                    last.then_inc(mv_set, 1)
            timeline(dve, FULL, True, 3, body, U)
    ph.close()


class Constants:
    pass


def build(nc, w, out):
    with ExitStack() as ctx:
        c = Constants()

        def keep(name, shape, dt=F32):
            return ctx.enter_context(nc.sbuf_tensor(name, shape, dt))

        c.ident, c.ones, c.lower = keep("ident", [P, P]), keep("ones", [P, P]), keep("lower", [P, P])
        c.iota_i, c.iota16 = keep("iota_i", [P, TILES], I32), keep("iota16", [P, TILES], F16)
        c.iota, c.iota1 = keep("iota", [P, TYPES]), keep("iota1", [P, TYPES])
        c.rows, c.after = keep("rows", [P, 3, 4, P], I32), keep("after", [P, 4, P], I32)
        c.src_i, c.dst_i, c.start_i = (keep(n, [P, TILES], I32) for n in ("src_i", "dst_i", "start_i"))
        c.dst_f, c.typ_f, c.place_p, c.place_f, c.count, c.norm = (
            keep(n, [P, TILES]) for n in ("dst_f", "typ_f", "place_p", "place_f", "count", "norm"))
        c.next_f = keep("next_f", [1, TILES])
        c.w_emb, c.b_emb = keep("w_emb", [P, D]), keep("b_emb", [P, D])
        c.bases, c.loop = keep("bases", [P, LAYERS, BASES, D]), keep("loop", [P, LAYERS, D])
        c.coe, c.bn = keep("coe", [P, LAYERS, TYPES * BASES]), keep("bn", [P, LAYERS, 4, D])
        c.qkv, c.wo, c.w1, c.w2 = keep("qkv", [P, 3 * D]), keep("wo", [P, D]), keep("w1", [P, 2 * D]), keep("w2", [P, 2, D])
        c.b1, c.col, c.stats = keep("b1", [P, 2]), keep("col", [P, 6]), keep("stats", [P, GROUPS * 6])
        c.zero, c.eps = keep("zero", [1, CNT]), keep("eps", [P, 2])
        h0, h1, q = (nc.dram_tensor(n, (NODES, D), F32, kind="Internal").ap() for n in ("h0", "h1", "q"))
        kv = nc.dram_tensor("kv", (NODES, 2 * D), F32, kind="Internal").ap()
        sums0, att = (nc.dram_tensor(n, (EPAD + 1, CNT), F32, kind="Internal").ap() for n in ("sums0", "att"))
        sums1 = nc.dram_tensor("sums1", (EPAD + 1, D), F32, kind="Internal").ap()
        x1T, y1T, y2T = (nc.dram_tensor(n, (GROUPS, P, GROUP), F32, kind="Internal").ap() for n in ("x1T", "y1T", "y2T"))
        c.zero_rows = [(t, n) for t, n in ((sums0, CNT), (att, CNT), (sums1, D))]
        load_constants(nc, c, w)
        arrange_edges(nc, c)
        embed_nodes(nc, c, w["x"], h0)
        index_nodes(nc, c)
        conv_edges(nc, c, 0, h0, sums0, CNT)
        update_nodes(nc, c, h0, sums0, h1)
        conv_edges(nc, c, 1, h1, sums1, D)
        finish_conv(nc, c, w["x"], h1, sums1, x1T, q, kv)
        attend_edges(nc, c, q, kv, att)
        project_nodes(nc, c, att, x1T, y1T)
        feed_forward(nc, c, y1T, y2T)
        final_norm(nc, c, x1T, y2T, out)


NAMES = ["x", "src", "dst", "edge_type_8", "L0_gnn_W_emb", "L0_gnn_b_emb", "L0_gnn_bases", "L0_gnn_w_coe",
         "L0_gnn_self_loop", "L0_gnn_bn_gamma", "L0_gnn_bn_beta", "L0_gnn_bn_mean", "L0_gnn_bn_var", "L1_gnn_Wq",
         "L1_gnn_Wk", "L1_gnn_Wv", "L1_gnn_Wo", "L1_gnn_bo", "L1_gnn_W1", "L1_gnn_b1", "L1_gnn_W2", "L1_gnn_b2",
         "L1_gnn_g1", "L1_gnn_be1", "L1_gnn_g2", "L1_gnn_be2"]


def kernel(**inputs):
    import concourse.bacc as bacc
    from concourse.bass_utils import run_bass_kernel_spmd

    nc = bacc.Bacc("TRN2", target_bir_lowering=False, num_devices=1)
    arrays, w = {}, {}
    for name in NAMES:
        a = np.ascontiguousarray(inputs[name])
        arrays["in_" + name] = a
        w[name] = nc.dram_tensor("in_" + name, a.shape, mybir.dt.from_np(a.dtype), kind="ExternalInput").ap()
    out = nc.dram_tensor("out", (NODES, D), F32, kind="ExternalOutput").ap()
    build(nc, w, out)
    return run_bass_kernel_spmd(nc, [arrays], core_ids=[0]).results[0]["out"]
```

```python
import numpy as np
import concourse.bass as bass
from concourse import mybir
from concourse.alu_op_type import AluOpType as ALU
from contextlib import ExitStack

F32 = mybir.dt.float32
F16 = mybir.dt.float16
I32 = mybir.dt.int32
ACT = mybir.ActivationFunctionType
X = mybir.AxisListType.X

NODES, EDGES, D, P = 50000, 50000, 128, 128
TYPES, BASES, LAYERS = 8, 4, 2
HEADS, HD = 8, 16
BN_EPS, EPS = 0.001, 1e-5
JN = 4
GROUP = P * JN
FULL = NODES // GROUP
TAIL_P = (NODES - FULL * GROUP) // JN
assert FULL * GROUP + TAIL_P * JN == NODES
GROUPS = FULL + 1
UT = 4
TILES = 392
STEPS = TILES // UT
EPAD = TILES * P
ZROW = EPAD
PAD_DST = 60000
CNT = D + TYPES


class Step:

    def __init__(self, unroll, i, h, parts=P):
        self.u, self.h, self.i, self.k = unroll, h, i, i * unroll + h
        self.p, self.n = parts, parts * JN


U = 4


def timeline(eng, full, tail, depth, body, unroll=U):
    total = full + (1 if tail else 0)
    lo = -(-(depth - 1) // unroll) * unroll
    rounds = (full - lo) // unroll

    def peeled(t):
        def at(s):
            k = t - s
            if 0 <= k < total:
                return Step(unroll, k // unroll, k % unroll, P if k < full else TAIL_P)
        body(at)

    for t in range(lo):
        peeled(t)
    with eng.Fori(lo // unroll, lo // unroll + rounds) as i:
        for h in range(unroll):
            body(lambda s: Step(unroll, i + (h - s) // unroll, (h - s) % unroll))
    for t in range(lo + unroll * rounds, total + depth - 1):
        peeled(t)


class Phase:

    def __init__(self, nc, name):
        self.nc, self.name, self.ctx, self.sems = nc, name, ExitStack(), []

    def sem(self, name):
        s = self.nc.alloc_semaphore(f"{self.name}_{name}")
        self.sems.append(s)
        return s

    def sem2(self, name, n=2):
        return [self.sem(f"{name}{h}") for h in range(n)]

    def sb(self, name, shape, dt=F32):
        return self.ctx.enter_context(self.nc.sbuf_tensor(f"{self.name}_{name}", shape, dt))

    def sb2(self, name, shape, dt=F32, n=2):
        return [self.sb(f"{name}{h}", shape, dt) for h in range(n)]

    def ps2(self, name, shape, n=2):
        return [self.ps(f"{name}{h}", shape) for h in range(n)]

    def ps(self, name, shape, dt=F32):
        return self.ctx.enter_context(self.nc.psum_tensor(f"{self.name}_{name}", shape, dt))

    def close(self):
        self.nc.clear_and_free_semaphores(self.sems)
        self.nc.all_engine_barrier()
        self.ctx.close()


def start(eng, sems, steps=U, counts=1):
    for q in sems:
        eng.sem_inc(q, steps * counts)


def start_dma(eng, *sets):
    for sems in sets:
        for q in sems:
            eng.sem_inc(q, 16)


def after(s, back=0):
    return s.k + (1 - back + s.u)


def after_tile(s, u, back=0):
    return s.k * UT + (UT - u + (s.u - back) * UT)


def arrived(s, transfers=1):
    return (s.i + 1) * (16 * transfers) + 16


def vacated(s, transfers=1):
    return s.i * (16 * transfers) + 16


def wait_all(eng, sems, steps, transfers=1):
    for h, q in enumerate(sems):
        eng.wait_ge(q, 16 + 16 * transfers * len(range(h, steps, len(sems))))


def landed(s, transfers):
    return (s.i + 1) * (16 * transfers)


def wait_indices_used(eng, gathered, s, transfers):
    if not isinstance(s.i, int) or s.i > 0:
        eng.wait_ge(gathered[s.h], s.i * (16 * transfers))


def slot(buffers, s):
    return buffers[s.h % len(buffers)]


def bc(ap, n):
    ap = ap.unsqueeze(len(ap.shape))
    return ap.to_broadcast(list(ap.shape[:-1]) + [n])


def mid(ap, n):
    ap = ap.unsqueeze(1)
    return ap.to_broadcast([ap.shape[0], n] + list(ap.shape[2:]))


def group_rows(table, s):
    start = s.k * GROUP
    return table[bass.ds(start, s.n), :].rearrange("(p j) d -> p j d", j=JN)


def load_constants(nc, c, w):
    ph = Phase(nc, "const")
    loaded, made, zeroed = ph.sem("loaded"), ph.sem("made"), ph.sem("zeroed")
    with nc.Block() as block:
        @block.sync
        def _(sp):
            def load(out, in_):
                sp.dma_start(out, in_).then_inc(loaded, 16)
                return 1
            sp.wait_ge(zeroed, 1)
            n = 0
            for a, name in enumerate(("src", "dst", "edge_type_8")):
                v = w[name]
                n += load(c.rows[:, a, 0:3, :], v[0:3 * P * P].rearrange("(c p f) -> p c f", p=P, f=P))
                n += load(c.rows[0:6, a, 3, :], v[3 * P * P:3 * P * P + 6 * P].rearrange("(p f) -> p f", f=P))
                n += load(c.rows[6:7, a, 3, 0:80], v[EDGES - 80:EDGES].rearrange("(p f) -> p f", p=1))
            v = w["dst"]
            n += load(c.after[:, 0:3, :], v[1:3 * P * P + 1].rearrange("(c p f) -> p c f", p=P, f=P))
            n += load(c.after[0:6, 3, :], v[3 * P * P + 1:3 * P * P + 6 * P + 1].rearrange("(p f) -> p f", f=P))
            n += load(c.after[6:7, 3, 0:79], v[EDGES - 79:EDGES].rearrange("(p f) -> p f", p=1))
            n += load(c.w_emb[:, :], w["L0_gnn_W_emb"])
            n += load(c.b_emb[:, :], w["L0_gnn_b_emb"].partition_broadcast(P))
            for l in range(LAYERS):
                n += load(c.bases[:, l, :, :], w["L0_gnn_bases"][l].rearrange("b d f -> d b f"))
                n += load(c.loop[:, l, :], w["L0_gnn_self_loop"][l])
                n += load(c.coe[:, l, :], w["L0_gnn_w_coe"][l].rearrange("r b -> (r b)").partition_broadcast(P))
                for a, name in enumerate(("gamma", "beta", "mean", "var")):
                    n += load(c.bn[:, l, a, :], w["L0_gnn_bn_" + name][l].partition_broadcast(P))
            for a, name in enumerate(("Wq", "Wk", "Wv")):
                n += load(c.qkv[:, a * D:(a + 1) * D], w["L1_gnn_" + name])
            n += load(c.wo[:, :], w["L1_gnn_Wo"])
            n += load(c.w1[:, :], w["L1_gnn_W1"])
            n += load(c.w2[:, :, :], w["L1_gnn_W2"].rearrange("(a p) f -> p a f", p=P))
            for a in range(2):
                n += load(c.b1[:, a:a + 1], w["L1_gnn_b1"][a * P:(a + 1) * P].rearrange("(p a) -> p a", a=1))
            for a, name in enumerate(("bo", "b2", "g1", "be1", "g2", "be2")):
                n += load(c.col[:, a:a + 1], w["L1_gnn_" + name].rearrange("(p a) -> p a", a=1))
            for table, width in c.zero_rows:
                n += load(table[ZROW:ZROW + 1, :], c.zero[0:1, 0:width])
            sp.wait_ge(loaded, 16 * n)

        @block.gpsimd
        def _(pool):
            pool.memset(c.ident[:, :], 0.0).then_inc(made, 1)
            pool.memset(c.ones[:, :], 1.0).then_inc(made, 1)
            pool.memset(c.lower[:, :], 0.0).then_inc(made, 1)
            pool.wait_ge(made, 3)
            pool.affine_select(out=c.ident[:, :], in_=c.ident[:, :], compare_op=ALU.not_equal, fill=1.0,
                               base=0, pattern=[[-1, P]], channel_multiplier=1).then_inc(made, 1)
            pool.affine_select(out=c.lower[:, :], in_=c.lower[:, :], compare_op=ALU.is_ge, fill=1.0,
                               base=0, pattern=[[-1, P]], channel_multiplier=1).then_inc(made, 1)
            pool.iota(c.iota_i[:, :], pattern=[[1, TILES]], base=0, channel_multiplier=0).then_inc(made, 1)

        @block.vector
        def _(dve):
            nc.vector.memset(c.zero[:, :], 0.0)
            nc.vector.memset(c.norm[:, :], 1.0)
            nc.vector.memset(c.eps[:, 0:1], BN_EPS)
            nc.vector.memset(c.eps[:, 1:2], EPS)
            nc.vector.memset(c.rows[:, 0, 3, :], 0)
            nc.vector.memset(c.rows[:, 2, 3, :], 0)
            nc.vector.memset(c.rows[:, 1, 3, :], PAD_DST)
            nc.vector.memset(c.after[:, 3, :], PAD_DST).then_inc(zeroed, 1)
            dve.wait_ge(made, 6)
            nc.vector.tensor_copy(c.iota16[:, :], c.iota_i[:, :])
            nc.vector.tensor_copy(c.iota[:, :], c.iota_i[:, 0:TYPES])
            nc.vector.tensor_copy(c.iota1[:, :], c.iota_i[:, 1:TYPES + 1])
    ph.close()


def arrange_edges(nc, c):
    ph = Phase(nc, "arr")
    rf = ph.sb("rf", [P, 3, 4, P])
    pt = [ph.ps(f"pt{a}", [P, 4 * P]) for a in range(3)]
    floats, turned, cols, ints = ph.sem("floats"), ph.sem("turned"), ph.sem("cols"), ph.sem("ints")
    lows, roots = ph.sem("lows"), ph.sem("roots")
    b1, b2, bn1, bn2 = ph.sem("w_scale"), ph.sem("w_shift"), ph.sem("w_var"), ph.sem("w_prod")
    lo_i = ph.sb("lo_i", [P, TILES], I32)
    hi_i = ph.sb("hi_i", [P, TILES], I32)
    j_i = ph.sb("j_i", [P, TILES], I32)
    d_i = ph.sb("d_i", [P, TILES], I32)
    hi_f = ph.sb("hi_f", [P, TILES])
    with nc.Block() as block:
        @block.vector
        def _(dve):
            nc.vector.tensor_copy(rf[:, :, :, :], c.rows[:, :, :, :]).then_inc(floats, 1)
            dve.wait_ge(turned, 3)
            nc.vector.tensor_copy(c.src_i[:, :], pt[0][:, 0:TILES])
            nc.vector.tensor_copy(c.dst_f[:, :], pt[1][:, 0:TILES]).then_inc(cols, 1)
            nc.vector.tensor_copy(d_i[:, :], pt[1][:, 0:TILES]).then_inc(ints, 1)
            nc.vector.tensor_copy(c.typ_f[:, :], pt[2][:, 0:TILES])
            nc.vector.memset(c.next_f[:, TILES - 1:TILES], -1.0)
            dve.wait_ge(cols, 1)
            nc.vector.tensor_copy(c.next_f[:, 0:TILES - 1], c.dst_f[0:1, 1:TILES])
            nc.vector.tensor_scalar(c.dst_i[:, :], c.dst_f[:, :], float(NODES - 1), None, ALU.min)
            dve.wait_ge(ints, 1)
            nc.vector.tensor_scalar(lo_i[:, :], d_i[:, :], 2, P - 1, ALU.logical_shift_right, ALU.bitwise_and).then_inc(lows, 1)
            nc.vector.tensor_scalar(hi_i[:, :], d_i[:, :], 9, 2, ALU.logical_shift_right, ALU.logical_shift_left).then_inc(lows, 1)
            nc.vector.tensor_scalar(j_i[:, :], d_i[:, :], JN - 1, None, ALU.bitwise_and).then_inc(lows, 1)
            dve.wait_ge(lows, 3)
            nc.vector.tensor_copy(c.place_p[:, :], lo_i[:, :])
            nc.vector.tensor_copy(hi_f[:, :], hi_i[:, :]).then_inc(lows, 1)
            dve.wait_ge(lows, 4)
            nc.vector.tensor_tensor(c.place_f[:, :], hi_f[:, :], j_i[:, :], ALU.add)
            dve.wait_ge(roots, 1)
            for l in range(LAYERS):
                gamma, beta, mean, var = (c.bn[:, l, a, :] for a in range(4))
                nc.vector.reciprocal(var, var).then_inc(bn1, 1)
                dve.wait_ge(bn1, l + 1)
                nc.vector.tensor_tensor(gamma, gamma, var, ALU.mult).then_inc(b1, 1)
                dve.wait_ge(b1, l + 1)
                nc.vector.tensor_tensor(mean, mean, gamma, ALU.mult).then_inc(bn2, 1)
                dve.wait_ge(bn2, l + 1)
                nc.vector.tensor_tensor(beta, beta, mean, ALU.subtract).then_inc(b2, 1)
                nc.vector.tensor_tensor(c.loop[:, l, :], c.loop[:, l, :], gamma, ALU.mult)
                nc.vector.tensor_tensor(c.bases[:, l, :, :], c.bases[:, l, :, :], mid(gamma, BASES), ALU.mult)

        @block.scalar
        def _(act):
            var = c.bn[:, :, 3, :]
            nc.scalar.activation(var, var, ACT.Sqrt, bias=c.eps[:, 0:1]).then_inc(roots, 1)

        @block.tensor
        def _(pe):
            pe.wait_ge(floats, 1)
            for a in range(3):
                for q in range(4):
                    last = nc.tensor.transpose(pt[a][:, q * P:(q + 1) * P], rf[:, a, q, :], c.ident[:, :])
                last.then_inc(turned, 1)
    ph.close()


def embed_nodes(nc, c, x, h0):
    ph = Phase(nc, "emb")
    xt, xT, hs = (ph.sb2(n, [P, GROUP], n=U) for n in ("xt", "xT", "hs"))
    xt, hs = ([b[:, :].rearrange("p (j d) -> p j d", j=JN) for b in x4] for x4 in (xt, hs))
    hot_p, hot_f = ph.sb2("hot_p", [P, UT, P], F16, U), ph.sb2("hot_f", [P, UT, TILES], F16, U)
    zero16 = ph.sb("zero16", [P, P], F16)
    xT_ps = [ph.ps(f"xT_ps{h}", [P, GROUP]) for h in range(2)]
    h_ps = [ph.ps(f"h_ps{h}", [P, JN, D]) for h in range(2)]
    hist = ph.ps("hist", [P, TILES])
    x_in, h_out = ph.sem2("x_in", U), ph.sem2("h_out", U)
    turned, copied, mul, biased = ph.sem("turned"), ph.sem("copied"), ph.sem("mul"), ph.sem("biased")
    hot, binned, zeroed, counted = ph.sem("hot"), ph.sem("binned"), ph.sem("zeroed"), ph.sem("counted")
    with nc.Block() as block:
        @block.sync
        def _(sp):
            start_dma(sp, x_in, h_out)

            def body(at):
                if s := at(0):
                    sp.wait_ge(turned, after(s, U))
                    sp.dma_start(xt[s.h][0:s.p, 0:JN, :], group_rows(x, s)).then_inc(x_in[s.h], 16)
                if s := at(3):
                    sp.wait_ge(biased, after(s))
                    sp.dma_start(group_rows(h0, s), hs[s.h][0:s.p, 0:JN, :]).then_inc(h_out[s.h], 16)
            timeline(sp, FULL, True, 4, body)
            wait_all(sp, h_out, GROUPS)

        @block.tensor
        def _(pe):
            start(pe, (turned, mul, binned))
            pe.wait_ge(zeroed, 1)
            nc.tensor.matmul(hist[:, :], zero16[:, :], c.iota16[:, :], start=True, stop=False)

            def body(at):
                if s := at(0):
                    pe.wait_ge(x_in[s.h], arrived(s))
                    pe.wait_ge(copied, after(s, 2))
                    for j in range(JN):
                        last = nc.tensor.transpose(xT_ps[s.h % 2][:, j * s.p:(j + 1) * s.p], xt[s.h][0:s.p, j, :],
                                                   c.ident[0:s.p, 0:s.p])
                    last.then_inc(turned, 1)
                if s := at(1):
                    pe.wait_ge(copied, after(s))
                    pe.wait_ge(biased, after(s, 2))
                    for j in range(JN):
                        last = nc.tensor.matmul(h_ps[s.h % 2][0:s.p, j, :], xT[s.h][:, j * s.p:(j + 1) * s.p],
                                                c.w_emb[:, :], start=True, stop=True)
                    last.then_inc(mul, 1)
                    pe.wait_ge(hot, after(s))
                    for u in range(UT):
                        last = nc.tensor.matmul(hist[:, :], hot_p[s.h][:, u, :], hot_f[s.h][:, u, :],
                                                start=False, stop=False)
                    last.then_inc(binned, 1)
            timeline(pe, FULL, True, 2, body)
            nc.tensor.matmul(hist[:, :], zero16[:, :], c.iota16[:, :], start=False, stop=True).then_inc(counted, 1)

        @block.scalar
        def _(act):
            start(act, (copied,))

            def body(at):
                if s := at(0):
                    act.wait_ge(turned, after(s))
                    act.wait_ge(mul, after(s, 2))
                    nc.scalar.copy(xT[s.h][:, 0:s.n], xT_ps[s.h % 2][:, 0:s.n]).then_inc(copied, 1)
            timeline(act, FULL, True, 1, body)

        @block.vector
        def _(dve):
            start(dve, (biased, hot))
            nc.vector.memset(zero16[:, :], 0.0).then_inc(zeroed, 1)

            def body(at):
                if s := at(0):
                    dve.wait_ge(binned, after(s, U))
                    for u in range(UT):
                        t = s.k * UT + u
                        nc.vector.tensor_scalar(hot_p[s.h][:, u, :], c.iota16[:, 0:P],
                                                c.place_p[:, bass.ds(t, 1)], None, ALU.is_equal)
                        last = nc.vector.tensor_scalar(hot_f[s.h][:, u, :], c.iota16[:, :],
                                                       c.place_f[:, bass.ds(t, 1)], None, ALU.is_equal)
                    last.then_inc(hot, 1)
                if s := at(2):
                    dve.wait_ge(mul, after(s))
                    dve.wait_ge(h_out[s.h], vacated(s))
                    nc.vector.tensor_tensor(hs[s.h][0:s.p, 0:JN, :], h_ps[s.h % 2][0:s.p, 0:JN, :],
                                            mid(c.b_emb[0:s.p, :], JN), ALU.add).then_inc(biased, 1)
            timeline(dve, FULL, True, 3, body)
            dve.wait_ge(counted, 1)
            nc.vector.tensor_copy(c.count[:, :], hist[:, :])
    ph.close()


def index_nodes(nc, c):
    ph = Phase(nc, "idx")
    rows = ph.sb("rows", [P, GROUPS])
    totals = ph.sb("totals", [GROUPS, P])
    base = ph.sb("base", [P, GROUPS])
    first, some, off = (ph.sb(n, [P, GROUPS, JN]) for n in ("first", "some", "off"))
    ps_t, ps_b, ps_g = ph.ps("ps_t", [GROUPS, P]), ph.ps("ps_b", [P, GROUPS]), ph.ps("ps_g", [P, GROUPS])
    summed, products, link = ph.sem("summed"), ph.sem("products"), ph.sem("link")
    count = c.count[:, :].rearrange("p (g j) -> p g j", j=JN)
    with nc.Block() as block:
        @block.tensor
        def _(pe):
            pe.wait_ge(summed, 1)
            nc.tensor.matmul(ps_t[:, :], rows[:, :], c.ones[:, :], start=True, stop=True).then_inc(products, 1)
            nc.tensor.matmul(ps_b[:, :], c.lower[:, :], rows[:, :], start=True, stop=True).then_inc(products, 1)
            pe.wait_ge(summed, 2)
            nc.tensor.matmul(ps_g[:, :], totals[:, :], c.lower[0:GROUPS, 0:GROUPS], start=True, stop=True)\
              .then_inc(products, 1)

        @block.vector
        def _(dve):
            links = [0]

            def chain(op):
                links[0] += 1
                op.then_inc(link, 1)
                dve.wait_ge(link, links[0])
            nc.vector.tensor_reduce(rows[:, :], count, X, ALU.add).then_inc(summed, 1)
            dve.wait_ge(products, 1)
            nc.vector.tensor_copy(totals[:, :], ps_t[:, :]).then_inc(summed, 1)
            dve.wait_ge(products, 2)
            chain(nc.vector.tensor_copy(base[:, :], ps_b[:, :]))
            dve.wait_ge(products, 3)
            chain(nc.vector.tensor_tensor(first[:, :, 0], base[:, :], ps_g[:, :], ALU.add))
            for j in range(1, JN):
                chain(nc.vector.tensor_tensor(first[:, :, j], first[:, :, j - 1], count[:, :, j - 1], ALU.add))
            chain(nc.vector.tensor_scalar(some[:, :, :], count, 0.0, None, ALU.is_gt))
            chain(nc.vector.tensor_scalar(off[:, :, :], first[:, :, :], -float(ZROW), None, ALU.add))
            chain(nc.vector.tensor_tensor(off[:, :, :], off[:, :, :], some[:, :, :], ALU.mult))
            nc.vector.tensor_scalar(c.start_i[:, :].rearrange("p (g j) -> p g j", j=JN), off[:, :, :], float(ZROW),
                                    None, ALU.add)
    ph.close()


def tile_columns(s):
    return (STEPS - 1 - s.k) * UT if isinstance(s.k, int) else (STEPS - 1) * UT - s.k * UT


def tile_rows(table, s):
    return table[bass.ds(tile_columns(s) * P, UT * P), :].rearrange("(u p) d -> p u d", p=P)


UP = tuple(range(UT - 1, -1, -1))


def conv_edges(nc, c, layer, nodes, table, width):
    ph = Phase(nc, f"conv{layer}")
    src4, dst4, next4 = ph.sb2("src4", [P, UT], I32, U), ph.sb2("dst4", [P, UT], n=U), ph.sb2("next4", [1, UT], n=U)
    hot, coe = ph.sb2("hot", [P, UT, TYPES], n=U), ph.sb2("coe", [P, UT, BASES], n=U)
    prod = ph.sb("prod", [P, UT, BASES, TYPES])
    xg, xT = ph.sb2("xg", [P, UT, D], n=U), ph.sb2("xT", [P, UT, P])
    same, join = ph.sb2("same", [P, UT, P], n=U), ph.sb2("join", [1, UT, P], n=U)
    val, out = ph.sb2("val", [P, UT, width]), ph.sb2("out", [P, UT, width], n=U)
    part = ph.sb("part", [P, UT, BASES - 1, D])
    dst_ps, xT_ps = ph.ps("dst_ps", [P, UT, P]), ph.ps("xT_ps", [P, UT, P])
    mul_ps = [ph.ps(f"mul_ps{u}", [P, BASES, D]) for u in range(UT)]
    sum_ps = ph.ps("sum_ps", [P, UT, 256])
    gathered, stored, pace, pace_out = ph.sem2("gathered", U), ph.sem2("stored", U), ph.sem("pace"), ph.sem("pace_out")
    src_set, dst_set, hot_set, prod_set, coe_set = (
        ph.sem(n) for n in ("src_set", "dst_set", "hot_set", "prod_set", "coe_set"))
    dst_turned, x_turned, xT_set, same_set = (ph.sem(n) for n in ("dst_turned", "x_turned", "xT_set", "same_set"))
    mul, scaled, added, val_set, summed, out_set = (
        ph.sem(n) for n in ("mul", "scaled", "added", "val_set", "summed", "out_set"))
    with nc.Block() as block:
        @block.gpsimd
        def _(pool):
            def body(at):
                if s := at(0):
                    pool.wait_ge(x_turned, after(s, U))
                    pool.wait_ge(src_set, after(s))
                    pool.sem_inc(pace, 1)
                    for u in UP:
                        pool.indirect_dma_start(out=xg[s.h][:, u, :], out_offset=None, in_=nodes,
                                                in_offset=bass.IndirectOffsetOnAxis(ap=src4[s.h][:, u:u + 1], axis=0))\
                            .then_inc(gathered[s.h], 16)
            timeline(pool, STEPS, False, 1, body)

        @block.vector
        def _(dve):
            start(dve, (src_set, dst_set, hot_set, prod_set, coe_set, same_set))
            start(dve, (val_set,), counts=UT)

            def combine(s, pair, n):
                for b in range(1, BASES):
                    for u in pair:
                        if b == 1:
                            dve.wait_ge(scaled, after_tile(s, u))
                        else:
                            n += 1
                            dve.wait_ge(added, s.k * (2 * UT) + n)
                        into = slot(val, s)[:, u, 0:D] if b == BASES - 1 else part[:, u, b, :]
                        nc.vector.scalar_tensor_tensor(into, mul_ps[u][:, b, :], coe[s.h][:, u, b:b + 1],
                                                       part[:, u, b - 1, :], ALU.mult, ALU.add)\
                            .then_inc(val_set if b == BASES - 1 else added, 1)

            def body(at):
                if s := at(0):
                    wait_indices_used(dve, gathered, s, UT)
                    nc.vector.tensor_copy(src4[s.h][:, :], c.src_i[:, bass.ds(tile_columns(s), UT)]).then_inc(src_set, 1)
                if s := at(1):
                    t = bass.ds(tile_columns(s), UT)
                    dve.wait_ge(dst_turned, after(s, U))
                    nc.vector.tensor_copy(next4[s.h][:, :], c.next_f[:, t])
                    nc.vector.tensor_copy(dst4[s.h][:, :], c.dst_f[:, t]).then_inc(dst_set, 1)
                    nc.vector.tensor_tensor(hot[s.h][:, :, :], bc(c.typ_f[:, t], TYPES), mid(c.iota[:, :], UT),
                                            ALU.is_equal).then_inc(hot_set, 1)
                    w = c.coe[:, layer, :].rearrange("p (r b) -> p b r", b=BASES)
                    dve.wait_ge(hot_set, after(s))
                    for u in range(UT):
                        last = nc.vector.tensor_tensor(prod[:, u, :, :], mid(hot[s.h][:, u, :], BASES), w, ALU.mult)
                    last.then_inc(prod_set, 1)
                    dve.wait_ge(scaled, after_tile(s, 0, U))
                    dve.wait_ge(prod_set, after(s))
                    nc.vector.tensor_reduce(coe[s.h][:, :, :], prod[:, :, :, :], X, ALU.add).then_inc(coe_set, 1)
                if s := at(3):
                    dve.wait_ge(summed, after_tile(s, 0, 2))
                    if width > D:
                        nc.vector.tensor_copy(slot(val, s)[:, :, D:], hot[s.h][:, :, :])
                    combine(s, UP[0:2], 0)
                    combine(s, UP[2:4], UT)
                if s := at(1):
                    compare_targets(nc, dve, s, dst_ps, dst4, next4, same, join, summed, dst_turned, same_set)
            timeline(dve, STEPS, False, 4, body)

        @block.scalar
        def _(act):
            start(act, (xT_set,))
            start(act, (scaled, out_set), counts=UT)

            def body(at):
                for u in UP:
                    if s := at(2):
                        if u == UP[0]:
                            act.wait_ge(coe_set, after(s))
                        act.wait_ge(val_set, after_tile(s, u, 1))
                        act.wait_ge(mul, after_tile(s, u))
                        nc.scalar.activation(part[:, u, 0, :], mul_ps[u][:, 0, :], ACT.Copy, scale=coe[s.h][:, u, 0:1])\
                            .then_inc(scaled, 1)
                    if s := at(3):
                        if u == UP[0]:
                            act.wait_ge(stored[s.h], vacated(s))
                        act.wait_ge(summed, after_tile(s, u))
                        nc.scalar.copy(out[s.h][:, u, :], sum_ps[:, u, 0:width]).then_inc(out_set, 1)
                    if u == UP[1]:
                        if s := at(1):
                            act.wait_ge(mul, after_tile(s, 0, 2))
                            act.wait_ge(x_turned, after(s))
                            nc.scalar.copy(slot(xT, s)[:, :, :], xT_ps[:, :, :]).then_inc(xT_set, 1)
            timeline(act, STEPS, False, 4, body)

        @block.tensor
        def _(pe):
            start(pe, (dst_turned, x_turned))
            start(pe, (mul, summed), counts=UT)
            basis = c.bases[:, layer, :, :].rearrange("p b d -> p (b d)")

            def body(at):
                for u in UP:
                    if s := at(2):
                        if u == UP[0]:
                            pe.wait_ge(xT_set, after(s))
                        pe.wait_ge(val_set, after_tile(s, u, 1))
                        nc.tensor.matmul(mul_ps[u][:, :, :].rearrange("p b d -> p (b d)"), slot(xT, s)[:, u, :], basis,
                                         start=True, stop=True).then_inc(mul, 1)
                    if s := at(3):
                        sum_tile(nc, pe, s, u, same, join, val, out, sum_ps, width, same_set, val_set, out_set, summed)
                    if u == UP[1]:
                        if s := at(1):
                            turn_targets(nc, c, pe, s, dst4, dst_set, dst_ps, same_set, dst_turned)
                            pe.wait_ge(xT_set, after(s, 1))
                            pe.wait_ge(gathered[s.h], landed(s, UT))
                            for v in UP:
                                last = nc.tensor.transpose(xT_ps[:, v, :], xg[s.h][:, v, :], c.ident[:, :])
                            last.then_inc(x_turned, 1)
            timeline(pe, STEPS, False, 4, body)

        @block.sync
        def _(sp):
            store_sums(sp, table, out, out_set, stored, pace_out)
    ph.close()


def turn_targets(nc, c, pe, s, dst4, dst_set, dst_ps, same_set, dst_turned):
    pe.wait_ge(same_set, after(s, 1))
    pe.wait_ge(dst_set, after(s))
    for u in UP:
        last = nc.tensor.transpose(dst_ps[:, u, :], dst4[s.h][:, u:u + 1].to_broadcast([P, P]), c.ident[:, :])
    last.then_inc(dst_turned, 1)


def compare_targets(nc, dve, s, dst_ps, dst4, next4, same, join, summed, dst_turned, same_set):
    dve.wait_ge(summed, after_tile(s, 0, U))
    dve.wait_ge(dst_turned, after(s))
    nc.vector.tensor_tensor(join[s.h][:, :, :], dst_ps[0:1, :, :], bc(next4[s.h][:, :], P), ALU.is_equal)
    nc.vector.tensor_tensor(same[s.h][:, :, :], dst_ps[:, :, :], bc(dst4[s.h][:, :], P), ALU.is_equal)\
        .then_inc(same_set, 1)


def sum_tile(nc, pe, s, u, same, join, val, out, sum_ps, width, same_set, val_set, out_set, summed):
    first = isinstance(s.k, int) and s.k == 0 and u == UP[0]
    if u == UP[0]:
        pe.wait_ge(same_set, after(s))
    pe.wait_ge(val_set, after_tile(s, u))
    pe.wait_ge(out_set, after_tile(s, u) - 1)
    total = nc.tensor.matmul(sum_ps[:, u, 0:width], same[s.h][:, u, :], slot(val, s)[:, u, :], start=True, stop=first)
    if not first:
        above = out[(s.h - 1) % U][0:1, 0, :] if u == UP[0] else out[s.h][0:1, u + 1, :]
        total = nc.tensor.matmul(sum_ps[:, u, 0:width], join[s.h][:, u, :], above, start=False, stop=True)
    total.then_inc(summed, 1)


def store_sums(sp, table, out, out_set, stored, pace_out):
    start_dma(sp, stored)

    def body(at):
        if s := at(0):
            sp.wait_ge(out_set, after_tile(s, 0))
            sp.sem_inc(pace_out, 1)
            sp.dma_start(tile_rows(table, s), out[s.h][:, :, :]).then_inc(stored[s.h], 16)
    timeline(sp, STEPS, False, 1, body)
    wait_all(sp, stored, STEPS)


def attend_edges(nc, c, q, x1, table):
    ph = Phase(nc, "att")
    src4, dsti4 = ph.sb2("src4", [P, UT], I32, U), ph.sb2("dsti4", [P, UT], I32, U)
    dst4, next4 = ph.sb2("dst4", [P, UT], n=U), ph.sb2("next4", [1, UT], n=U)
    qg, xg, xT = ph.sb2("qg", [P, UT, D], n=U), ph.sb2("xg", [P, UT, D], n=U), ph.sb2("xT", [P, UT, P])
    qk, score = ph.sb("qk", [P, UT, D]), ph.sb2("score", [P, UT, HEADS])
    same, join = ph.sb2("same", [P, UT, P], n=U), ph.sb2("join", [1, UT, P], n=U)
    val, out = ph.sb2("val", [P, UT, CNT]), ph.sb2("out", [P, UT, CNT], n=U)
    dst_ps, xT_ps, sum_ps = ph.ps("dst_ps", [P, UT, P]), ph.ps("xT_ps", [P, UT, P]), ph.ps("sum_ps", [P, UT, 256])
    kv_ps = ph.ps2("kv_ps", [P, UT, 2 * D])
    gathered, stored, pace, pace_out = ph.sem2("gathered", U), ph.sem2("stored", U), ph.sem("pace"), ph.sem("pace_out")
    idx_set, dst_set, dst_turned, same_set, x_turned, xT_set, kv_set = (
        ph.sem(n) for n in ("idx_set", "dst_set", "dst_turned", "same_set", "x_turned", "xT_set", "kv_set"))
    qk_set, dots_set, score_set, low_set, exp_set, val_set = (
        ph.sem(n) for n in ("qk_set", "dots_set", "score_set", "low_set", "exp_set", "val_set"))
    summed, out_set = ph.sem("summed"), ph.sem("out_set")
    loads = 2 * UT
    with nc.Block() as block:
        @block.gpsimd
        def _(pool):
            def body(at):
                if s := at(0):
                    pool.wait_ge(qk_set, after(s, U))
                    pool.wait_ge(idx_set, after(s))
                    pool.sem_inc(pace, 1)
                    for u in UP:
                        for into, rows, idx in ((qg, q, dsti4), (xg, x1, src4)):
                            pool.indirect_dma_start(out=into[s.h][:, u, :], out_offset=None, in_=rows,
                                                    in_offset=bass.IndirectOffsetOnAxis(ap=idx[s.h][:, u:u + 1], axis=0))\
                                .then_inc(gathered[s.h], 16)
            timeline(pool, STEPS, False, 1, body)

        @block.vector
        def _(dve):
            start(dve, (idx_set, dst_set, same_set, qk_set, dots_set, score_set, low_set))
            start(dve, (val_set,), counts=UT)

            def body(at):
                if s := at(0):
                    t = bass.ds(tile_columns(s), UT)
                    wait_indices_used(dve, gathered, s, loads)
                    nc.vector.tensor_copy(src4[s.h][:, :], c.src_i[:, t])
                    nc.vector.tensor_copy(dsti4[s.h][:, :], c.dst_i[:, t]).then_inc(idx_set, 1)
                if s := at(1):
                    t = bass.ds(tile_columns(s), UT)
                    dve.wait_ge(dst_turned, after(s, U))
                    nc.vector.tensor_copy(next4[s.h][:, :], c.next_f[:, t])
                    nc.vector.tensor_copy(dst4[s.h][:, :], c.dst_f[:, t]).then_inc(dst_set, 1)
                if s := at(2):
                    dve.wait_ge(kv_set, after(s))
                    nc.vector.tensor_tensor(qk[:, :, :], qg[s.h][:, :, :], slot(kv_ps, s)[:, :, 0:D], ALU.mult)\
                        .then_inc(qk_set, 1)
                    dve.wait_ge(qk_set, after(s))
                    nc.vector.tensor_reduce(slot(score, s)[:, :, :], qk[:, :, :].rearrange("p u (h e) -> p u h e", e=HD),
                                            X, ALU.add).then_inc(dots_set, 1)
                    dve.wait_ge(dots_set, after(s))
                    nc.vector.tensor_scalar(slot(score, s)[:, :, :], slot(score, s)[:, :, :], 1.0 / HD ** 0.5, 5.0,
                                            ALU.mult, ALU.min).then_inc(low_set, 1)
                    dve.wait_ge(low_set, after(s))
                    nc.vector.tensor_scalar(slot(score, s)[:, :, :], slot(score, s)[:, :, :], -5.0, None, ALU.max)\
                        .then_inc(score_set, 1)
                if s := at(1):
                    compare_targets(nc, dve, s, dst_ps, dst4, next4, same, join, summed, dst_turned, same_set)
                if s := at(2):
                    dve.wait_ge(exp_set, after(s))
                    for u in UP:
                        nc.vector.tensor_tensor(slot(val, s)[:, u, 0:D].rearrange("p (h e) -> p h e", e=HD),
                                                slot(kv_ps, s)[:, u, D:].rearrange("p (h e) -> p h e", e=HD),
                                                bc(slot(val, s)[:, u, D:], HD), ALU.mult).then_inc(val_set, 1)
            timeline(dve, STEPS, False, 3, body)

        @block.scalar
        def _(act):
            start(act, (exp_set, xT_set))
            start(act, (out_set,), counts=UT)

            def body(at):
                if s := at(0):
                    act.wait_ge(kv_set, after(s, 2))
                    act.wait_ge(x_turned, after(s))
                    nc.scalar.copy(slot(xT, s)[:, :, :], xT_ps[:, :, :]).then_inc(xT_set, 1)
                if s := at(1):
                    act.wait_ge(summed, after_tile(s, 0, 2))
                    act.wait_ge(score_set, after(s))
                    nc.scalar.activation(slot(val, s)[:, :, D:], slot(score, s)[:, :, :], ACT.Exp).then_inc(exp_set, 1)
                if s := at(2):
                    for u in UP:
                        if u == UP[0]:
                            act.wait_ge(stored[s.h], vacated(s))
                        act.wait_ge(summed, after_tile(s, u))
                        nc.scalar.copy(out[s.h][:, u, :], sum_ps[:, u, 0:CNT]).then_inc(out_set, 1)
            timeline(act, STEPS, False, 3, body)

        @block.tensor
        def _(pe):
            start(pe, (dst_turned, x_turned, kv_set))
            start(pe, (summed,), counts=UT)

            def body(at):
                if s := at(0):
                    turn_targets(nc, c, pe, s, dst4, dst_set, dst_ps, same_set, dst_turned)
                    pe.wait_ge(xT_set, after(s, 1))
                    pe.wait_ge(gathered[s.h], landed(s, loads))
                    for u in UP:
                        last = nc.tensor.transpose(xT_ps[:, u, :], xg[s.h][:, u, :], c.ident[:, :])
                    last.then_inc(x_turned, 1)
                if s := at(1):
                    pe.wait_ge(xT_set, after(s))
                    pe.wait_ge(val_set, after_tile(s, 0, 2))
                    for u in UP:
                        last = nc.tensor.matmul(slot(kv_ps, s)[:, u, :], slot(xT, s)[:, u, :], c.qkv[:, D:],
                                                start=True, stop=True)
                    last.then_inc(kv_set, 1)
                if s := at(2):
                    for u in UP:
                        sum_tile(nc, pe, s, u, same, join, val, out, sum_ps, CNT, same_set, val_set, out_set, summed)
            timeline(pe, STEPS, False, 3, body)

        @block.sync
        def _(sp):
            store_sums(sp, table, out, out_set, stored, pace_out)
    ph.close()


def gather_groups(nc, c, pool, table, into, idx4, idx_set, used, gathered, pace):
    def body(at):
        if s := at(0):
            pool.wait_ge(used, after(s, U))
            pool.wait_ge(idx_set, after(s))
            pool.sem_inc(pace, 1)
            for j in range(JN):
                pool.indirect_dma_start(out=into[s.h][0:s.p, j, :], out_offset=None, in_=table,
                                        in_offset=bass.IndirectOffsetOnAxis(ap=idx4[s.h][0:s.p, j:j + 1], axis=0))\
                    .then_inc(gathered[s.h], 16)
    timeline(pool, FULL, True, 1, body)


def turn(nc, c, ps, rows, s):
    for j in range(JN):
        last = nc.tensor.transpose(ps[:, j * s.p:(j + 1) * s.p], rows[0:s.p, j, :], c.ident[0:s.p, 0:s.p])
    return last


def update_nodes(nc, c, h_in, table, h_out):
    ph = Phase(nc, "node0")
    idx4 = ph.sb2("idx4", [P, JN], I32, U)
    ag, ht, hs, z = (ph.sb2("ag", [P, JN, CNT], n=U), ph.sb2("ht", [P, JN, D], n=U), ph.sb2("hs", [P, JN, D], n=U),
                     ph.sb2("z", [P, JN, D], n=U))
    hT = ph.sb2("hT", [P, GROUP])
    rank, top = ph.sb("rank", [P, JN, TYPES]), ph.sb("top", [P, JN])
    hT_ps, mul_ps = ph.ps2("hT_ps", [P, GROUP]), ph.ps2("mul_ps", [P, JN, D], 4)
    h_in_s, gathered, stored = ph.sem2("h_in", U), ph.sem2("gathered", U), ph.sem2("stored", U)
    pace, idx_set, turned, copied, mul = (ph.sem(n) for n in ("pace", "idx_set", "turned", "copied", "mul"))
    norm_step, scaled, shifted, rectified = (ph.sem(n) for n in ("norm_step", "scaled", "shifted", "rectified"))
    LINKS = 8
    with nc.Block() as block:
        @block.gpsimd
        def _(pool):
            gather_groups(nc, c, pool, table, ag, idx4, idx_set, scaled, gathered, pace)

        @block.sync
        def _(sp):
            start_dma(sp, h_in_s, stored)

            def body(at):
                if s := at(0):
                    sp.wait_ge(turned, after(s, U))
                    sp.dma_start(ht[s.h][0:s.p, :, :], group_rows(h_in, s)).then_inc(h_in_s[s.h], 16)
                if s := at(3):
                    sp.wait_ge(rectified, after(s))
                    sp.dma_start(group_rows(h_out, s), hs[s.h][0:s.p, :, :]).then_inc(stored[s.h], 16)
            timeline(sp, FULL, True, 4, body)
            wait_all(sp, stored, GROUPS)

        @block.tensor
        def _(pe):
            start(pe, (turned, mul))

            def body(at):
                if s := at(0):
                    pe.wait_ge(h_in_s[s.h], arrived(s))
                    pe.wait_ge(copied, after(s, 2))
                    turn(nc, c, slot(hT_ps, s), ht[s.h], s).then_inc(turned, 1)
                if s := at(1):
                    pe.wait_ge(copied, after(s))
                    pe.wait_ge(scaled, after(s, 4))
                    for j in range(JN):
                        last = nc.tensor.matmul(mul_ps[s.h][0:s.p, j, :], slot(hT, s)[:, j * s.p:(j + 1) * s.p],
                                                c.loop[:, 0, :], start=True, stop=True)
                    last.then_inc(mul, 1)
            timeline(pe, FULL, True, 2, body)

        @block.scalar
        def _(act):
            start(act, (copied, rectified))

            def body(at):
                if s := at(0):
                    act.wait_ge(mul, after(s, 2))
                    act.wait_ge(turned, after(s))
                    nc.scalar.copy(slot(hT, s)[:, 0:s.n], slot(hT_ps, s)[:, 0:s.n]).then_inc(copied, 1)
                if s := at(3):
                    act.wait_ge(stored[s.h], vacated(s))
                    act.wait_ge(shifted, after(s))
                    nc.scalar.activation(hs[s.h][0:s.p, :, :], z[s.h][0:s.p, :, :], ACT.Relu).then_inc(rectified, 1)
            timeline(act, FULL, True, 4, body)

        @block.vector
        def _(dve):
            start(dve, (idx_set, scaled, shifted))

            def body(at):
                if s := at(0):
                    wait_indices_used(dve, gathered, s, JN)
                    nc.vector.tensor_copy(idx4[s.h][:, :], c.start_i[:, bass.ds(s.k * JN, JN)]).then_inc(idx_set, 1)
                if s := at(2):
                    p, n = s.p, 0
                    counts = ag[s.h][0:p, :, D:]
                    steps = [
                        lambda: nc.vector.tensor_scalar(rank[0:p, :, :], counts, 0.0, None, ALU.is_gt),
                        lambda: nc.vector.tensor_tensor(rank[0:p, :, :], rank[0:p, :, :], mid(c.iota1[0:p, :], JN), ALU.mult),
                        lambda: nc.vector.tensor_reduce(top[0:p, :], rank[0:p, :, :], X, ALU.max),
                        lambda: nc.vector.tensor_tensor(rank[0:p, :, :], rank[0:p, :, :], bc(top[0:p, :], TYPES), ALU.is_equal),
                        lambda: nc.vector.tensor_tensor(rank[0:p, :, :], rank[0:p, :, :], counts, ALU.mult),
                        lambda: nc.vector.tensor_reduce(top[0:p, :], rank[0:p, :, :], X, ALU.add),
                        lambda: nc.vector.tensor_scalar(top[0:p, :], top[0:p, :], 1.0, None, ALU.max),
                        lambda: nc.vector.reciprocal(top[0:p, :], top[0:p, :]),
                    ]
                    dve.wait_ge(gathered[s.h], landed(s, JN))
                    for step in steps:
                        n += 1
                        step().then_inc(norm_step, 1)
                        dve.wait_ge(norm_step, s.k * LINKS + n)
                    nc.vector.tensor_copy(c.norm[0:p, bass.ds(s.k * JN, JN)], top[0:p, :])
                    dve.wait_ge(mul, after(s))
                    dve.wait_ge(rectified, after(s, U))
                    for j in range(JN):
                        last = nc.vector.scalar_tensor_tensor(z[s.h][0:p, j, :], ag[s.h][0:p, j, 0:D], top[0:p, j:j + 1],
                                                              mul_ps[s.h][0:p, j, :], ALU.mult, ALU.add)
                    last.then_inc(scaled, 1)
                    dve.wait_ge(scaled, after(s))
                    nc.vector.tensor_tensor(z[s.h][0:p, :, :], z[s.h][0:p, :, :], mid(c.bn[0:p, 0, 1, :], JN), ALU.add)\
                        .then_inc(shifted, 1)
            timeline(dve, FULL, True, 3, body)
    ph.close()


def finish_conv(nc, c, x, h_in, table, x1_out, q_out):
    ph = Phase(nc, "node1")
    idx4, norm4 = ph.sb2("idx4", [P, JN], I32, U), ph.sb2("norm4", [P, JN], n=U)
    ag, ht, xt, z, x1, qs = (ph.sb2(n, [P, JN, D], n=U) for n in ("ag", "ht", "xt", "z", "x1", "qs"))
    hT, x1T = ph.sb2("hT", [P, GROUP]), ph.sb2("x1T", [P, GROUP])
    stats, mv, sd = ph.sb("stats", [P, JN, 6]), ph.sb2("mv", [P, JN, 2], n=U), ph.sb2("sd", [P, JN], n=U)
    rstd, off = ph.sb2("rstd", [P, JN], n=U), ph.sb2("off", [P, JN], n=U)
    hT_ps, mul_ps, x1T_ps, q_ps = (ph.ps2("hT_ps", [P, GROUP]), ph.ps2("mul_ps", [P, JN, D], 4), ph.ps("x1T_ps", [P, GROUP]),
                                   ph.ps("q_ps", [P, JN, D]))
    h_in_s, x_in, gathered = ph.sem2("h_in", U), ph.sem2("x_in", U), ph.sem2("gathered", U)
    x1_st, q_st, pace_bn = ph.sem2("x1_st", U), ph.sem2("q_st", U), ph.sem("pace_bn")
    pace, idx_set, turned, copied, mul = (ph.sem(n) for n in ("pace", "idx_set", "turned", "copied", "mul"))
    scaled, summed, counted, mv_set, sd_set, rstd_set, off_set, x1_set = (
        ph.sem(n) for n in ("scaled", "summed", "counted", "mv_set", "sd_set", "rstd_set", "off_set", "x1_set"))
    x1_turned, x1_copied, q_mul, q_set = (ph.sem(n) for n in ("x1_turned", "x1_copied", "q_mul", "q_set"))
    with nc.Block() as block:
        @block.gpsimd
        def _(pool):
            gather_groups(nc, c, pool, table, ag, idx4, idx_set, scaled, gathered, pace)

        @block.sync
        def _(sp):
            start_dma(sp, h_in_s, x_in, x1_st, q_st)

            def body(at):
                if s := at(0):
                    sp.wait_ge(turned, after(s, U))
                    sp.dma_start(ht[s.h][0:s.p, :, :], group_rows(h_in, s)).then_inc(h_in_s[s.h], 16)
                    sp.wait_ge(summed, after(s, U))
                    sp.dma_start(xt[s.h][0:s.p, :, :], group_rows(x, s)).then_inc(x_in[s.h], 16)
                if s := at(5):
                    sp.wait_ge(x1_set, after(s))
                    sp.dma_start(group_rows(x1_out, s), x1[s.h][0:s.p, :, :]).then_inc(x1_st[s.h], 16)
                if s := at(7):
                    sp.wait_ge(q_set, after(s))
                    sp.dma_start(group_rows(q_out, s), qs[s.h][0:s.p, :, :]).then_inc(q_st[s.h], 16)
            timeline(sp, FULL, True, 8, body)
            wait_all(sp, x1_st, GROUPS)
            wait_all(sp, q_st, GROUPS)

        @block.tensor
        def _(pe):
            start(pe, (turned, mul, x1_turned, q_mul))

            def body(at):
                if s := at(0):
                    pe.wait_ge(h_in_s[s.h], arrived(s))
                    pe.wait_ge(copied, after(s, 2))
                    turn(nc, c, slot(hT_ps, s), ht[s.h], s).then_inc(turned, 1)
                if s := at(1):
                    pe.wait_ge(copied, after(s))
                    pe.wait_ge(scaled, after(s, 4))
                    for j in range(JN):
                        nc.tensor.matmul(mul_ps[s.h][0:s.p, j, :], hT[s.h % 2][:, j * s.p:(j + 1) * s.p],
                                         c.loop[:, 1, :], start=True, stop=False)
                        last = nc.tensor.matmul(mul_ps[s.h][0:s.p, j, :], c.ones[0:1, 0:s.p], c.bn[0:1, 1, 1, :],
                                                start=False, stop=True)
                    last.then_inc(mul, 1)
                if s := at(5):
                    pe.wait_ge(x1_set, after(s))
                    pe.wait_ge(x1_copied, after(s, 1))
                    turn(nc, c, x1T_ps, x1[s.h], s).then_inc(x1_turned, 1)
                if s := at(6):
                    pe.wait_ge(x1_copied, after(s))
                    pe.wait_ge(q_set, after(s, 1))
                    for j in range(JN):
                        last = nc.tensor.matmul(q_ps[0:s.p, j, :], slot(x1T, s)[:, j * s.p:(j + 1) * s.p], c.qkv[:, 0:D],
                                                start=True, stop=True)
                    last.then_inc(q_mul, 1)
            timeline(pe, FULL, True, 7, body)

        @block.scalar
        def _(act):
            start(act, (copied, x1_copied, sd_set, x1_set, q_set))

            def body(at):
                if s := at(0):
                    act.wait_ge(mul, after(s, 2))
                    act.wait_ge(turned, after(s))
                    nc.scalar.copy(slot(hT, s)[:, 0:s.n], slot(hT_ps, s)[:, 0:s.n]).then_inc(copied, 1)
                if s := at(3):
                    act.wait_ge(rstd_set, after(s, U))
                    act.wait_ge(mv_set, after(s))
                    nc.scalar.activation(sd[s.h][0:s.p, :], mv[s.h][0:s.p, :, 1], ACT.Sqrt, bias=c.eps[0:s.p, 1:2])\
                        .then_inc(sd_set, 1)
                if s := at(5):
                    act.wait_ge(q_mul, after(s, 2))
                    act.wait_ge(x1_turned, after(s))
                    nc.scalar.copy(slot(x1T, s)[:, 0:s.n], x1T_ps[:, 0:s.n]).then_inc(x1_copied, 1)
                if s := at(6):
                    act.wait_ge(q_st[s.h], vacated(s))
                    act.wait_ge(q_mul, after(s))
                    nc.scalar.copy(qs[s.h][0:s.p, :, :], q_ps[0:s.p, :, :]).then_inc(q_set, 1)
                if s := at(4):
                    act.wait_ge(x1_st[s.h], vacated(s))
                    act.wait_ge(x1_turned, after(s, U))
                    act.wait_ge(off_set, after(s))
                    for j in range(JN):
                        last = nc.scalar.activation(x1[s.h][0:s.p, j, :], z[s.h][0:s.p, j, :], ACT.Identity,
                                                    bias=off[s.h][0:s.p, j:j + 1], scale=rstd[s.h][0:s.p, j:j + 1])
                    last.then_inc(x1_set, 1)
            timeline(act, FULL, True, 7, body)

        @block.vector
        def _(dve):
            start(dve, (idx_set, scaled, summed, counted, mv_set, rstd_set, off_set))

            def body(at):
                if s := at(0):
                    wait_indices_used(dve, gathered, s, JN)
                    nc.vector.tensor_copy(norm4[s.h][:, :], c.norm[:, bass.ds(s.k * JN, JN)])
                    nc.vector.tensor_copy(idx4[s.h][:, :], c.start_i[:, bass.ds(s.k * JN, JN)]).then_inc(idx_set, 1)
                if s := at(2):
                    p, r = s.p, z[s.h]
                    dve.wait_ge(x1_set, after(s, U))
                    dve.wait_ge(gathered[s.h], landed(s, JN))
                    dve.wait_ge(mul, after(s))
                    for j in range(JN):
                        last = nc.vector.scalar_tensor_tensor(r[0:p, j, :], ag[s.h][0:p, j, :], norm4[s.h][0:p, j:j + 1],
                                                              mul_ps[s.h][0:p, j, :], ALU.mult, ALU.add)
                    last.then_inc(scaled, 1)
                    dve.wait_ge(scaled, after(s))
                    dve.wait_ge(x_in[s.h], arrived(s))
                    nc.vector.scalar_tensor_tensor(r[0:p, :, :], r[0:p, :, :], 0.0, xt[s.h][0:p, :, :], ALU.max, ALU.add)\
                        .then_inc(summed, 1)
                    dve.wait_ge(summed, after(s))
                    statistics(nc, dve, s, r, stats, mv, counted, mv_set, sd_set, pace_bn)
                if s := at(3):
                    scale_and_offset(nc, dve, s, mv, sd, rstd, off, sd_set, rstd_set, x1_set, off_set)
            timeline(dve, FULL, True, 4, body)
    ph.close()


def statistics(nc, dve, s, rows, stats, mv, counted, mv_set, sd_set, pace_bn):
    for j in range(JN):
        last = nc.vector.bn_stats(stats[0:s.p, j, :], rows[0:s.p, j, :])
    last.then_inc(counted, 1)
    dve.wait_ge(sd_set, after(s, U))
    dve.wait_ge(counted, after(s))
    dve.sem_inc(pace_bn, 1)
    for j in range(JN):
        last = nc.vector.bn_aggr(mv[s.h][0:s.p, j, :], stats[0:s.p, j, :])
    last.then_inc(mv_set, 1)


def scale_and_offset(nc, dve, s, mv, sd, rstd, off, sd_set, rstd_set, applied, off_set):
    dve.wait_ge(applied, after(s, U))
    dve.wait_ge(sd_set, after(s))
    nc.vector.reciprocal(rstd[s.h][0:s.p, :], sd[s.h][0:s.p, :]).then_inc(rstd_set, 1)
    dve.wait_ge(rstd_set, after(s))
    nc.vector.scalar_tensor_tensor(off[s.h][0:s.p, :], mv[s.h][0:s.p, :, 0], -1.0, rstd[s.h][0:s.p, :], ALU.mult,
                                   ALU.mult).then_inc(off_set, 1)


def group_cols(table, s):
    return table[bass.ds(s.k, 1), :, 0:s.n].rearrange("g f n -> (g f) n")


def project_nodes(nc, c, table, x1_in, y_out):
    ph = Phase(nc, "proj")
    idx4 = ph.sb2("idx4", [P, JN], I32, U)
    ag, xb, o, y = (ph.sb2("ag", [P, JN, CNT], n=U), ph.sb2("xb", [P, JN, D], n=U), ph.sb2("o", [P, JN, D], n=U),
                    ph.sb2("y", [P, GROUP], n=U))
    oT = ph.sb2("oT", [P, GROUP])
    den, inv = ph.sb("den", [P, JN, HEADS]), ph.sb("inv", [P, JN, HEADS])
    oT_ps, mul_ps = ph.ps2("oT_ps", [P, GROUP]), ph.ps2("mul_ps", [P, GROUP], 4)
    x_in, gathered, stored = ph.sem2("x_in", U), ph.sem2("gathered", U), ph.sem2("stored", U)
    pace, idx_set, den_set, inv_set, o_set, turned, copied, mul, y_set, counted = (
        ph.sem(n) for n in ("pace", "idx_set", "den_set", "inv_set", "o_set", "turned", "copied", "mul", "y_set",
                            "counted"))
    with nc.Block() as block:
        @block.gpsimd
        def _(pool):
            gather_groups(nc, c, pool, table, ag, idx4, idx_set, o_set, gathered, pace)

        @block.sync
        def _(sp):
            start_dma(sp, x_in, stored)

            def body(at):
                if s := at(0):
                    sp.wait_ge(mul, after(s, U))
                    sp.dma_start(xb[s.h][0:s.p, :, :], group_rows(x1_in, s)).then_inc(x_in[s.h], 16)
                if s := at(3):
                    sp.wait_ge(y_set, after(s))
                    sp.dma_start(group_cols(y_out, s), y[s.h][:, 0:s.n]).then_inc(stored[s.h], 16)
            timeline(sp, FULL, True, 4, body)
            wait_all(sp, stored, GROUPS)

        @block.vector
        def _(dve):
            start(dve, (idx_set, den_set, inv_set, o_set, counted))

            def body(at):
                if s := at(0):
                    wait_indices_used(dve, gathered, s, JN)
                    nc.vector.tensor_copy(idx4[s.h][:, :], c.start_i[:, bass.ds(s.k * JN, JN)]).then_inc(idx_set, 1)
                if s := at(2):
                    p = s.p
                    dve.wait_ge(gathered[s.h], landed(s, JN))
                    nc.vector.tensor_scalar(den[0:p, :, :], ag[s.h][0:p, :, D:], 1e-30, None, ALU.max).then_inc(den_set, 1)
                    dve.wait_ge(den_set, after(s))
                    nc.vector.reciprocal(inv[0:p, :, :], den[0:p, :, :]).then_inc(inv_set, 1)
                    dve.wait_ge(inv_set, after(s))
                    dve.wait_ge(turned, after(s, U))
                    for j in range(JN):
                        last = nc.vector.tensor_tensor(o[s.h][0:p, j, :].rearrange("p (h e) -> p h e", e=HD),
                                                       ag[s.h][0:p, j, 0:D].rearrange("p (h e) -> p h e", e=HD),
                                                       bc(inv[0:p, j, :], HD), ALU.mult)
                    last.then_inc(o_set, 1)
                if s := at(5):
                    dve.wait_ge(y_set, after(s))
                    nc.vector.bn_stats(c.stats[:, bass.ds(s.k * 6, 6)], y[s.h][:, 0:s.n]).then_inc(counted, 1)
            timeline(dve, FULL, True, 6, body)

        @block.tensor
        def _(pe):
            start(pe, (turned, mul))

            def body(at):
                if s := at(0):
                    pe.wait_ge(o_set, after(s))
                    pe.wait_ge(copied, after(s, 2))
                    turn(nc, c, slot(oT_ps, s), o[s.h], s).then_inc(turned, 1)
                if s := at(1):
                    pe.wait_ge(y_set, after(s, 4))
                    pe.wait_ge(copied, after(s))
                    nc.tensor.matmul(mul_ps[s.h][:, 0:s.n], c.wo[:, :], slot(oT, s)[:, 0:s.n], start=True, stop=False)
                    pe.wait_ge(x_in[s.h], arrived(s))
                    for j in range(JN):
                        last = nc.tensor.matmul(mul_ps[s.h][:, j * s.p:(j + 1) * s.p], xb[s.h][0:s.p, j, :],
                                                c.ident[0:s.p, 0:s.p], start=False, stop=j == JN - 1)
                    last.then_inc(mul, 1)
            timeline(pe, FULL, True, 2, body)

        @block.scalar
        def _(act):
            start(act, (copied, y_set))

            def body(at):
                if s := at(0):
                    act.wait_ge(mul, after(s, 2))
                    act.wait_ge(turned, after(s))
                    nc.scalar.copy(slot(oT, s)[:, 0:s.n], slot(oT_ps, s)[:, 0:s.n]).then_inc(copied, 1)
                if s := at(2):
                    act.wait_ge(stored[s.h], vacated(s))
                    act.wait_ge(counted, after(s, U))
                    act.wait_ge(mul, after(s))
                    nc.scalar.activation(y[s.h][:, 0:s.n], mul_ps[s.h][:, 0:s.n], ACT.Identity, bias=c.col[:, 0:1])\
                        .then_inc(y_set, 1)
            timeline(act, FULL, True, 3, body)
    ph.close()


def close_stats(nc, dve, c, mv, aff, gamma, beta, link, root):
    nc.vector.bn_aggr(mv[:, :], c.stats[:, :]).then_inc(link, 1)
    dve.wait_ge(link, 1)
    dve.wait_ge(root, 1)
    nc.vector.reciprocal(aff[:, 2:3], aff[:, 2:3]).then_inc(link, 1)
    dve.wait_ge(link, 2)
    nc.vector.tensor_tensor(aff[:, 0:1], aff[:, 2:3], gamma, ALU.mult).then_inc(link, 1)
    dve.wait_ge(link, 3)
    nc.vector.tensor_tensor(aff[:, 2:3], aff[:, 0:1], mv[:, 0:1], ALU.mult).then_inc(link, 1)
    dve.wait_ge(link, 4)
    nc.vector.tensor_tensor(aff[:, 1:2], beta, aff[:, 2:3], ALU.subtract).then_inc(link, 1)


def root_stats(nc, act, c, mv, aff, link, root):
    act.wait_ge(link, 1)
    nc.scalar.activation(aff[:, 2:3], mv[:, 1:2], ACT.Sqrt, bias=c.eps[:, 1:2]).then_inc(root, 1)
    act.wait_ge(link, 5)


def feed_forward(nc, c, y_in, y_out):
    ph = Phase(nc, "ffn")
    yb, hb, f, y2 = (ph.sb2("yb", [P, GROUP], n=U), ph.sb2("hb", [P, GROUP], n=U), ph.sb2("f", [P, 2, GROUP]),
                     ph.sb2("y2", [P, GROUP], n=U))
    mv, aff = ph.sb("mv", [P, 2]), ph.sb("aff", [P, 3])
    f_ps = [ph.ps2(f"f{a}_ps", [P, GROUP]) for a in range(2)]
    g_ps = ph.ps2("g_ps", [P, GROUP])
    y_in_s, stored = ph.sem2("y_in", U), ph.sem2("stored", U)
    link, root, h_set, f_mul, f0_set, f1_set, mul, y2_set, counted = (
        ph.sem(n) for n in ("link", "root", "h_set", "f_mul", "f0_set", "f1_set", "mul", "y2_set", "counted"))
    with nc.Block() as block:
        @block.sync
        def _(sp):
            start_dma(sp, y_in_s, stored)

            def body(at):
                if s := at(0):
                    sp.wait_ge(h_set, after(s, U))
                    sp.dma_start(yb[s.h][:, 0:s.n], group_cols(y_in, s)).then_inc(y_in_s[s.h], 16)
                if s := at(3):
                    sp.wait_ge(y2_set, after(s))
                    sp.dma_start(group_cols(y_out, s), y2[s.h][:, 0:s.n]).then_inc(stored[s.h], 16)
            timeline(sp, FULL, True, 4, body)
            wait_all(sp, stored, GROUPS)

        @block.scalar
        def _(act):
            start(act, (h_set, f0_set))
            root_stats(nc, act, c, mv, aff, link, root)

            def body(at):
                if s := at(0):
                    act.wait_ge(y2_set, after(s, U))
                    act.wait_ge(y_in_s[s.h], arrived(s))
                    nc.scalar.activation(hb[s.h][:, 0:s.n], yb[s.h][:, 0:s.n], ACT.Identity, bias=aff[:, 1:2],
                                         scale=aff[:, 0:1]).then_inc(h_set, 1)
                if s := at(1):
                    act.wait_ge(mul, after(s, 2))
                    act.wait_ge(f_mul, after(s))
                    nc.scalar.activation(f[s.h % 2][:, 0, 0:s.n], f_ps[0][s.h % 2][:, 0:s.n], ACT.Relu, bias=c.b1[:, 0:1])\
                        .then_inc(f0_set, 1)
            timeline(act, FULL, True, 2, body)

        @block.tensor
        def _(pe):
            start(pe, (f_mul, mul))

            def body(at):
                if s := at(0):
                    pe.wait_ge(f0_set, after(s, 2))
                    pe.wait_ge(f1_set, after(s, 2))
                    pe.wait_ge(h_set, after(s))
                    for a in range(2):
                        last = nc.tensor.matmul(f_ps[a][s.h % 2][:, 0:s.n], c.w1[:, a * P:(a + 1) * P], hb[s.h][:, 0:s.n],
                                                start=True, stop=True)
                    last.then_inc(f_mul, 1)
                if s := at(1):
                    pe.wait_ge(y2_set, after(s, 2))
                    pe.wait_ge(f0_set, after(s))
                    pe.wait_ge(f1_set, after(s))
                    for a in range(2):
                        last = nc.tensor.matmul(g_ps[s.h % 2][:, 0:s.n], c.w2[:, a, :], f[s.h % 2][:, a, 0:s.n],
                                                start=a == 0, stop=a == 1)
                    last.then_inc(mul, 1)
            timeline(pe, FULL, True, 2, body)

        @block.vector
        def _(dve):
            start(dve, (f1_set, y2_set, counted))
            close_stats(nc, dve, c, mv, aff, c.col[:, 2:3], c.col[:, 3:4], link, root)

            def body(at):
                if s := at(0):
                    dve.wait_ge(mul, after(s, 2))
                    dve.wait_ge(f_mul, after(s))
                    nc.vector.tensor_scalar(f[s.h % 2][:, 1, 0:s.n], f_ps[1][s.h % 2][:, 0:s.n], c.b1[:, 1:2], 0.0,
                                            ALU.add, ALU.max).then_inc(f1_set, 1)
                if s := at(1):
                    dve.wait_ge(stored[s.h], vacated(s))
                    dve.wait_ge(mul, after(s))
                    nc.vector.scalar_tensor_tensor(y2[s.h][:, 0:s.n], g_ps[s.h % 2][:, 0:s.n], c.col[:, 1:2],
                                                   hb[s.h][:, 0:s.n], ALU.add, ALU.add).then_inc(y2_set, 1)
                    dve.wait_ge(y2_set, after(s))
                    nc.vector.bn_stats(c.stats[:, bass.ds(s.k * 6, 6)], y2[s.h][:, 0:s.n]).then_inc(counted, 1)
            timeline(dve, FULL, True, 2, body)
    ph.close()


def final_norm(nc, c, x1_in, y_in, out):
    ph = Phase(nc, "fin")
    yb, ub = ph.sb2("yb", [P, GROUP], n=U), ph.sb2("ub", [P, GROUP], n=U)
    xb, r, rows = (ph.sb2(n, [P, JN, D], n=U) for n in ("xb", "r", "rows"))
    stats, mv2, sd = ph.sb("stats", [P, JN, 6]), ph.sb2("mv2", [P, JN, 2], n=U), ph.sb2("sd", [P, JN], n=U)
    rstd, off = ph.sb2("rstd", [P, JN], n=U), ph.sb2("off", [P, JN], n=U)
    mv, aff = ph.sb("mv", [P, 2]), ph.sb("aff", [P, 3])
    u_ps = ph.ps2("u_ps", [P, JN, D], 4)
    y_in_s, x_in, stored = ph.sem2("y_in", U), ph.sem2("x_in", U), ph.sem2("stored", U)
    link, root, u_set, turned, r_set, counted, mv_set, sd_set, rstd_set, off_set, rows_set, pace_bn = (
        ph.sem(n) for n in ("link", "root", "u_set", "turned", "r_set", "counted", "mv_set", "sd_set", "rstd_set",
                            "off_set", "rows_set", "pace_bn"))
    with nc.Block() as block:
        @block.sync
        def _(sp):
            start_dma(sp, y_in_s, x_in, stored)

            def body(at):
                if s := at(0):
                    sp.wait_ge(u_set, after(s, U))
                    sp.dma_start(yb[s.h][:, 0:s.n], group_cols(y_in, s)).then_inc(y_in_s[s.h], 16)
                    sp.wait_ge(r_set, after(s, U))
                    sp.dma_start(xb[s.h][0:s.p, :, :], group_rows(x1_in, s)).then_inc(x_in[s.h], 16)
                if s := at(5):
                    sp.wait_ge(rows_set, after(s))
                    sp.dma_start(group_rows(out, s), rows[s.h][0:s.p, :, :]).then_inc(stored[s.h], 16)
            timeline(sp, FULL, True, 6, body)
            wait_all(sp, stored, GROUPS)

        @block.scalar
        def _(act):
            start(act, (u_set, sd_set, rows_set))
            root_stats(nc, act, c, mv, aff, link, root)

            def body(at):
                if s := at(3):
                    act.wait_ge(rstd_set, after(s, U))
                    act.wait_ge(mv_set, after(s))
                    nc.scalar.activation(sd[s.h][0:s.p, :], mv2[s.h][0:s.p, :, 1], ACT.Sqrt, bias=c.eps[0:s.p, 1:2])\
                        .then_inc(sd_set, 1)
                if s := at(0):
                    act.wait_ge(turned, after(s, U))
                    act.wait_ge(y_in_s[s.h], arrived(s))
                    nc.scalar.activation(ub[s.h][:, 0:s.n], yb[s.h][:, 0:s.n], ACT.Identity, bias=aff[:, 1:2],
                                         scale=aff[:, 0:1]).then_inc(u_set, 1)
                if s := at(4):
                    act.wait_ge(stored[s.h], vacated(s))
                    act.wait_ge(off_set, after(s))
                    for j in range(JN):
                        last = nc.scalar.activation(rows[s.h][0:s.p, j, :], r[s.h][0:s.p, j, :], ACT.Identity,
                                                    bias=off[s.h][0:s.p, j:j + 1], scale=rstd[s.h][0:s.p, j:j + 1])
                    last.then_inc(rows_set, 1)
            timeline(act, FULL, True, 5, body)

        @block.tensor
        def _(pe):
            start(pe, (turned,))

            def body(at):
                if s := at(0):
                    pe.wait_ge(r_set, after(s, U))
                    pe.wait_ge(u_set, after(s))
                    for j in range(JN):
                        last = nc.tensor.transpose(u_ps[s.h][0:s.p, j, :], ub[s.h][:, j * s.p:(j + 1) * s.p], c.ident[:, :])
                    last.then_inc(turned, 1)
            timeline(pe, FULL, True, 1, body)

        @block.vector
        def _(dve):
            start(dve, (r_set, counted, mv_set, rstd_set, off_set))
            close_stats(nc, dve, c, mv, aff, c.col[:, 4:5], c.col[:, 5:6], link, root)

            def body(at):
                if s := at(1):
                    dve.wait_ge(rows_set, after(s, U))
                    dve.wait_ge(x_in[s.h], arrived(s))
                    dve.wait_ge(turned, after(s))
                    nc.vector.tensor_tensor(r[s.h][0:s.p, :, :], u_ps[s.h][0:s.p, :, :], xb[s.h][0:s.p, :, :], ALU.add)\
                        .then_inc(r_set, 1)
                    dve.wait_ge(r_set, after(s))
                    statistics(nc, dve, s, r[s.h], stats, mv2, counted, mv_set, sd_set, pace_bn)
                if s := at(2):
                    scale_and_offset(nc, dve, s, mv2, sd, rstd, off, sd_set, rstd_set, rows_set, off_set)
            timeline(dve, FULL, True, 3, body)
    ph.close()


class Constants:
    pass


def build(nc, w, out):
    with ExitStack() as ctx:
        c = Constants()

        def keep(name, shape, dt=F32):
            return ctx.enter_context(nc.sbuf_tensor(name, shape, dt))

        c.ident, c.ones, c.lower = keep("ident", [P, P]), keep("ones", [P, P]), keep("lower", [P, P])
        c.iota_i, c.iota16 = keep("iota_i", [P, TILES], I32), keep("iota16", [P, TILES], F16)
        c.iota, c.iota1 = keep("iota", [P, TYPES]), keep("iota1", [P, TYPES])
        c.rows, c.after = keep("rows", [P, 3, 4, P], I32), keep("after", [P, 4, P], I32)
        c.src_i, c.dst_i, c.start_i = (keep(n, [P, TILES], I32) for n in ("src_i", "dst_i", "start_i"))
        c.dst_f, c.typ_f, c.place_p, c.place_f, c.count, c.norm = (
            keep(n, [P, TILES]) for n in ("dst_f", "typ_f", "place_p", "place_f", "count", "norm"))
        c.next_f = keep("next_f", [1, TILES])
        c.w_emb, c.b_emb = keep("w_emb", [P, D]), keep("b_emb", [P, D])
        c.bases, c.loop = keep("bases", [P, LAYERS, BASES, D]), keep("loop", [P, LAYERS, D])
        c.coe, c.bn = keep("coe", [P, LAYERS, TYPES * BASES]), keep("bn", [P, LAYERS, 4, D])
        c.qkv, c.wo, c.w1, c.w2 = keep("qkv", [P, 3 * D]), keep("wo", [P, D]), keep("w1", [P, 2 * D]), keep("w2", [P, 2, D])
        c.b1, c.col, c.stats = keep("b1", [P, 2]), keep("col", [P, 6]), keep("stats", [P, GROUPS * 6])
        c.zero, c.eps = keep("zero", [1, CNT]), keep("eps", [P, 2])
        h0, h1, x1, q = (nc.dram_tensor(n, (NODES, D), F32, kind="Internal").ap() for n in ("h0", "h1", "x1", "q"))
        sums0, att = (nc.dram_tensor(n, (EPAD + 1, CNT), F32, kind="Internal").ap() for n in ("sums0", "att"))
        sums1 = nc.dram_tensor("sums1", (EPAD + 1, D), F32, kind="Internal").ap()
        y1T, y2T = (nc.dram_tensor(n, (GROUPS, P, GROUP), F32, kind="Internal").ap() for n in ("y1T", "y2T"))
        c.zero_rows = [(t, n) for t, n in ((sums0, CNT), (att, CNT), (sums1, D))]
        load_constants(nc, c, w)
        arrange_edges(nc, c)
        embed_nodes(nc, c, w["x"], h0)
        index_nodes(nc, c)
        conv_edges(nc, c, 0, h0, sums0, CNT)
        update_nodes(nc, c, h0, sums0, h1)
        conv_edges(nc, c, 1, h1, sums1, D)
        finish_conv(nc, c, w["x"], h1, sums1, x1, q)
        attend_edges(nc, c, q, x1, att)
        project_nodes(nc, c, att, x1, y1T)
        feed_forward(nc, c, y1T, y2T)
        final_norm(nc, c, x1, y2T, out)


NAMES = ["x", "src", "dst", "edge_type_8", "L0_gnn_W_emb", "L0_gnn_b_emb", "L0_gnn_bases", "L0_gnn_w_coe",
         "L0_gnn_self_loop", "L0_gnn_bn_gamma", "L0_gnn_bn_beta", "L0_gnn_bn_mean", "L0_gnn_bn_var", "L1_gnn_Wq",
         "L1_gnn_Wk", "L1_gnn_Wv", "L1_gnn_Wo", "L1_gnn_bo", "L1_gnn_W1", "L1_gnn_b1", "L1_gnn_W2", "L1_gnn_b2",
         "L1_gnn_g1", "L1_gnn_be1", "L1_gnn_g2", "L1_gnn_be2"]


def kernel(**inputs):
    import concourse.bacc as bacc
    from concourse.bass_utils import run_bass_kernel_spmd

    nc = bacc.Bacc("TRN2", target_bir_lowering=False, num_devices=1)
    arrays, w = {}, {}
    for name in NAMES:
        a = np.ascontiguousarray(inputs[name])
        arrays["in_" + name] = a
        w[name] = nc.dram_tensor("in_" + name, a.shape, mybir.dt.from_np(a.dtype), kind="ExternalInput").ap()
    out = nc.dram_tensor("out", (NODES, D), F32, kind="ExternalOutput").ap()
    build(nc, w, out)
    return run_bass_kernel_spmd(nc, [arrays], core_ids=[0]).results[0]["out"]
```

```python
import numpy as np
import concourse.bass as bass
from concourse import mybir
from concourse.alu_op_type import AluOpType as ALU
from contextlib import ExitStack

F32 = mybir.dt.float32
F16 = mybir.dt.float16
BF16 = mybir.dt.bfloat16
I32 = mybir.dt.int32
ACT = mybir.ActivationFunctionType
X = mybir.AxisListType.X

NODES, EDGES, D, P = 50000, 50000, 128, 128
TYPES, BASES, LAYERS = 8, 4, 2
HEADS, HD = 8, 16
BN_EPS, EPS = 0.001, 1e-5
JN = 4
GROUP = P * JN
FULL = NODES // GROUP
TAIL_P = (NODES - FULL * GROUP) // JN
assert FULL * GROUP + TAIL_P * JN == NODES
GROUPS = FULL + 1
UT = 4
COLS = GROUPS * JN
EDGES_T = P - 1
TILES = -(-EDGES // (EDGES_T * UT)) * UT
STEPS = TILES // UT
WHOLE = 3 * P
REST = EDGES // EDGES_T - WHOLE
LEFT = EDGES - (WHOLE + REST) * EDGES_T
EPAD = TILES * P
ZROW = EPAD
PAD_DST = 60000
CNT = D + TYPES


class Step:

    def __init__(self, unroll, i, h, parts=P):
        self.u, self.h, self.i, self.k = unroll, h, i, i * unroll + h
        self.p, self.n = parts, parts * JN


U = 4


def timeline(eng, full, tail, depth, body, unroll=U):
    total = full + (1 if tail else 0)
    lo = -(-(depth - 1) // unroll) * unroll
    rounds = (full - lo) // unroll

    def peeled(t):
        def at(s):
            k = t - s
            if 0 <= k < total:
                return Step(unroll, k // unroll, k % unroll, P if k < full else TAIL_P)
        body(at)

    for t in range(lo):
        peeled(t)
    with eng.Fori(lo // unroll, lo // unroll + rounds) as i:
        for h in range(unroll):
            body(lambda s: Step(unroll, i + (h - s) // unroll, (h - s) % unroll))
    for t in range(lo + unroll * rounds, total + depth - 1):
        peeled(t)


class Phase:

    def __init__(self, nc, name):
        self.nc, self.name, self.ctx, self.sems = nc, name, ExitStack(), []

    def sem(self, name):
        s = self.nc.alloc_semaphore(f"{self.name}_{name}")
        self.sems.append(s)
        return s

    def sem2(self, name, n=2):
        return [self.sem(f"{name}{h}") for h in range(n)]

    def sb(self, name, shape, dt=F32):
        return self.ctx.enter_context(self.nc.sbuf_tensor(f"{self.name}_{name}", shape, dt))

    def sb2(self, name, shape, dt=F32, n=2):
        return [self.sb(f"{name}{h}", shape, dt) for h in range(n)]

    def ps2(self, name, shape, n=2):
        return [self.ps(f"{name}{h}", shape) for h in range(n)]

    def ps(self, name, shape, dt=F32):
        return self.ctx.enter_context(self.nc.psum_tensor(f"{self.name}_{name}", shape, dt))

    def close(self):
        self.nc.clear_and_free_semaphores(self.sems)
        self.nc.all_engine_barrier()
        self.ctx.close()


def start(eng, sems, steps=U, counts=1):
    for q in sems:
        eng.sem_inc(q, steps * counts)


def start_dma(eng, *sets):
    for sems in sets:
        for q in sems:
            eng.sem_inc(q, 16)


def after(s, back=0):
    return s.k + (1 - back + s.u)


def after_tile(s, u, back=0):
    return s.k * UT + (UT - u + (s.u - back) * UT)


def arrived(s, transfers=1):
    return (s.i + 1) * (16 * transfers) + 16


def vacated(s, transfers=1):
    return s.i * (16 * transfers) + 16


def wait_all(eng, sems, steps, transfers=1):
    for h, q in enumerate(sems):
        eng.wait_ge(q, 16 + 16 * transfers * len(range(h, steps, len(sems))))


def landed(s, transfers):
    return (s.i + 1) * (16 * transfers)


def wait_indices_used(eng, gathered, s, transfers):
    if not isinstance(s.i, int) or s.i > 0:
        eng.wait_ge(gathered[s.h], s.i * (16 * transfers))


def slot(buffers, s):
    return buffers[s.h % len(buffers)]


def bc(ap, n):
    ap = ap.unsqueeze(len(ap.shape))
    return ap.to_broadcast(list(ap.shape[:-1]) + [n])


def mid(ap, n):
    ap = ap.unsqueeze(1)
    return ap.to_broadcast([ap.shape[0], n] + list(ap.shape[2:]))


def group_rows(table, s):
    start = s.k * GROUP
    return table[bass.ds(start, s.n), :].rearrange("(p j) d -> p j d", j=JN)


def load_constants(nc, c, w):
    ph = Phase(nc, "const")
    loaded, made, zeroed = ph.sem("loaded"), ph.sem("made"), ph.sem("zeroed")
    with nc.Block() as block:
        @block.sync
        def _(sp):
            def load(out, in_):
                sp.dma_start(out, in_).then_inc(loaded, 16)
                return 1
            sp.wait_ge(zeroed, 1)
            n = 0
            for a, name in enumerate(("src", "dst", "edge_type_8")):
                v = w[name]
                n += load(c.rows[:, a, 0:3, 1:], v[0:WHOLE * EDGES_T].rearrange("(c p f) -> p c f", p=P, f=EDGES_T))
                rest = v[WHOLE * EDGES_T:(WHOLE + REST) * EDGES_T]
                n += load(c.rows[0:REST, a, 3, 1:], rest.rearrange("(p f) -> p f", f=EDGES_T))
                n += load(c.rows[REST:REST + 1, a, 3, 1:LEFT + 1], v[EDGES - LEFT:EDGES].rearrange("(p f) -> p f", p=1))
            v = w["dst"]
            n += load(c.after[:, 0:3, :], v[1:WHOLE * EDGES_T + 1].rearrange("(c p f) -> p c f", p=P, f=EDGES_T))
            rest = v[WHOLE * EDGES_T + 1:(WHOLE + REST) * EDGES_T + 1]
            n += load(c.after[0:REST, 3, :], rest.rearrange("(p f) -> p f", f=EDGES_T))
            n += load(c.after[REST:REST + 1, 3, 0:LEFT - 1], v[EDGES - LEFT + 1:EDGES].rearrange("(p f) -> p f", p=1))
            n += load(c.w_emb[:, :], w["L0_gnn_W_emb"])
            n += load(c.b_emb[:, :], w["L0_gnn_b_emb"].partition_broadcast(P))
            for l in range(LAYERS):
                n += load(c.bases[:, l, :, :], w["L0_gnn_bases"][l].rearrange("b d f -> d b f"))
                n += load(c.loop[:, l, :], w["L0_gnn_self_loop"][l])
                n += load(c.coe[:, l, :], w["L0_gnn_w_coe"][l].rearrange("r b -> (r b)").partition_broadcast(P))
                for a, name in enumerate(("gamma", "beta", "mean", "var")):
                    n += load(c.bn[:, l, a, :], w["L0_gnn_bn_" + name][l].partition_broadcast(P))
            for a, name in enumerate(("Wq", "Wk", "Wv")):
                n += load(c.qkv[:, a * D:(a + 1) * D], w["L1_gnn_" + name])
            n += load(c.wo[:, :], w["L1_gnn_Wo"])
            n += load(c.w1[:, :], w["L1_gnn_W1"])
            n += load(c.w2[:, :, :], w["L1_gnn_W2"].rearrange("(a p) f -> p a f", p=P))
            for a in range(2):
                n += load(c.b1[:, a:a + 1], w["L1_gnn_b1"][a * P:(a + 1) * P].rearrange("(p a) -> p a", a=1))
            for a, name in enumerate(("bo", "b2", "g1", "be1", "g2", "be2")):
                n += load(c.col[:, a:a + 1], w["L1_gnn_" + name].rearrange("(p a) -> p a", a=1))
            for table, width in c.zero_rows:
                n += load(table[ZROW:ZROW + 1, :], c.zero[0:1, 0:width])
            sp.wait_ge(loaded, 16 * n)

        @block.gpsimd
        def _(pool):
            pool.memset(c.ident[:, :], 0.0).then_inc(made, 1)
            pool.memset(c.ones[:, :], 1.0).then_inc(made, 1)
            pool.memset(c.lower[:, :], 0.0).then_inc(made, 1)
            pool.wait_ge(made, 3)
            pool.affine_select(out=c.ident[:, :], in_=c.ident[:, :], compare_op=ALU.not_equal, fill=1.0,
                               base=0, pattern=[[-1, P]], channel_multiplier=1).then_inc(made, 1)
            pool.affine_select(out=c.lower[:, :], in_=c.lower[:, :], compare_op=ALU.is_ge, fill=1.0,
                               base=0, pattern=[[-1, P]], channel_multiplier=1).then_inc(made, 1)
            pool.iota(c.iota_i[:, :], pattern=[[1, COLS]], base=0, channel_multiplier=0).then_inc(made, 1)

        @block.vector
        def _(dve):
            nc.vector.memset(c.zero[:, :], 0.0)
            nc.vector.memset(c.norm[:, :], 1.0)
            nc.vector.memset(c.eps[:, 0:1], BN_EPS)
            nc.vector.memset(c.eps[:, 1:2], EPS)
            nc.vector.memset(c.ones16[:, :], 1.0)
            nc.vector.memset(c.shift16[:, :, :, :], 0.0)
            nc.vector.memset(c.after[:, :, :], PAD_DST)
            nc.vector.memset(c.rows[:, 0, :, :], 0)
            nc.vector.memset(c.rows[:, 2, :, :], 0)
            nc.vector.memset(c.rows[:, 1, :, :], PAD_DST).then_inc(zeroed, 1)
            dve.wait_ge(made, 6)
            nc.vector.tensor_copy(c.iota16[:, :], c.iota_i[:, :])
            nc.vector.tensor_copy(c.iota[:, :], c.iota_i[:, 0:TYPES])
            nc.vector.tensor_copy(c.iota1[:, :], c.iota_i[:, 1:TYPES + 1])
    ph.close()


def arrange_edges(nc, c):
    ph = Phase(nc, "arr")
    rf = ph.sb("rf", [P, 4, 4, P])
    falls, fall = ph.sb("falls", [P, 4, EDGES_T]), ph.sb("fall", [P, 1])
    pt, fall_ps = [ph.ps(f"pt{a}", [P, 4 * P]) for a in range(4)], ph.ps("fall_ps", [P, 1])
    high, mid16, rest = ph.sb("high", [P, D], BF16), ph.sb("mid16", [P, D], BF16), ph.sb("rest", [P, D])
    split, floats, turned, fell, fall_sum = (ph.sem(n) for n in ("split", "floats", "turned", "fell", "fall_sum"))
    roots, b1, b2, bn1, bn2 = (ph.sem(n) for n in ("roots", "w_scale", "w_shift", "w_var", "w_prod"))
    with nc.Block() as block:
        @block.vector
        def _(dve):
            nc.vector.tensor_copy(rf[:, 0:3, :, :], c.rows[:, :, :, :])
            nc.vector.tensor_copy(rf[:, 3, :, 1:], c.rows[:, 1, :, 1:])
            nc.vector.tensor_copy(rf[:, 3, :, 0:1], c.rows[:, 1, :, 1:2]).then_inc(floats, 1)
            nc.vector.tensor_tensor(falls[:, :, :], c.after[:, :, :], c.rows[:, 1, :, 1:], ALU.is_lt).then_inc(fell, 1)
            dve.wait_ge(fell, 1)
            nc.vector.tensor_reduce(fall[:, :], falls[:, :, :].rearrange("p c f -> p (c f)"), X, ALU.add)\
                .then_inc(fell, 1)
            dve.wait_ge(turned, 4)
            nc.vector.tensor_copy(c.src_i[:, :], pt[0][:, 0:TILES])
            nc.vector.tensor_copy(c.dst_f[:, :], pt[1][:, 0:TILES])
            nc.vector.tensor_copy(c.typ_f[:, :], pt[2][:, 0:TILES])
            nc.vector.tensor_copy(c.out_f[:, :], pt[3][:, 0:TILES])
            dve.wait_ge(fall_sum, 1)
            nc.vector.tensor_copy(c.unsorted[:, :], fall_ps[0:1, :])
            dve.wait_ge(roots, 1)
            for l in range(LAYERS):
                gamma, beta, mean, var = (c.bn[:, l, a, :] for a in range(4))
                nc.vector.reciprocal(var, var).then_inc(bn1, 1)
                dve.wait_ge(bn1, l + 1)
                nc.vector.tensor_tensor(gamma, gamma, var, ALU.mult).then_inc(b1, 1)
                dve.wait_ge(b1, l + 1)
                nc.vector.tensor_tensor(mean, mean, gamma, ALU.mult).then_inc(bn2, 1)
                dve.wait_ge(bn2, l + 1)
                nc.vector.tensor_tensor(beta, beta, mean, ALU.subtract).then_inc(b2, 1)
                dve.wait_ge(b2, l + 1)
                split_row(nc, dve, beta, c.shift16[:, l, :, :], high, mid16, rest, split, SPLITS * l)
                nc.vector.tensor_tensor(c.loop[:, l, :], c.loop[:, l, :], gamma, ALU.mult)
                nc.vector.tensor_tensor(c.bases[:, l, :, :], c.bases[:, l, :, :], mid(gamma, BASES), ALU.mult)

        @block.scalar
        def _(act):
            var = c.bn[:, :, 3, :]
            nc.scalar.activation(var, var, ACT.Sqrt, bias=c.eps[:, 0:1]).then_inc(roots, 1)

        @block.tensor
        def _(pe):
            pe.wait_ge(floats, 1)
            for a in range(4):
                for q in range(4):
                    last = nc.tensor.transpose(pt[a][:, q * P:(q + 1) * P], rf[:, a, q, :], c.ident[:, :])
                last.then_inc(turned, 1)
            pe.wait_ge(fell, 2)
            nc.tensor.matmul(fall_ps[:, :], c.ones[:, :], fall[:, :], start=True, stop=True).then_inc(fall_sum, 1)
    ph.close()


SPLITS = 7


def split_row(nc, dve, row, into, high, mid16, rest, split, done):
    nc.vector.tensor_copy(high[:, :], row).then_inc(split, 1)
    dve.wait_ge(split, done + 1)
    nc.vector.tensor_tensor(rest[:, :], row, high[:, :], ALU.subtract).then_inc(split, 1)
    nc.vector.tensor_copy(into[0:1, :, :], mid(high[0:1, :], JN)).then_inc(split, 1)
    dve.wait_ge(split, done + 2)
    nc.vector.tensor_copy(mid16[:, :], rest[:, :]).then_inc(split, 1)
    dve.wait_ge(split, done + 4)
    nc.vector.tensor_tensor(rest[:, :], rest[:, :], mid16[:, :], ALU.subtract).then_inc(split, 1)
    nc.vector.tensor_copy(into[32:33, :, :], mid(mid16[32:33, :], JN)).then_inc(split, 1)
    dve.wait_ge(split, done + 5)
    nc.vector.tensor_copy(into[64:65, :, :], mid(rest[64:65, :], JN)).then_inc(split, 1)


def sort_edges(nc, c, dst, scratch):
    PART = 6250
    PARTS = EDGES // PART
    SORTED = -(-EDGES // EDGES_T)
    ph = Phase(nc, "sort")
    keys_i, keys, number = ph.sb("keys_i", [P, PART], I32), ph.sb("keys", [P, PART]), ph.sb("number", [P, PART])
    number_i, edge_i, edge = ph.sb("number_i", [P, PART], I32), ph.sb("edge_i", [P, TILES], I32), ph.sb("edge", [P, TILES])
    lane_i, lane, pad = ph.sb("lane_i", [P, 1], I32), ph.sb("lane", [P, 1]), ph.sb("pad", [P, TILES])
    below, part_rank, rank = ph.sb("below", [P, PART]), ph.sb("part_rank", [P, TILES]), ph.sb("rank", [P, TILES])
    rank_i, packed, cols = ph.sb("rank_i", [P, TILES], I32), ph.sb("packed", [P, TILES, 3], I32), ph.sb("cols", [P, SORTED, 3], I32)
    rank1, packed1 = ph.sb("rank1", [P, 1], I32), ph.sb("packed1", [P, 3], I32)
    staged_free = ph.sem("staged_free")
    loaded, numbered, ready, compared, part_done, staged, scattered, reloaded = (
        ph.sem(n) for n in ("loaded", "numbered", "ready", "compared", "part_done", "staged", "scattered", "reloaded"))
    with nc.Block() as block:
        @block.sync
        def _(sp):
            with sp.If(sp.value_load(c.unsorted[0:1, 0:1], min_val=0, max_val=EDGES) > 0):
                for part in range(PARTS):
                    if part:
                        sp.wait_ge(part_done, part)
                    keys_in = dst[part * PART:(part + 1) * PART].partition_broadcast(P)
                    sp.dma_start(keys_i[:, :], keys_in).then_inc(loaded, 16)
                sp.wait_ge(scattered, TILES * 16)
                with sp.Fori(0, SORTED) as t:
                    edges = scratch[bass.ds(t * EDGES_T, EDGES_T), :]
                    sp.dma_start(cols[1:P, bass.ds(t, 1), :], edges.rearrange("(p t) a -> p t a", t=1))\
                        .then_inc(reloaded, 16)
                    first = scratch[bass.ds(t * EDGES_T, 1), :]
                    sp.dma_start(cols[0:1, bass.ds(t, 1), :], first.rearrange("(p t) a -> p t a", t=1))\
                        .then_inc(reloaded, 16)

        @block.gpsimd
        def _(pool):
            with pool.If(pool.value_load(c.unsorted[0:1, 0:1], min_val=0, max_val=EDGES) > 0):
                pool.iota(number_i[:, :], pattern=[[1, PART]], base=0, channel_multiplier=0).then_inc(numbered, 1)
                pool.iota(edge_i[:, :], pattern=[[EDGES_T, TILES]], base=-1, channel_multiplier=1).then_inc(numbered, 1)
                pool.iota(lane_i[:, :], pattern=[[0, 1]], base=0, channel_multiplier=1).then_inc(numbered, 1)
                with pool.Fori(0, TILES) as t:
                    pool.wait_ge(staged, t + 1)
                    pool.sem_inc(numbered, 1)
                    pool.indirect_dma_start(out=scratch, out_offset=bass.IndirectOffsetOnAxis(ap=rank1[:, 0:1], axis=0),
                                            in_=packed1[:, :], in_offset=None).then_inc(scattered, 16)
                    pool.wait_ge(scattered, t * 16 + 16)
                    pool.sem_inc(staged_free, 1)

        @block.vector
        def _(dve):
            links = [0]

            def chain(op):
                links[0] += 1
                op.then_inc(ready, 1)
                dve.wait_ge(ready, links[0])
            with dve.If(dve.value_load(c.unsorted[0:1, 0:1], min_val=0, max_val=EDGES) > 0):
                dve.wait_ge(numbered, 3)
                nc.vector.tensor_copy(edge[:, :], edge_i[:, :])
                nc.vector.tensor_copy(lane[:, :], lane_i[:, :])
                nc.vector.memset(rank[:, :], 0.0)
                dve.sem_inc(compared, 1)
                chain(nc.vector.tensor_copy(number[:, :], number_i[:, :]))
                for part in range(PARTS):
                    dve.wait_ge(loaded, 16 * (part + 1))
                    chain(nc.vector.tensor_copy(keys[:, :], keys_i[:, :]))
                    first = 4 * TILES * part
                    with dve.Fori(0, TILES) as t:
                        col = bass.ds(t, 1)
                        dve.wait_ge(compared, t * 4 + (first + 1))
                        nc.vector.tensor_scalar(below[:, :], number[:, :], edge[:, col], None, ALU.is_lt)\
                            .then_inc(compared, 1)
                        dve.wait_ge(compared, t * 4 + (first + 2))
                        nc.vector.scalar_tensor_tensor(below[:, :], keys[:, :], c.dst_f[:, col], below[:, :],
                                                       ALU.is_equal, ALU.mult).then_inc(compared, 1)
                        dve.wait_ge(compared, t * 4 + (first + 3))
                        nc.vector.scalar_tensor_tensor(below[:, :], keys[:, :], c.dst_f[:, col], below[:, :],
                                                       ALU.is_lt, ALU.add).then_inc(compared, 1)
                        dve.wait_ge(compared, t * 4 + (first + 4))
                        nc.vector.tensor_reduce(part_rank[:, col], below[:, :], X, ALU.add).then_inc(compared, 1)
                    dve.wait_ge(compared, 4 * TILES * (part + 1) + 1)
                    dve.sem_inc(part_done, 1)
                    chain(nc.vector.tensor_tensor(rank[:, :], rank[:, :], part_rank[:, :], ALU.add))
                    chain(nc.vector.tensor_scalar(number[:, :], number[:, :], float(PART), None, ALU.add))
                chain(nc.vector.tensor_scalar(pad[:, :], c.dst_f[:, :], float(PAD_DST), lane[:, 0:1], ALU.is_equal,
                                              ALU.mult))
                nc.vector.tensor_copy(packed[:, :, 0], c.src_i[:, :])
                nc.vector.tensor_copy(packed[:, :, 1], c.dst_f[:, :])
                nc.vector.tensor_copy(packed[:, :, 2], c.typ_f[:, :])
                chain(nc.vector.tensor_tensor(rank_i[:, :], rank[:, :], pad[:, :], ALU.add))
                start(dve, (staged_free,), 1)
                with dve.Fori(0, TILES) as t:
                    dve.wait_ge(staged_free, t + 1)
                    nc.vector.tensor_copy(rank1[:, :], rank_i[:, bass.ds(t, 1)])
                    nc.vector.tensor_copy(packed1[:, :], packed[:, bass.ds(t, 1), :].rearrange("p t a -> p (t a)"))\
                        .then_inc(staged, 1)
                dve.wait_ge(reloaded, SORTED * 32)
                nc.vector.tensor_copy(c.src_i[:, 0:SORTED], cols[:, :, 0])
                nc.vector.tensor_copy(c.typ_f[:, 0:SORTED], cols[:, :, 2])
                nc.vector.tensor_copy(c.out_f[:, 0:SORTED], cols[:, :, 1])
                chain(nc.vector.tensor_copy(c.dst_f[:, 0:SORTED], cols[:, :, 1]))
                nc.vector.memset(c.dst_f[0:1, :], float(PAD_DST))
    ph.close()


def place_edges(nc, c):
    ph = Phase(nc, "place")
    copied, ints, lows = ph.sem("copied"), ph.sem("ints"), ph.sem("lows")
    lo_i, hi_i, j_i, d_i = (ph.sb(n, [P, TILES], I32) for n in ("lo_i", "hi_i", "j_i", "d_i"))
    hi_f = ph.sb("hi_f", [P, TILES])
    with nc.Block() as block:
        @block.vector
        def _(dve):
            nc.vector.tensor_copy(c.in_f[:, :], c.out_f[:, :]).then_inc(copied, 1)
            nc.vector.tensor_copy(d_i[:, :], c.dst_f[:, :]).then_inc(ints, 1)
            dve.wait_ge(copied, 1)
            nc.vector.memset(c.in_f[0:1, TILES - 1:TILES], -1.0)
            nc.vector.tensor_copy(c.in_f[0:1, 0:TILES - 1], c.out_f[0:1, 1:TILES])
            nc.vector.tensor_scalar(c.dst_i[:, :], c.dst_f[:, :], float(NODES - 1), None, ALU.min)
            dve.wait_ge(ints, 1)
            nc.vector.tensor_scalar(lo_i[:, :], d_i[:, :], 2, P - 1, ALU.logical_shift_right, ALU.bitwise_and).then_inc(lows, 1)
            nc.vector.tensor_scalar(hi_i[:, :], d_i[:, :], 9, 2, ALU.logical_shift_right, ALU.logical_shift_left).then_inc(lows, 1)
            nc.vector.tensor_scalar(j_i[:, :], d_i[:, :], JN - 1, None, ALU.bitwise_and).then_inc(lows, 1)
            dve.wait_ge(lows, 3)
            nc.vector.tensor_copy(c.place_p[:, :], lo_i[:, :])
            nc.vector.tensor_copy(hi_f[:, :], hi_i[:, :]).then_inc(lows, 1)
            dve.wait_ge(lows, 4)
            nc.vector.tensor_tensor(c.place_f[:, :], hi_f[:, :], j_i[:, :], ALU.add)
    ph.close()


def embed_nodes(nc, c, x, h0):
    ph = Phase(nc, "emb")
    xt, xT, hs = (ph.sb2(n, [P, GROUP], n=U) for n in ("xt", "xT", "hs"))
    xt, hs = ([b[:, :].rearrange("p (j d) -> p j d", j=JN) for b in x4] for x4 in (xt, hs))
    hot_p, hot_f = ph.sb2("hot_p", [P, UT, P], F16, U), ph.sb2("hot_f", [P, UT, COLS], F16, U)
    zero16 = ph.sb("zero16", [P, P], F16)
    xT_ps = [ph.ps(f"xT_ps{h}", [P, GROUP]) for h in range(2)]
    h_ps = [ph.ps(f"h_ps{h}", [P, JN, D]) for h in range(2)]
    hist = ph.ps("hist", [P, COLS])
    more = Step(U, GROUPS // U, GROUPS % U)
    x_in, h_out = ph.sem2("x_in", U), ph.sem2("h_out", U)
    turned, copied, mul, biased = ph.sem("turned"), ph.sem("copied"), ph.sem("mul"), ph.sem("biased")
    hot, binned, zeroed, counted = ph.sem("hot"), ph.sem("binned"), ph.sem("zeroed"), ph.sem("counted")
    with nc.Block() as block:
        @block.sync
        def _(sp):
            start_dma(sp, x_in, h_out)

            def body(at):
                if s := at(0):
                    sp.wait_ge(turned, after(s, U))
                    sp.dma_start(xt[s.h][0:s.p, 0:JN, :], group_rows(x, s)).then_inc(x_in[s.h], 16)
                if s := at(4):
                    sp.wait_ge(biased, after(s))
                    sp.dma_start(group_rows(h0, s), hs[s.h][0:s.p, 0:JN, :]).then_inc(h_out[s.h], 16)
            timeline(sp, FULL, True, 5, body)
            wait_all(sp, h_out, GROUPS)

        @block.tensor
        def _(pe):
            start(pe, (turned, mul, binned))
            pe.wait_ge(zeroed, 1)
            nc.tensor.matmul(hist[:, :], zero16[:, :], c.iota16[:, :], start=True, stop=False)

            def bin_targets(s):
                pe.wait_ge(hot, after(s))
                for u in range(UT):
                    last = nc.tensor.matmul(hist[:, :], hot_p[s.h][:, u, :], hot_f[s.h][:, u, :],
                                            start=False, stop=False)
                last.then_inc(binned, 1)

            def body(at):
                if s := at(0):
                    pe.wait_ge(x_in[s.h], arrived(s))
                    pe.wait_ge(copied, after(s, 2))
                    for j in range(JN):
                        last = nc.tensor.transpose(xT_ps[s.h % 2][:, j * s.p:(j + 1) * s.p], xt[s.h][0:s.p, j, :],
                                                   c.ident[0:s.p, 0:s.p])
                    last.then_inc(turned, 1)
                if s := at(1):
                    pe.wait_ge(copied, after(s))
                    pe.wait_ge(biased, after(s, 2))
                    for j in range(JN):
                        last = nc.tensor.matmul(h_ps[s.h % 2][0:s.p, j, :], xT[s.h][:, j * s.p:(j + 1) * s.p],
                                                c.w_emb[:, :], start=True, stop=True)
                    last.then_inc(mul, 1)
                    bin_targets(s)
            timeline(pe, FULL, True, 2, body)
            bin_targets(more)
            nc.tensor.matmul(hist[:, :], zero16[:, :], c.iota16[:, :], start=False, stop=True).then_inc(counted, 1)

        @block.scalar
        def _(act):
            start(act, (copied,))

            def body(at):
                if s := at(0):
                    act.wait_ge(turned, after(s))
                    act.wait_ge(mul, after(s, 2))
                    nc.scalar.copy(xT[s.h][:, 0:s.n], xT_ps[s.h % 2][:, 0:s.n]).then_inc(copied, 1)
            timeline(act, FULL, True, 1, body)

        @block.vector
        def _(dve):
            start(dve, (biased, hot))
            nc.vector.memset(zero16[:, :], 0.0).then_inc(zeroed, 1)

            def place_targets(s):
                dve.wait_ge(binned, after(s, U))
                for u in range(UT):
                    t = s.k * UT + u
                    nc.vector.tensor_scalar(hot_p[s.h][:, u, :], c.iota16[:, 0:P],
                                            c.place_p[:, bass.ds(t, 1)], None, ALU.is_equal)
                    last = nc.vector.tensor_scalar(hot_f[s.h][:, u, :], c.iota16[:, :],
                                                   c.place_f[:, bass.ds(t, 1)], None, ALU.is_equal)
                last.then_inc(hot, 1)

            def body(at):
                if s := at(0):
                    place_targets(s)
                if s := at(2):
                    dve.wait_ge(mul, after(s))
                    dve.wait_ge(h_out[s.h], vacated(s))
                    nc.vector.tensor_tensor(hs[s.h][0:s.p, 0:JN, :], h_ps[s.h % 2][0:s.p, 0:JN, :],
                                            mid(c.b_emb[0:s.p, :], JN), ALU.add).then_inc(biased, 1)
            timeline(dve, FULL, True, 3, body)
            place_targets(more)
            dve.wait_ge(counted, 1)
            nc.vector.tensor_copy(c.count[:, :], hist[:, :])
    ph.close()


def index_nodes(nc, c):
    ph = Phase(nc, "idx")
    rows = ph.sb("rows", [P, GROUPS])
    totals = ph.sb("totals", [GROUPS, P])
    base = ph.sb("base", [P, GROUPS])
    first, some, tile, off = (ph.sb(n, [P, GROUPS, JN]) for n in ("first", "some", "tile", "off"))
    ps_t, ps_b, ps_g = ph.ps("ps_t", [GROUPS, P]), ph.ps("ps_b", [P, GROUPS]), ph.ps("ps_g", [P, GROUPS])
    summed, products, link = ph.sem("summed"), ph.sem("products"), ph.sem("link")
    count = c.count[:, :].rearrange("p (g j) -> p g j", j=JN)
    with nc.Block() as block:
        @block.tensor
        def _(pe):
            pe.wait_ge(summed, 1)
            nc.tensor.matmul(ps_t[:, :], rows[:, :], c.ones[:, :], start=True, stop=True).then_inc(products, 1)
            nc.tensor.matmul(ps_b[:, :], c.lower[:, :], rows[:, :], start=True, stop=True).then_inc(products, 1)
            pe.wait_ge(summed, 2)
            nc.tensor.matmul(ps_g[:, :], totals[:, :], c.lower[0:GROUPS, 0:GROUPS], start=True, stop=True)\
              .then_inc(products, 1)

        @block.vector
        def _(dve):
            links = [0]

            def chain(op):
                links[0] += 1
                op.then_inc(link, 1)
                dve.wait_ge(link, links[0])
            nc.vector.tensor_reduce(rows[:, :], count, X, ALU.add).then_inc(summed, 1)
            dve.wait_ge(products, 1)
            nc.vector.tensor_copy(totals[:, :], ps_t[:, :]).then_inc(summed, 1)
            dve.wait_ge(products, 2)
            chain(nc.vector.tensor_copy(base[:, :], ps_b[:, :]))
            dve.wait_ge(products, 3)
            chain(nc.vector.tensor_tensor(first[:, :, 0], base[:, :], ps_g[:, :], ALU.add))
            for j in range(1, JN):
                chain(nc.vector.tensor_tensor(first[:, :, j], first[:, :, j - 1], count[:, :, j - 1], ALU.add))
            chain(nc.vector.tensor_scalar(some[:, :, :], count, 0.0, None, ALU.is_gt))
            chain(nc.vector.tensor_scalar(tile[:, :, :], first[:, :, :], 0.5, 1.0 / EDGES_T, ALU.add, ALU.mult))
            chain(nc.vector.tensor_scalar(tile[:, :, :], tile[:, :, :], -0.5, 2.0 ** 23, ALU.add, ALU.add))
            chain(nc.vector.tensor_scalar(tile[:, :, :], tile[:, :, :], -2.0 ** 23, None, ALU.add))
            chain(nc.vector.tensor_tensor(first[:, :, :], first[:, :, :], tile[:, :, :], ALU.add))
            chain(nc.vector.tensor_scalar(off[:, :, :], first[:, :, :], 1.0 - ZROW, None, ALU.add))
            chain(nc.vector.tensor_tensor(off[:, :, :], off[:, :, :], some[:, :, :], ALU.mult))
            nc.vector.tensor_scalar(c.start_i[:, :].rearrange("p (g j) -> p g j", j=JN), off[:, :, :], float(ZROW),
                                    None, ALU.add)
    ph.close()


def tile_columns(s):
    return (STEPS - 1 - s.k) * UT if isinstance(s.k, int) else (STEPS - 1) * UT - s.k * UT


def tile_rows(table, s):
    return table[bass.ds(tile_columns(s) * P, UT * P), :].rearrange("(u p) d -> p u d", p=P)


UP = tuple(range(UT - 1, -1, -1))
PLACE = (0, 2, 1, 3)


def conv_edges(nc, c, layer, nodes, table, width):
    ph = Phase(nc, f"conv{layer}")
    src4, out4, in4 = ph.sb2("src4", [P, UT], I32, U), ph.sb2("out4", [P, UT], n=U), ph.sb2("in4", [P, UT], n=U)
    hot, coe = ph.sb2("hot", [P, UT, TYPES], n=U), ph.sb2("coe", [P, UT, BASES], n=U)
    prod = ph.sb("prod", [P, UT, BASES, TYPES])
    xg, xT = ph.sb2("xg", [P, UT, D], n=U), ph.sb2("xT", [P, UT, P])
    same = ph.sb2("same", [P, UT, P], n=U)
    val, out = ph.sb2("val", [P, UT, width]), ph.sb2("out", [P, UT, width], n=U)
    part = ph.sb("part", [P, UT, BASES - 1, D])
    dst_ps, xT_ps = ph.ps("dst_ps", [P, UT, P]), ph.ps("xT_ps", [P, UT, P])
    mul_ps = [ph.ps(f"mul_ps{u}", [P, BASES, D]) for u in range(UT)]
    sum_ps = ph.ps("sum_ps", [P, UT, 256])
    gathered, stored, pace, pace_out = ph.sem2("gathered", U), ph.sem2("stored", U), ph.sem("pace"), ph.sem("pace_out")
    src_set, dst_set, hot_set, prod_set, coe_set = (
        ph.sem(n) for n in ("src_set", "dst_set", "hot_set", "prod_set", "coe_set"))
    dst_turned, x_turned, xT_set, same_set = (ph.sem(n) for n in ("dst_turned", "x_turned", "xT_set", "same_set"))
    mul, scaled, added, val_set, carried, summed, out_set = (
        ph.sem(n) for n in ("mul", "scaled", "added", "val_set", "carried", "summed", "out_set"))
    with nc.Block() as block:
        @block.gpsimd
        def _(pool):
            def body(at):
                if s := at(0):
                    pool.wait_ge(x_turned, after(s, U))
                    pool.wait_ge(src_set, after(s))
                    pool.sem_inc(pace, 1)
                    for u in UP:
                        pool.indirect_dma_start(out=xg[s.h][:, u, :], out_offset=None, in_=nodes,
                                                in_offset=bass.IndirectOffsetOnAxis(ap=src4[s.h][:, u:u + 1], axis=0))\
                            .then_inc(gathered[s.h], 16)
            timeline(pool, STEPS, False, 1, body)

        @block.vector
        def _(dve):
            start(dve, (src_set, dst_set, hot_set, prod_set, coe_set, same_set))
            start(dve, (val_set,), counts=UT)

            def combine(s, pair, n):
                for b in range(1, BASES):
                    for u in pair:
                        if b == 1:
                            dve.wait_ge(scaled, after_tile(s, u))
                        else:
                            n += 1
                            dve.wait_ge(added, s.k * (2 * UT) + n)
                        into = slot(val, s)[:, u, 0:D] if b == BASES - 1 else part[:, u, b, :]
                        nc.vector.scalar_tensor_tensor(into, mul_ps[u][:, b, :], coe[s.h][:, u, b:b + 1],
                                                       part[:, u, b - 1, :], ALU.mult, ALU.add)\
                            .then_inc(val_set if b == BASES - 1 else added, 1)

            def body(at):
                if s := at(0):
                    wait_indices_used(dve, gathered, s, UT)
                    nc.vector.tensor_copy(src4[s.h][:, :], c.src_i[:, bass.ds(tile_columns(s), UT)]).then_inc(src_set, 1)
                if s := at(1):
                    t = bass.ds(tile_columns(s), UT)
                    dve.wait_ge(dst_turned, after(s, U))
                    nc.vector.tensor_copy(in4[s.h][:, :], c.in_f[:, t])
                    nc.vector.tensor_copy(out4[s.h][:, :], c.out_f[:, t]).then_inc(dst_set, 1)
                    nc.vector.tensor_tensor(hot[s.h][:, :, :], bc(c.typ_f[:, t], TYPES), mid(c.iota[:, :], UT),
                                            ALU.is_equal).then_inc(hot_set, 1)
                    w = c.coe[:, layer, :].rearrange("p (r b) -> p b r", b=BASES)
                    dve.wait_ge(hot_set, after(s))
                    for u in range(UT):
                        last = nc.vector.tensor_tensor(prod[:, u, :, :], mid(hot[s.h][:, u, :], BASES), w, ALU.mult)
                    last.then_inc(prod_set, 1)
                    dve.wait_ge(scaled, after_tile(s, 0, U))
                    dve.wait_ge(prod_set, after(s))
                    nc.vector.tensor_reduce(coe[s.h][:, :, :], prod[:, :, :, :], X, ALU.add).then_inc(coe_set, 1)
                if s := at(3):
                    dve.wait_ge(summed, after_tile(s, 0, 2))
                    if width > D:
                        nc.vector.tensor_copy(slot(val, s)[:, :, D:], hot[s.h][:, :, :])
                    combine(s, UP[0:2], 0)
                if s := at(2):
                    compare_targets(nc, dve, s, dst_ps, in4, same, summed, dst_turned, same_set)
                if s := at(3):
                    combine(s, UP[2:4], UT)
            timeline(dve, STEPS, False, 4, body)

        @block.scalar
        def _(act):
            start(act, (xT_set,))
            start(act, (scaled, carried, out_set), counts=UT)

            def body(at):
                for u in UP:
                    if s := at(3):
                        carry_on(nc, act, s, u, val, out, sum_ps, width, val_set, summed, stored, carried, out_set)
                    if s := at(2):
                        if u == UP[0]:
                            act.wait_ge(coe_set, after(s))
                        act.wait_ge(val_set, after_tile(s, u, 1))
                        act.wait_ge(mul, after_tile(s, u))
                        nc.scalar.activation(part[:, u, 0, :], mul_ps[u][:, 0, :], ACT.Copy, scale=coe[s.h][:, u, 0:1])\
                            .then_inc(scaled, 1)
                    if u == UP[1]:
                        if s := at(1):
                            act.wait_ge(mul, after_tile(s, 0, 2))
                            act.wait_ge(x_turned, after(s))
                            nc.scalar.copy(slot(xT, s)[:, :, :], xT_ps[:, :, :]).then_inc(xT_set, 1)
            timeline(act, STEPS, False, 4, body)
            copy_last(nc, act, out, sum_ps, width, summed, out_set)

        @block.tensor
        def _(pe):
            start(pe, (dst_turned, x_turned))
            start(pe, (mul, summed), counts=UT)
            basis = c.bases[:, layer, :, :].rearrange("p b d -> p (b d)")

            def body(at):
                for u in UP:
                    if s := at(2):
                        if u == UP[0]:
                            pe.wait_ge(xT_set, after(s))
                        pe.wait_ge(val_set, after_tile(s, u, 1))
                        nc.tensor.matmul(mul_ps[u][:, :, :].rearrange("p b d -> p (b d)"), slot(xT, s)[:, u, :], basis,
                                         start=True, stop=True).then_inc(mul, 1)
                    if s := at(3):
                        sum_tile(nc, pe, s, u, same, val, sum_ps, width, same_set, carried, out_set, summed)
                    if u == UP[1]:
                        if s := at(1):
                            turn_targets(nc, c, pe, s, out4, dst_set, dst_ps, same_set, dst_turned)
                            pe.wait_ge(xT_set, after(s, 1))
                            pe.wait_ge(gathered[s.h], landed(s, UT))
                            for v in UP:
                                last = nc.tensor.transpose(xT_ps[:, v, :], xg[s.h][:, v, :], c.ident[:, :])
                            last.then_inc(x_turned, 1)
            timeline(pe, STEPS, False, 4, body)

        @block.sync
        def _(sp):
            store_sums(sp, table, out, out_set, stored, pace_out)
    ph.close()


def turn_targets(nc, c, pe, s, out4, dst_set, dst_ps, same_set, dst_turned):
    pe.wait_ge(same_set, after(s, 1))
    pe.wait_ge(dst_set, after(s))
    for u in UP:
        last = nc.tensor.transpose(dst_ps[:, u, :], out4[s.h][:, u:u + 1].to_broadcast([P, P]), c.ident[:, :])
    last.then_inc(dst_turned, 1)


def compare_targets(nc, dve, s, dst_ps, in4, same, summed, dst_turned, same_set):
    dve.wait_ge(summed, after_tile(s, 0, U))
    dve.wait_ge(dst_turned, after(s))
    nc.vector.tensor_tensor(same[s.h][:, :, :], dst_ps[:, :, :], bc(in4[s.h][:, :], P), ALU.is_equal)\
        .then_inc(same_set, 1)


def sum_tile(nc, pe, s, u, same, val, sum_ps, width, same_set, carried, out_set, summed):
    if u == UP[0]:
        pe.wait_ge(same_set, after(s))
    pe.wait_ge(carried, after_tile(s, u))
    pe.wait_ge(out_set, after_tile(s, u) - 2)
    nc.tensor.matmul(sum_ps[:, PLACE[u], 0:width], same[s.h][:, u, :], slot(val, s)[:, u, :], start=True, stop=True)\
        .then_inc(summed, 1)


def carry_on(nc, act, s, u, val, out, sum_ps, width, val_set, summed, stored, carried, out_set):
    act.wait_ge(val_set, after_tile(s, u))
    if isinstance(s.k, int) and s.k == 0 and u == UP[0]:
        act.sem_inc(carried, 1)
        return
    v, rows = (0, out[(s.h - 1) % U]) if u == UP[0] else (u + 1, out[s.h])
    act.wait_ge(summed, after_tile(s, u) - 1)
    nc.scalar.copy(slot(val, s)[0:1, u, :], sum_ps[0:1, PLACE[v], 0:width]).then_inc(carried, 1)
    if u == UP[1]:
        act.wait_ge(stored[s.h], vacated(s))
    nc.scalar.copy(rows[:, v, :], sum_ps[:, PLACE[v], 0:width]).then_inc(out_set, 1)


def copy_last(nc, act, out, sum_ps, width, summed, out_set):
    act.wait_ge(summed, (U + STEPS) * UT)
    nc.scalar.copy(out[(STEPS - 1) % U][:, 0, :], sum_ps[:, PLACE[0], 0:width]).then_inc(out_set, 1)


def store_sums(sp, table, out, out_set, stored, pace_out):
    start_dma(sp, stored)

    def body(at):
        if s := at(0):
            sp.wait_ge(out_set, after_tile(s, 0))
            sp.sem_inc(pace_out, 1)
            sp.dma_start(tile_rows(table, s), out[s.h][:, :, :]).then_inc(stored[s.h], 16)
    timeline(sp, STEPS, False, 1, body)
    wait_all(sp, stored, STEPS)


def attend_edges(nc, c, q, x1, table):
    ph = Phase(nc, "att")
    src4, dsti4 = ph.sb2("src4", [P, UT], I32, U), ph.sb2("dsti4", [P, UT], I32, U)
    out4, in4 = ph.sb2("out4", [P, UT], n=U), ph.sb2("in4", [P, UT], n=U)
    qg, xg, xT = ph.sb2("qg", [P, UT, D], n=U), ph.sb2("xg", [P, UT, D], n=U), ph.sb2("xT", [P, UT, P])
    qk, score = ph.sb("qk", [P, UT, D]), ph.sb2("score", [P, UT, HEADS])
    same = ph.sb2("same", [P, UT, P], n=U)
    val, out = ph.sb2("val", [P, UT, CNT]), ph.sb2("out", [P, UT, CNT], n=U)
    dst_ps, xT_ps, sum_ps = ph.ps("dst_ps", [P, UT, P]), ph.ps("xT_ps", [P, UT, P]), ph.ps("sum_ps", [P, UT, 256])
    kv_ps = ph.ps2("kv_ps", [P, UT, 2 * D])
    gathered, stored, pace, pace_out = ph.sem2("gathered", U), ph.sem2("stored", U), ph.sem("pace"), ph.sem("pace_out")
    idx_set, dst_set, dst_turned, same_set, x_turned, xT_set, kv_set = (
        ph.sem(n) for n in ("idx_set", "dst_set", "dst_turned", "same_set", "x_turned", "xT_set", "kv_set"))
    qk_set, dots_set, score_set, low_set, exp_set, val_set = (
        ph.sem(n) for n in ("qk_set", "dots_set", "score_set", "low_set", "exp_set", "val_set"))
    carried, summed, out_set = ph.sem("carried"), ph.sem("summed"), ph.sem("out_set")
    loads = 2 * UT
    with nc.Block() as block:
        @block.gpsimd
        def _(pool):
            def body(at):
                if s := at(0):
                    pool.wait_ge(qk_set, after(s, U))
                    pool.wait_ge(idx_set, after(s))
                    pool.sem_inc(pace, 1)
                    for u in UP:
                        for into, rows, idx in ((qg, q, dsti4), (xg, x1, src4)):
                            pool.indirect_dma_start(out=into[s.h][:, u, :], out_offset=None, in_=rows,
                                                    in_offset=bass.IndirectOffsetOnAxis(ap=idx[s.h][:, u:u + 1], axis=0))\
                                .then_inc(gathered[s.h], 16)
            timeline(pool, STEPS, False, 1, body)

        @block.vector
        def _(dve):
            start(dve, (idx_set, dst_set, same_set, qk_set, dots_set, score_set, low_set))
            start(dve, (val_set,), counts=UT)

            def body(at):
                if s := at(0):
                    t = bass.ds(tile_columns(s), UT)
                    wait_indices_used(dve, gathered, s, loads)
                    nc.vector.tensor_copy(src4[s.h][:, :], c.src_i[:, t])
                    nc.vector.tensor_copy(dsti4[s.h][:, :], c.dst_i[:, t]).then_inc(idx_set, 1)
                if s := at(1):
                    t = bass.ds(tile_columns(s), UT)
                    dve.wait_ge(dst_turned, after(s, U))
                    nc.vector.tensor_copy(in4[s.h][:, :], c.in_f[:, t])
                    nc.vector.tensor_copy(out4[s.h][:, :], c.out_f[:, t]).then_inc(dst_set, 1)
                if s := at(2):
                    dve.wait_ge(kv_set, after(s))
                    nc.vector.tensor_tensor(qk[:, :, :], qg[s.h][:, :, :], slot(kv_ps, s)[:, :, 0:D], ALU.mult)\
                        .then_inc(qk_set, 1)
                    dve.wait_ge(qk_set, after(s))
                    nc.vector.tensor_reduce(slot(score, s)[:, :, :], qk[:, :, :].rearrange("p u (h e) -> p u h e", e=HD),
                                            X, ALU.add).then_inc(dots_set, 1)
                    dve.wait_ge(dots_set, after(s))
                    nc.vector.tensor_scalar(slot(score, s)[:, :, :], slot(score, s)[:, :, :], 1.0 / HD ** 0.5, 5.0,
                                            ALU.mult, ALU.min).then_inc(low_set, 1)
                    dve.wait_ge(low_set, after(s))
                    nc.vector.tensor_scalar(slot(score, s)[:, :, :], slot(score, s)[:, :, :], -5.0, None, ALU.max)\
                        .then_inc(score_set, 1)
                if s := at(1):
                    compare_targets(nc, dve, s, dst_ps, in4, same, summed, dst_turned, same_set)
                if s := at(2):
                    dve.wait_ge(exp_set, after(s))
                    for u in UP:
                        nc.vector.tensor_tensor(slot(val, s)[:, u, 0:D].rearrange("p (h e) -> p h e", e=HD),
                                                slot(kv_ps, s)[:, u, D:].rearrange("p (h e) -> p h e", e=HD),
                                                bc(slot(val, s)[:, u, D:], HD), ALU.mult).then_inc(val_set, 1)
            timeline(dve, STEPS, False, 3, body)

        @block.scalar
        def _(act):
            start(act, (exp_set, xT_set))
            start(act, (carried, out_set), counts=UT)

            def body(at):
                for u in UP:
                    if s := at(3):
                        carry_on(nc, act, s, u, val, out, sum_ps, CNT, val_set, summed, stored, carried, out_set)
                    if u == UP[1]:
                        if s := at(2):
                            act.wait_ge(summed, after_tile(s, 0, 2))
                            act.wait_ge(score_set, after(s))
                            nc.scalar.activation(slot(val, s)[:, :, D:], slot(score, s)[:, :, :], ACT.Exp)\
                                .then_inc(exp_set, 1)
                    if u == UP[2]:
                        if s := at(0):
                            act.wait_ge(kv_set, after(s, 2))
                            act.wait_ge(x_turned, after(s))
                            nc.scalar.copy(slot(xT, s)[:, :, :], xT_ps[:, :, :]).then_inc(xT_set, 1)
            timeline(act, STEPS, False, 4, body)
            copy_last(nc, act, out, sum_ps, CNT, summed, out_set)

        @block.tensor
        def _(pe):
            start(pe, (dst_turned, x_turned, kv_set))
            start(pe, (summed,), counts=UT)

            def body(at):
                for u in UP:
                    if s := at(3):
                        sum_tile(nc, pe, s, u, same, val, sum_ps, CNT, same_set, carried, out_set, summed)
                    if s := at(1):
                        if u == UP[0]:
                            pe.wait_ge(xT_set, after(s))
                            pe.wait_ge(val_set, after_tile(s, 0, 2))
                        kv = nc.tensor.matmul(slot(kv_ps, s)[:, u, :], slot(xT, s)[:, u, :], c.qkv[:, D:],
                                              start=True, stop=True)
                        if u == UP[-1]:
                            kv.then_inc(kv_set, 1)
                    if s := at(0):
                        if u == UP[1]:
                            turn_targets(nc, c, pe, s, out4, dst_set, dst_ps, same_set, dst_turned)
                        if u == UP[2]:
                            pe.wait_ge(xT_set, after(s, 1))
                            pe.wait_ge(gathered[s.h], landed(s, loads))
                            for v in UP:
                                last = nc.tensor.transpose(xT_ps[:, v, :], xg[s.h][:, v, :], c.ident[:, :])
                            last.then_inc(x_turned, 1)
            timeline(pe, STEPS, False, 4, body)

        @block.sync
        def _(sp):
            store_sums(sp, table, out, out_set, stored, pace_out)
    ph.close()


def gather_groups(nc, c, pool, table, into, idx4, idx_set, used, gathered, pace):
    def body(at):
        if s := at(0):
            pool.wait_ge(used, after(s, U))
            pool.wait_ge(idx_set, after(s))
            pool.sem_inc(pace, 1)
            for j in range(JN):
                pool.indirect_dma_start(out=into[s.h][0:s.p, j, :], out_offset=None, in_=table,
                                        in_offset=bass.IndirectOffsetOnAxis(ap=idx4[s.h][0:s.p, j:j + 1], axis=0))\
                    .then_inc(gathered[s.h], 16)
    timeline(pool, FULL, True, 1, body)


def turn(nc, c, ps, rows, s):
    for j in range(JN):
        last = nc.tensor.transpose(ps[:, j * s.p:(j + 1) * s.p], rows[0:s.p, j, :], c.ident[0:s.p, 0:s.p])
    return last


def multiply_rows(nc, c, layer, ps, hT, s):
    nc.tensor.matmul(ps[0:s.p, :, :], c.ones16[:, 0:s.p], c.shift16[:, layer, :, :], start=True, stop=False)
    for j in range(JN):
        last = nc.tensor.matmul(ps[0:s.p, j, :], hT[:, j * s.p:(j + 1) * s.p], c.loop[:, layer, :], start=False,
                                stop=j == JN - 1)
    return last


def update_nodes(nc, c, h_in, table, h_out):
    ph = Phase(nc, "node0")
    idx4 = ph.sb2("idx4", [P, JN], I32, U)
    ag, ht, hs, z = (ph.sb2("ag", [P, JN, CNT], n=U), ph.sb2("ht", [P, JN, D], n=U), ph.sb2("hs", [P, JN, D], n=U),
                     ph.sb2("z", [P, JN, D], n=U))
    hT = ph.sb2("hT", [P, GROUP])
    rank, top = ph.sb("rank", [P, JN, TYPES]), ph.sb("top", [P, JN])
    hT_ps, mul_ps = ph.ps2("hT_ps", [P, GROUP]), ph.ps2("mul_ps", [P, JN, D], 4)
    h_in_s, gathered, stored = ph.sem2("h_in", U), ph.sem2("gathered", U), ph.sem2("stored", U)
    pace, idx_set, turned, copied, mul = (ph.sem(n) for n in ("pace", "idx_set", "turned", "copied", "mul"))
    norm_step, scaled, rectified = (ph.sem(n) for n in ("norm_step", "scaled", "rectified"))
    LINKS = 8
    with nc.Block() as block:
        @block.gpsimd
        def _(pool):
            gather_groups(nc, c, pool, table, ag, idx4, idx_set, scaled, gathered, pace)

        @block.sync
        def _(sp):
            start_dma(sp, h_in_s, stored)

            def body(at):
                if s := at(0):
                    sp.wait_ge(turned, after(s, U))
                    sp.dma_start(ht[s.h][0:s.p, :, :], group_rows(h_in, s)).then_inc(h_in_s[s.h], 16)
                if s := at(5):
                    sp.wait_ge(rectified, after(s))
                    sp.dma_start(group_rows(h_out, s), hs[s.h][0:s.p, :, :]).then_inc(stored[s.h], 16)
            timeline(sp, FULL, True, 6, body)
            wait_all(sp, stored, GROUPS)

        @block.tensor
        def _(pe):
            start(pe, (turned, mul))

            def body(at):
                if s := at(0):
                    pe.wait_ge(h_in_s[s.h], arrived(s))
                    pe.wait_ge(copied, after(s, 2))
                    turn(nc, c, slot(hT_ps, s), ht[s.h], s).then_inc(turned, 1)
                if s := at(1):
                    pe.wait_ge(copied, after(s))
                    pe.wait_ge(scaled, after(s, 4))
                    multiply_rows(nc, c, 0, mul_ps[s.h], slot(hT, s), s).then_inc(mul, 1)
            timeline(pe, FULL, True, 2, body)

        @block.scalar
        def _(act):
            start(act, (copied, rectified))

            def body(at):
                if s := at(0):
                    act.wait_ge(mul, after(s, 2))
                    act.wait_ge(turned, after(s))
                    nc.scalar.copy(slot(hT, s)[:, 0:s.n], slot(hT_ps, s)[:, 0:s.n]).then_inc(copied, 1)
                if s := at(3):
                    act.wait_ge(stored[s.h], vacated(s))
                    act.wait_ge(scaled, after(s))
                    nc.scalar.activation(hs[s.h][0:s.p, :, :], z[s.h][0:s.p, :, :], ACT.Relu).then_inc(rectified, 1)
            timeline(act, FULL, True, 4, body)

        @block.vector
        def _(dve):
            start(dve, (idx_set, scaled))

            def body(at):
                if s := at(0):
                    wait_indices_used(dve, gathered, s, JN)
                    nc.vector.tensor_copy(idx4[s.h][:, :], c.start_i[:, bass.ds(s.k * JN, JN)]).then_inc(idx_set, 1)
                if s := at(2):
                    p, n = s.p, 0
                    counts = ag[s.h][0:p, :, D:]
                    steps = [
                        lambda: nc.vector.tensor_scalar(rank[0:p, :, :], counts, 0.0, None, ALU.is_gt),
                        lambda: nc.vector.tensor_tensor(rank[0:p, :, :], rank[0:p, :, :], mid(c.iota1[0:p, :], JN), ALU.mult),
                        lambda: nc.vector.tensor_reduce(top[0:p, :], rank[0:p, :, :], X, ALU.max),
                        lambda: nc.vector.tensor_tensor(rank[0:p, :, :], rank[0:p, :, :], bc(top[0:p, :], TYPES), ALU.is_equal),
                        lambda: nc.vector.tensor_tensor(rank[0:p, :, :], rank[0:p, :, :], counts, ALU.mult),
                        lambda: nc.vector.tensor_reduce(top[0:p, :], rank[0:p, :, :], X, ALU.add),
                        lambda: nc.vector.tensor_scalar(top[0:p, :], top[0:p, :], 1.0, None, ALU.max),
                        lambda: nc.vector.reciprocal(top[0:p, :], top[0:p, :]),
                    ]
                    dve.wait_ge(gathered[s.h], landed(s, JN))
                    for step in steps:
                        n += 1
                        step().then_inc(norm_step, 1)
                        dve.wait_ge(norm_step, s.k * LINKS + n)
                    nc.vector.tensor_copy(c.norm[0:p, bass.ds(s.k * JN, JN)], top[0:p, :])
                    dve.wait_ge(mul, after(s))
                    dve.wait_ge(rectified, after(s, U))
                    for j in range(JN):
                        last = nc.vector.scalar_tensor_tensor(z[s.h][0:p, j, :], ag[s.h][0:p, j, 0:D], top[0:p, j:j + 1],
                                                              mul_ps[s.h][0:p, j, :], ALU.mult, ALU.add)
                    last.then_inc(scaled, 1)
            timeline(dve, FULL, True, 3, body)
    ph.close()


def finish_conv(nc, c, x, h_in, table, x1_out, q_out):
    ph = Phase(nc, "node1")
    idx4, norm4 = ph.sb2("idx4", [P, JN], I32, U), ph.sb2("norm4", [P, JN], n=U)
    ag, ht, xt, z, x1, qs = (ph.sb2(n, [P, JN, D], n=U) for n in ("ag", "ht", "xt", "z", "x1", "qs"))
    hT, x1T = ph.sb2("hT", [P, GROUP]), ph.sb2("x1T", [P, GROUP])
    stats, mv, sd = ph.sb("stats", [P, JN, 6]), ph.sb2("mv", [P, JN, 2], n=U), ph.sb2("sd", [P, JN], n=U)
    rstd, off = ph.sb2("rstd", [P, JN], n=U), ph.sb2("off", [P, JN], n=U)
    hT_ps, mul_ps, x1T_ps, q_ps = (ph.ps2("hT_ps", [P, GROUP]), ph.ps2("mul_ps", [P, JN, D], 4), ph.ps("x1T_ps", [P, GROUP]),
                                   ph.ps("q_ps", [P, JN, D]))
    h_in_s, x_in, gathered = ph.sem2("h_in", U), ph.sem2("x_in", U), ph.sem2("gathered", U)
    x1_st, q_st, pace_bn = ph.sem2("x1_st", U), ph.sem2("q_st", U), ph.sem("pace_bn")
    pace, idx_set, turned, copied, mul = (ph.sem(n) for n in ("pace", "idx_set", "turned", "copied", "mul"))
    scaled, summed, counted, mv_set, sd_set, rstd_set, off_set, x1_set = (
        ph.sem(n) for n in ("scaled", "summed", "counted", "mv_set", "sd_set", "rstd_set", "off_set", "x1_set"))
    x1_turned, x1_copied, q_mul, q_set = (ph.sem(n) for n in ("x1_turned", "x1_copied", "q_mul", "q_set"))
    with nc.Block() as block:
        @block.gpsimd
        def _(pool):
            gather_groups(nc, c, pool, table, ag, idx4, idx_set, scaled, gathered, pace)

        @block.sync
        def _(sp):
            start_dma(sp, h_in_s, x_in, x1_st, q_st)

            def body(at):
                if s := at(0):
                    sp.wait_ge(turned, after(s, U))
                    sp.dma_start(ht[s.h][0:s.p, :, :], group_rows(h_in, s)).then_inc(h_in_s[s.h], 16)
                    sp.wait_ge(summed, after(s, U))
                    sp.dma_start(xt[s.h][0:s.p, :, :], group_rows(x, s)).then_inc(x_in[s.h], 16)
                if s := at(6):
                    sp.wait_ge(x1_set, after(s))
                    sp.dma_start(group_rows(x1_out, s), x1[s.h][0:s.p, :, :]).then_inc(x1_st[s.h], 16)
                if s := at(8):
                    sp.wait_ge(q_set, after(s))
                    sp.dma_start(group_rows(q_out, s), qs[s.h][0:s.p, :, :]).then_inc(q_st[s.h], 16)
            timeline(sp, FULL, True, 9, body)
            wait_all(sp, x1_st, GROUPS)
            wait_all(sp, q_st, GROUPS)

        @block.tensor
        def _(pe):
            start(pe, (turned, mul, x1_turned, q_mul))

            def body(at):
                if s := at(0):
                    pe.wait_ge(h_in_s[s.h], arrived(s))
                    pe.wait_ge(copied, after(s, 2))
                    turn(nc, c, slot(hT_ps, s), ht[s.h], s).then_inc(turned, 1)
                if s := at(1):
                    pe.wait_ge(copied, after(s))
                    pe.wait_ge(scaled, after(s, 4))
                    multiply_rows(nc, c, 1, mul_ps[s.h], slot(hT, s), s).then_inc(mul, 1)
                if s := at(5):
                    pe.wait_ge(x1_set, after(s))
                    pe.wait_ge(x1_copied, after(s, 1))
                    turn(nc, c, x1T_ps, x1[s.h], s).then_inc(x1_turned, 1)
                if s := at(6):
                    pe.wait_ge(x1_copied, after(s))
                    pe.wait_ge(q_set, after(s, 1))
                    for j in range(JN):
                        last = nc.tensor.matmul(q_ps[0:s.p, j, :], slot(x1T, s)[:, j * s.p:(j + 1) * s.p], c.qkv[:, 0:D],
                                                start=True, stop=True)
                    last.then_inc(q_mul, 1)
            timeline(pe, FULL, True, 7, body)

        @block.scalar
        def _(act):
            start(act, (copied, x1_copied, sd_set, x1_set, q_set))

            def body(at):
                if s := at(0):
                    act.wait_ge(mul, after(s, 2))
                    act.wait_ge(turned, after(s))
                    nc.scalar.copy(slot(hT, s)[:, 0:s.n], slot(hT_ps, s)[:, 0:s.n]).then_inc(copied, 1)
                if s := at(3):
                    act.wait_ge(rstd_set, after(s, U))
                    act.wait_ge(mv_set, after(s))
                    nc.scalar.activation(sd[s.h][0:s.p, :], mv[s.h][0:s.p, :, 1], ACT.Sqrt, bias=c.eps[0:s.p, 1:2])\
                        .then_inc(sd_set, 1)
                if s := at(5):
                    act.wait_ge(q_mul, after(s, 2))
                    act.wait_ge(x1_turned, after(s))
                    nc.scalar.copy(slot(x1T, s)[:, 0:s.n], x1T_ps[:, 0:s.n]).then_inc(x1_copied, 1)
                if s := at(6):
                    act.wait_ge(q_st[s.h], vacated(s))
                    act.wait_ge(q_mul, after(s))
                    nc.scalar.copy(qs[s.h][0:s.p, :, :], q_ps[0:s.p, :, :]).then_inc(q_set, 1)
                if s := at(4):
                    act.wait_ge(x1_st[s.h], vacated(s))
                    act.wait_ge(x1_turned, after(s, U))
                    act.wait_ge(off_set, after(s))
                    for j in range(JN):
                        last = nc.scalar.activation(x1[s.h][0:s.p, j, :], z[s.h][0:s.p, j, :], ACT.Identity,
                                                    bias=off[s.h][0:s.p, j:j + 1], scale=rstd[s.h][0:s.p, j:j + 1])
                    last.then_inc(x1_set, 1)
            timeline(act, FULL, True, 7, body)

        @block.vector
        def _(dve):
            start(dve, (idx_set, scaled, summed, counted, mv_set, rstd_set, off_set))

            def body(at):
                if s := at(0):
                    wait_indices_used(dve, gathered, s, JN)
                    nc.vector.tensor_copy(norm4[s.h][:, :], c.norm[:, bass.ds(s.k * JN, JN)])
                    nc.vector.tensor_copy(idx4[s.h][:, :], c.start_i[:, bass.ds(s.k * JN, JN)]).then_inc(idx_set, 1)
                if s := at(2):
                    p, r = s.p, z[s.h]
                    dve.wait_ge(x1_set, after(s, U))
                    dve.wait_ge(gathered[s.h], landed(s, JN))
                    dve.wait_ge(mul, after(s))
                    for j in range(JN):
                        last = nc.vector.scalar_tensor_tensor(r[0:p, j, :], ag[s.h][0:p, j, :], norm4[s.h][0:p, j:j + 1],
                                                              mul_ps[s.h][0:p, j, :], ALU.mult, ALU.add)
                    last.then_inc(scaled, 1)
                    dve.wait_ge(scaled, after(s))
                    dve.wait_ge(x_in[s.h], arrived(s))
                    nc.vector.scalar_tensor_tensor(r[0:p, :, :], r[0:p, :, :], 0.0, xt[s.h][0:p, :, :], ALU.max, ALU.add)\
                        .then_inc(summed, 1)
                    dve.wait_ge(summed, after(s))
                    statistics(nc, dve, s, r, stats, mv, counted, mv_set, sd_set, pace_bn)
                if s := at(3):
                    scale_and_offset(nc, dve, s, mv, sd, rstd, off, sd_set, rstd_set, x1_set, off_set)
            timeline(dve, FULL, True, 4, body)
    ph.close()


def statistics(nc, dve, s, rows, stats, mv, counted, mv_set, sd_set, pace_bn):
    for j in range(JN):
        last = nc.vector.bn_stats(stats[0:s.p, j, :], rows[0:s.p, j, :])
    last.then_inc(counted, 1)
    dve.wait_ge(sd_set, after(s, U))
    dve.wait_ge(counted, after(s))
    dve.sem_inc(pace_bn, 1)
    for j in range(JN):
        last = nc.vector.bn_aggr(mv[s.h][0:s.p, j, :], stats[0:s.p, j, :])
    last.then_inc(mv_set, 1)


def scale_and_offset(nc, dve, s, mv, sd, rstd, off, sd_set, rstd_set, applied, off_set):
    dve.wait_ge(applied, after(s, U))
    dve.wait_ge(sd_set, after(s))
    nc.vector.reciprocal(rstd[s.h][0:s.p, :], sd[s.h][0:s.p, :]).then_inc(rstd_set, 1)
    dve.wait_ge(rstd_set, after(s))
    nc.vector.scalar_tensor_tensor(off[s.h][0:s.p, :], mv[s.h][0:s.p, :, 0], -1.0, rstd[s.h][0:s.p, :], ALU.mult,
                                   ALU.mult).then_inc(off_set, 1)


def group_cols(table, s):
    return table[bass.ds(s.k, 1), :, 0:s.n].rearrange("g f n -> (g f) n")


def project_nodes(nc, c, table, x1_in, y_out):
    ph = Phase(nc, "proj")
    idx4 = ph.sb2("idx4", [P, JN], I32, U)
    ag, xb, o, y = (ph.sb2("ag", [P, JN, CNT], n=U), ph.sb2("xb", [P, JN, D], n=U), ph.sb2("o", [P, JN, D], n=U),
                    ph.sb2("y", [P, GROUP], n=U))
    oT = ph.sb2("oT", [P, GROUP])
    den, inv = ph.sb("den", [P, JN, HEADS]), ph.sb("inv", [P, JN, HEADS])
    oT_ps, mul_ps = ph.ps2("oT_ps", [P, GROUP]), ph.ps2("mul_ps", [P, GROUP], 4)
    x_in, gathered, stored = ph.sem2("x_in", U), ph.sem2("gathered", U), ph.sem2("stored", U)
    pace, idx_set, den_set, inv_set, o_set, turned, copied, mul, y_set, counted = (
        ph.sem(n) for n in ("pace", "idx_set", "den_set", "inv_set", "o_set", "turned", "copied", "mul", "y_set",
                            "counted"))
    with nc.Block() as block:
        @block.gpsimd
        def _(pool):
            gather_groups(nc, c, pool, table, ag, idx4, idx_set, o_set, gathered, pace)

        @block.sync
        def _(sp):
            start_dma(sp, x_in, stored)

            def body(at):
                if s := at(0):
                    sp.wait_ge(mul, after(s, U))
                    sp.dma_start(xb[s.h][0:s.p, :, :], group_rows(x1_in, s)).then_inc(x_in[s.h], 16)
                if s := at(3):
                    sp.wait_ge(y_set, after(s))
                    sp.dma_start(group_cols(y_out, s), y[s.h][:, 0:s.n]).then_inc(stored[s.h], 16)
            timeline(sp, FULL, True, 4, body)
            wait_all(sp, stored, GROUPS)

        @block.vector
        def _(dve):
            start(dve, (idx_set, den_set, inv_set, o_set, counted))

            def body(at):
                if s := at(0):
                    wait_indices_used(dve, gathered, s, JN)
                    nc.vector.tensor_copy(idx4[s.h][:, :], c.start_i[:, bass.ds(s.k * JN, JN)]).then_inc(idx_set, 1)
                if s := at(2):
                    p = s.p
                    dve.wait_ge(gathered[s.h], landed(s, JN))
                    nc.vector.tensor_scalar(den[0:p, :, :], ag[s.h][0:p, :, D:], 1e-30, None, ALU.max).then_inc(den_set, 1)
                    dve.wait_ge(den_set, after(s))
                    nc.vector.reciprocal(inv[0:p, :, :], den[0:p, :, :]).then_inc(inv_set, 1)
                    dve.wait_ge(inv_set, after(s))
                    dve.wait_ge(turned, after(s, U))
                    for j in range(JN):
                        last = nc.vector.tensor_tensor(o[s.h][0:p, j, :].rearrange("p (h e) -> p h e", e=HD),
                                                       ag[s.h][0:p, j, 0:D].rearrange("p (h e) -> p h e", e=HD),
                                                       bc(inv[0:p, j, :], HD), ALU.mult)
                    last.then_inc(o_set, 1)
                if s := at(5):
                    dve.wait_ge(y_set, after(s))
                    nc.vector.bn_stats(c.stats[:, bass.ds(s.k * 6, 6)], y[s.h][:, 0:s.n]).then_inc(counted, 1)
            timeline(dve, FULL, True, 6, body)

        @block.tensor
        def _(pe):
            start(pe, (turned, mul))

            def body(at):
                if s := at(0):
                    pe.wait_ge(o_set, after(s))
                    pe.wait_ge(copied, after(s, 2))
                    turn(nc, c, slot(oT_ps, s), o[s.h], s).then_inc(turned, 1)
                if s := at(1):
                    pe.wait_ge(y_set, after(s, 4))
                    pe.wait_ge(copied, after(s))
                    nc.tensor.matmul(mul_ps[s.h][:, 0:s.n], c.wo[:, :], slot(oT, s)[:, 0:s.n], start=True, stop=False)
                    pe.wait_ge(x_in[s.h], arrived(s))
                    for j in range(JN):
                        last = nc.tensor.matmul(mul_ps[s.h][:, j * s.p:(j + 1) * s.p], xb[s.h][0:s.p, j, :],
                                                c.ident[0:s.p, 0:s.p], start=False, stop=j == JN - 1)
                    last.then_inc(mul, 1)
            timeline(pe, FULL, True, 2, body)

        @block.scalar
        def _(act):
            start(act, (copied, y_set))

            def body(at):
                if s := at(0):
                    act.wait_ge(mul, after(s, 2))
                    act.wait_ge(turned, after(s))
                    nc.scalar.copy(slot(oT, s)[:, 0:s.n], slot(oT_ps, s)[:, 0:s.n]).then_inc(copied, 1)
                if s := at(2):
                    act.wait_ge(stored[s.h], vacated(s))
                    act.wait_ge(counted, after(s, U))
                    act.wait_ge(mul, after(s))
                    nc.scalar.activation(y[s.h][:, 0:s.n], mul_ps[s.h][:, 0:s.n], ACT.Identity, bias=c.col[:, 0:1])\
                        .then_inc(y_set, 1)
            timeline(act, FULL, True, 3, body)
    ph.close()


def close_stats(nc, dve, c, mv, aff, gamma, beta, link, root):
    nc.vector.bn_aggr(mv[:, :], c.stats[:, :]).then_inc(link, 1)
    dve.wait_ge(link, 1)
    dve.wait_ge(root, 1)
    nc.vector.reciprocal(aff[:, 2:3], aff[:, 2:3]).then_inc(link, 1)
    dve.wait_ge(link, 2)
    nc.vector.tensor_tensor(aff[:, 0:1], aff[:, 2:3], gamma, ALU.mult).then_inc(link, 1)
    dve.wait_ge(link, 3)
    nc.vector.tensor_tensor(aff[:, 2:3], aff[:, 0:1], mv[:, 0:1], ALU.mult).then_inc(link, 1)
    dve.wait_ge(link, 4)
    nc.vector.tensor_tensor(aff[:, 1:2], beta, aff[:, 2:3], ALU.subtract).then_inc(link, 1)


def root_stats(nc, act, c, mv, aff, link, root):
    act.wait_ge(link, 1)
    nc.scalar.activation(aff[:, 2:3], mv[:, 1:2], ACT.Sqrt, bias=c.eps[:, 1:2]).then_inc(root, 1)
    act.wait_ge(link, 5)


def feed_forward(nc, c, y_in, y_out):
    ph = Phase(nc, "ffn")
    yb, hb, f, y2 = (ph.sb2("yb", [P, GROUP], n=U), ph.sb2("hb", [P, GROUP], n=U), ph.sb2("f", [P, 2, GROUP]),
                     ph.sb2("y2", [P, GROUP], n=U))
    mv, aff = ph.sb("mv", [P, 2]), ph.sb("aff", [P, 3])
    f_ps = [ph.ps2(f"f{a}_ps", [P, GROUP]) for a in range(2)]
    g_ps = ph.ps2("g_ps", [P, GROUP])
    y_in_s, stored = ph.sem2("y_in", U), ph.sem2("stored", U)
    link, root, h_set, f_mul, f0_set, f1_set, mul, y2_set, counted = (
        ph.sem(n) for n in ("link", "root", "h_set", "f_mul", "f0_set", "f1_set", "mul", "y2_set", "counted"))
    with nc.Block() as block:
        @block.sync
        def _(sp):
            start_dma(sp, y_in_s, stored)

            def body(at):
                if s := at(0):
                    sp.wait_ge(h_set, after(s, U))
                    sp.dma_start(yb[s.h][:, 0:s.n], group_cols(y_in, s)).then_inc(y_in_s[s.h], 16)
                if s := at(3):
                    sp.wait_ge(y2_set, after(s))
                    sp.dma_start(group_cols(y_out, s), y2[s.h][:, 0:s.n]).then_inc(stored[s.h], 16)
            timeline(sp, FULL, True, 4, body)
            wait_all(sp, stored, GROUPS)

        @block.scalar
        def _(act):
            start(act, (h_set, f0_set))
            root_stats(nc, act, c, mv, aff, link, root)

            def body(at):
                if s := at(0):
                    act.wait_ge(y2_set, after(s, U))
                    act.wait_ge(y_in_s[s.h], arrived(s))
                    nc.scalar.activation(hb[s.h][:, 0:s.n], yb[s.h][:, 0:s.n], ACT.Identity, bias=aff[:, 1:2],
                                         scale=aff[:, 0:1]).then_inc(h_set, 1)
                if s := at(1):
                    act.wait_ge(mul, after(s, 2))
                    act.wait_ge(f_mul, after(s))
                    nc.scalar.activation(f[s.h % 2][:, 0, 0:s.n], f_ps[0][s.h % 2][:, 0:s.n], ACT.Relu, bias=c.b1[:, 0:1])\
                        .then_inc(f0_set, 1)
            timeline(act, FULL, True, 2, body)

        @block.tensor
        def _(pe):
            start(pe, (f_mul, mul))

            def body(at):
                if s := at(0):
                    pe.wait_ge(f0_set, after(s, 2))
                    pe.wait_ge(f1_set, after(s, 2))
                    pe.wait_ge(h_set, after(s))
                    for a in range(2):
                        last = nc.tensor.matmul(f_ps[a][s.h % 2][:, 0:s.n], c.w1[:, a * P:(a + 1) * P], hb[s.h][:, 0:s.n],
                                                start=True, stop=True)
                    last.then_inc(f_mul, 1)
                if s := at(1):
                    pe.wait_ge(y2_set, after(s, 2))
                    pe.wait_ge(f0_set, after(s))
                    pe.wait_ge(f1_set, after(s))
                    for a in range(2):
                        last = nc.tensor.matmul(g_ps[s.h % 2][:, 0:s.n], c.w2[:, a, :], f[s.h % 2][:, a, 0:s.n],
                                                start=a == 0, stop=a == 1)
                    last.then_inc(mul, 1)
            timeline(pe, FULL, True, 2, body)

        @block.vector
        def _(dve):
            start(dve, (f1_set, y2_set, counted))
            close_stats(nc, dve, c, mv, aff, c.col[:, 2:3], c.col[:, 3:4], link, root)

            def body(at):
                if s := at(0):
                    dve.wait_ge(mul, after(s, 2))
                    dve.wait_ge(f_mul, after(s))
                    nc.vector.tensor_scalar(f[s.h % 2][:, 1, 0:s.n], f_ps[1][s.h % 2][:, 0:s.n], c.b1[:, 1:2], 0.0,
                                            ALU.add, ALU.max).then_inc(f1_set, 1)
                if s := at(1):
                    dve.wait_ge(stored[s.h], vacated(s))
                    dve.wait_ge(mul, after(s))
                    nc.vector.scalar_tensor_tensor(y2[s.h][:, 0:s.n], g_ps[s.h % 2][:, 0:s.n], c.col[:, 1:2],
                                                   hb[s.h][:, 0:s.n], ALU.add, ALU.add).then_inc(y2_set, 1)
                    dve.wait_ge(y2_set, after(s))
                    nc.vector.bn_stats(c.stats[:, bass.ds(s.k * 6, 6)], y2[s.h][:, 0:s.n]).then_inc(counted, 1)
            timeline(dve, FULL, True, 2, body)
    ph.close()


def final_norm(nc, c, x1_in, y_in, out):
    ph = Phase(nc, "fin")
    yb = ph.sb2("yb", [P, GROUP], n=U)
    scale, shift, row = ph.sb("scale", [P, D]), ph.sb("shift", [P, D]), ph.sb("row", [P, D])
    high, mid16, rest = ph.sb("high", [P, D], BF16), ph.sb("mid16", [P, D], BF16), ph.sb("rest", [P, D])
    xb, rows = (ph.sb2(n, [P, JN, D], n=U) for n in ("xb", "rows"))
    stats, mv2, sd = ph.sb2("stats", [P, JN, 6], n=U), ph.sb2("mv2", [P, JN, 2], n=U), ph.sb2("sd", [P, JN], n=U)
    rstd, off = ph.sb2("rstd", [P, JN], n=U), ph.sb2("off", [P, JN], n=U)
    mv, aff = ph.sb("mv", [P, 2]), ph.sb("aff", [P, 3])
    r_ps, row_ps = ph.ps2("r_ps", [P, JN, D], U), ph.ps("row_ps", [P, D])
    y_in_s, x_in, stored = ph.sem2("y_in", U), ph.sem2("x_in", U), ph.sem2("stored", U)
    link, root, affine, row_mul, row_copied, split, turned, counted, mv_set, sd_set, rstd_set, off_set, rows_set, pace_bn = (
        ph.sem(n) for n in ("link", "root", "affine", "row_mul", "row_copied", "split", "turned", "counted", "mv_set", "sd_set", "rstd_set",
                            "off_set", "rows_set", "pace_bn"))
    with nc.Block() as block:
        @block.sync
        def _(sp):
            start_dma(sp, y_in_s, x_in, stored)

            def body(at):
                if s := at(0):
                    sp.wait_ge(turned, after(s, U))
                    sp.dma_start(yb[s.h][:, 0:s.n], group_cols(y_in, s)).then_inc(y_in_s[s.h], 16)
                    sp.dma_start(xb[s.h][0:s.p, :, :], group_rows(x1_in, s)).then_inc(x_in[s.h], 16)
                if s := at(6):
                    sp.wait_ge(rows_set, after(s))
                    sp.dma_start(group_rows(out, s), rows[s.h][0:s.p, :, :]).then_inc(stored[s.h], 16)
            timeline(sp, FULL, True, 7, body)
            wait_all(sp, stored, GROUPS)

        @block.scalar
        def _(act):
            start(act, (sd_set, rows_set))
            root_stats(nc, act, c, mv, aff, link, root)

            def body(at):
                if s := at(3):
                    act.wait_ge(rstd_set, after(s, U))
                    act.wait_ge(mv_set, after(s))
                    nc.scalar.activation(sd[s.h][0:s.p, :], mv2[s.h][0:s.p, :, 1], ACT.Sqrt, bias=c.eps[0:s.p, 1:2])\
                        .then_inc(sd_set, 1)
                if s := at(4):
                    act.wait_ge(stored[s.h], vacated(s))
                    act.wait_ge(off_set, after(s))
                    for j in range(JN):
                        last = nc.scalar.activation(rows[s.h][0:s.p, j, :], r_ps[s.h][0:s.p, j, :], ACT.Identity,
                                                    bias=off[s.h][0:s.p, j:j + 1], scale=rstd[s.h][0:s.p, j:j + 1])
                    last.then_inc(rows_set, 1)
            timeline(act, FULL, True, 5, body)

        @block.tensor
        def _(pe):
            start(pe, (turned,))
            pe.wait_ge(affine, 2)
            nc.tensor.matmul(row_ps[:, :], c.ones[:, :], shift[:, :], start=True, stop=True).then_inc(row_mul, 1)
            pe.wait_ge(split, SPLITS)

            def body(at):
                if s := at(0):
                    pe.wait_ge(rows_set, after(s, U))
                    nc.tensor.matmul(r_ps[s.h][0:s.p, :, :], c.ones16[:, 0:s.p], c.shift16[:, 0, :, :], start=True, stop=False)
                    pe.wait_ge(x_in[s.h], arrived(s))
                    nc.tensor.matmul(r_ps[s.h][0:s.p, :, :], c.ident[0:s.p, 0:s.p], xb[s.h][0:s.p, :, :], start=False,
                                     stop=False)
                    pe.wait_ge(y_in_s[s.h], arrived(s))
                    for j in range(JN):
                        last = nc.tensor.matmul(r_ps[s.h][0:s.p, j, :], yb[s.h][:, j * s.p:(j + 1) * s.p], scale[:, :],
                                                start=False, stop=j == JN - 1)
                    last.then_inc(turned, 1)
            timeline(pe, FULL, True, 1, body)

        @block.vector
        def _(dve):
            start(dve, (counted, mv_set, rstd_set, off_set))
            close_stats(nc, dve, c, mv, aff, c.col[:, 4:5], c.col[:, 5:6], link, root)
            dve.wait_ge(link, 5)
            nc.vector.tensor_scalar(scale[:, :], c.ident[:, :], aff[:, 0:1], None, ALU.mult).then_inc(affine, 1)
            nc.vector.tensor_scalar(shift[:, :], c.ident[:, :], aff[:, 1:2], None, ALU.mult).then_inc(affine, 1)
            dve.wait_ge(row_mul, 1)
            nc.vector.tensor_copy(row[:, :], row_ps[:, :]).then_inc(row_copied, 1)
            dve.wait_ge(row_copied, 1)
            split_row(nc, dve, row[:, :], c.shift16[:, 0, :, :], high, mid16, rest, split, 0)

            def body(at):
                if s := at(1):
                    dve.wait_ge(turned, after(s))
                    statistics(nc, dve, s, r_ps[s.h], stats[s.h], mv2, counted, mv_set, sd_set, pace_bn)
                if s := at(2):
                    scale_and_offset(nc, dve, s, mv2, sd, rstd, off, sd_set, rstd_set, rows_set, off_set)
            timeline(dve, FULL, True, 3, body)
    ph.close()


class Constants:
    pass


def build(nc, w, out):
    with ExitStack() as ctx:
        c = Constants()

        def keep(name, shape, dt=F32):
            return ctx.enter_context(nc.sbuf_tensor(name, shape, dt))

        c.ident, c.ones, c.lower = keep("ident", [P, P]), keep("ones", [P, P]), keep("lower", [P, P])
        c.iota_i, c.iota16 = keep("iota_i", [P, COLS], I32), keep("iota16", [P, COLS], F16)
        c.iota, c.iota1 = keep("iota", [P, TYPES]), keep("iota1", [P, TYPES])
        c.rows, c.after = keep("rows", [P, 3, 4, P], I32), keep("after", [P, 4, EDGES_T], I32)
        c.start_i, c.unsorted = keep("start_i", [P, COLS], I32), keep("unsorted", [1, 1], I32)
        c.src_i, c.dst_i = (keep(n, [P, TILES], I32) for n in ("src_i", "dst_i"))
        c.in_f, c.out_f, c.dst_f, c.typ_f, c.place_p, c.place_f = (
            keep(n, [P, TILES]) for n in ("in_f", "out_f", "dst_f", "typ_f", "place_p", "place_f"))
        c.count, c.norm = keep("count", [P, COLS]), keep("norm", [P, COLS])
        c.ones16, c.shift16 = keep("ones16", [P, P], BF16), keep("shift16", [P, LAYERS, JN, D], BF16)
        c.w_emb, c.b_emb = keep("w_emb", [P, D]), keep("b_emb", [P, D])
        c.bases, c.loop = keep("bases", [P, LAYERS, BASES, D]), keep("loop", [P, LAYERS, D])
        c.coe, c.bn = keep("coe", [P, LAYERS, TYPES * BASES]), keep("bn", [P, LAYERS, 4, D])
        c.qkv, c.wo, c.w1, c.w2 = keep("qkv", [P, 3 * D]), keep("wo", [P, D]), keep("w1", [P, 2 * D]), keep("w2", [P, 2, D])
        c.b1, c.col, c.stats = keep("b1", [P, 2]), keep("col", [P, 6]), keep("stats", [P, GROUPS * 6])
        c.zero, c.eps = keep("zero", [1, CNT]), keep("eps", [P, 2])
        h0, h1, x1, q = (nc.dram_tensor(n, (NODES, D), F32, kind="Internal").ap() for n in ("h0", "h1", "x1", "q"))
        sums0, att = (nc.dram_tensor(n, (EPAD + 1, CNT), F32, kind="Internal").ap() for n in ("sums0", "att"))
        sums1 = nc.dram_tensor("sums1", (EPAD + 1, D), F32, kind="Internal").ap()
        y1T, y2T = (nc.dram_tensor(n, (GROUPS, P, GROUP), F32, kind="Internal").ap() for n in ("y1T", "y2T"))
        scratch = nc.dram_tensor("scratch", (EDGES + P, 3), I32, kind="Internal").ap()
        c.zero_rows = [(t, n) for t, n in ((sums0, CNT), (att, CNT), (sums1, D))]
        load_constants(nc, c, w)
        arrange_edges(nc, c)
        sort_edges(nc, c, w["dst"], scratch)
        place_edges(nc, c)
        embed_nodes(nc, c, w["x"], h0)
        index_nodes(nc, c)
        conv_edges(nc, c, 0, h0, sums0, CNT)
        update_nodes(nc, c, h0, sums0, h1)
        conv_edges(nc, c, 1, h1, sums1, D)
        finish_conv(nc, c, w["x"], h1, sums1, x1, q)
        attend_edges(nc, c, q, x1, att)
        project_nodes(nc, c, att, x1, y1T)
        feed_forward(nc, c, y1T, y2T)
        final_norm(nc, c, x1, y2T, out)


NAMES = ["x", "src", "dst", "edge_type_8", "L0_gnn_W_emb", "L0_gnn_b_emb", "L0_gnn_bases", "L0_gnn_w_coe",
         "L0_gnn_self_loop", "L0_gnn_bn_gamma", "L0_gnn_bn_beta", "L0_gnn_bn_mean", "L0_gnn_bn_var", "L1_gnn_Wq",
         "L1_gnn_Wk", "L1_gnn_Wv", "L1_gnn_Wo", "L1_gnn_bo", "L1_gnn_W1", "L1_gnn_b1", "L1_gnn_W2", "L1_gnn_b2",
         "L1_gnn_g1", "L1_gnn_be1", "L1_gnn_g2", "L1_gnn_be2"]


def kernel(**inputs):
    import concourse.bacc as bacc
    from concourse.bass_utils import run_bass_kernel_spmd

    nc = bacc.Bacc("TRN2", target_bir_lowering=False, num_devices=1)
    arrays, w = {}, {}
    for name in NAMES:
        a = np.ascontiguousarray(inputs[name])
        arrays["in_" + name] = a
        w[name] = nc.dram_tensor("in_" + name, a.shape, mybir.dt.from_np(a.dtype), kind="ExternalInput").ap()
    out = nc.dram_tensor("out", (NODES, D), F32, kind="ExternalOutput").ap()
    build(nc, w, out)
    return run_bass_kernel_spmd(nc, [arrays], core_ids=[0]).results[0]["out"]
```
